# Optimizing a Trainium2 kernel written in Bass

```python
import numpy as np
import jax
import jax.numpy as jnp

def _softmax(x, axis=-1):
    return jax.nn.softmax(x, axis=axis)

def _gelu(x):
    return jax.nn.gelu(x, approximate=True)

def _silu(x):
    return jax.nn.silu(x)

def _sigmoid(x):
    return jax.nn.sigmoid(x)

def _layernorm(x, axis=-1, eps=1e-05):
    m = jnp.mean(x, axis=axis, keepdims=True)
    v = jnp.var(x, axis=axis, keepdims=True)
    return (x - m) / jnp.sqrt(v + eps)

def _scatter_add(tgt, idx, src, axis=0):
    return tgt.at[idx].add(src)

def _segment_sum(src, seg, n):
    return jax.ops.segment_sum(src, seg, n)
kernel_name = 'mk_adaln_ffn_d2_seqx_r8_e3431a'

def setup_inputs(seed: int=0):
    np.random.seed(seed)
    _w = jnp.asarray

    def _rec_inputs():
        import jax
        import jax.numpy as jnp
        _rk = jax.random.key(seed)
        x = -5.722e-05 + 0.9998 * jax.random.normal(jax.random.fold_in(_rk, 1), (2, 512, 128), jnp.float32)
        _lenS = 512 - jax.random.randint(jax.random.fold_in(_rk, 7), (2,), 0, max(1, 512 // 4) + 1, jnp.int32)
        _lenS2 = 512 - jax.random.randint(jax.random.fold_in(_rk, 8), (2,), 0, max(1, 512 // 4) + 1, jnp.int32)
        cond_1024 = -0.00499425 + 1.0058 * jax.random.normal(jax.random.fold_in(_rk, 11), (2, 128), jnp.float32)
        _validS = jnp.arange(512)[None, :] < _lenS[:, None]
        _validS2 = jnp.arange(512)[None, :] < _lenS2[:, None]
        _causal = jnp.tril(jnp.ones((512, 512), dtype=bool))
        mask_Bx1x1xS_ff0 = jnp.where(jnp.ones((2, 1, 1, 512), dtype=bool), 0.0, -1000000000.0).astype(jnp.float32)
        return (x, cond_1024, mask_Bx1x1xS_ff0)
    x, cond_1024, mask_Bx1x1xS_ff0 = _rec_inputs()

    def _L0_cond_setup():
        import jax, jax.numpy as jnp
        import numpy as np
        key = jax.random.key(seed)
        k1, k2 = jax.random.split(key)
        B, S, D = (32, 256, 128)
        query = jax.random.normal(k1, (B, D), dtype=jnp.float32)
        values = jax.random.normal(k2, (B, S, D), dtype=jnp.float32)
        return {'query': query, 'values': values}
    _L0_cond_all = _L0_cond_setup()
    _L0_cond_in = {k: v for k, v in _L0_cond_all.items() if k in ()}
    del _L0_cond_all

    def _L0_ffn_setup():
        import jax, jax.numpy as jnp
        import numpy as np
        HIDDEN = 128
        INNER = 512

        def _weight_quant(w):
            scale = 1.0 / jnp.clip(jnp.mean(jnp.abs(w)), 1e-05)
            wq = jnp.clip(jnp.round(w * scale), -1.0, 1.0) / scale
            return w + jax.lax.stop_gradient(wq - w)

        def _act_quant(x):
            scale = 127.0 / jnp.clip(jnp.max(jnp.abs(x), axis=-1, keepdims=True), 1e-05)
            xq = jnp.clip(jnp.round(x * scale), -128.0, 127.0) / scale
            return x + jax.lax.stop_gradient(xq - x)

        def _bitlinear(x, w):
            return jnp.einsum('bsi,oi->bso', _act_quant(x), _weight_quant(w))
        key = jax.random.key(seed)
        k0, k1, k2, k3 = jax.random.split(key, 4)
        x = jax.random.normal(k0, (4, 256, HIDDEN), dtype=jnp.float32)
        w_gate = jax.random.normal(k1, (INNER, HIDDEN), dtype=jnp.float32) / np.sqrt(HIDDEN)
        w_up = jax.random.normal(k2, (INNER, HIDDEN), dtype=jnp.float32) / np.sqrt(HIDDEN)
        w_down = jax.random.normal(k3, (HIDDEN, INNER), dtype=jnp.float32) / np.sqrt(INNER)
        return {'x': x, 'w_gate': w_gate, 'w_up': w_up, 'w_down': w_down}
    _L0_ffn_all = _L0_ffn_setup()
    _L0_ffn_in = {k: v for k, v in _L0_ffn_all.items() if k in ('w_gate', 'w_up', 'w_down')}
    del _L0_ffn_all

    def _L1_cond_setup():
        import jax, jax.numpy as jnp
        import numpy as np
        EMBED = 128
        HEADS = 16
        HDIM = EMBED // HEADS
        MASK_OUT = -10000.0

        def _split_heads(t):
            B, T, _ = t.shape
            return t.reshape(B, T, HEADS, HDIM).transpose(0, 2, 1, 3)
        key = jax.random.key(seed)
        ks = jax.random.split(key, 12)
        B, S = (4, 1023)
        scale = 0.02
        return {'word_hidden_states': jax.random.normal(ks[0], (B, S, EMBED), jnp.float32), 'image_hidden_states': jax.random.normal(ks[1], (B, EMBED), jnp.float32), 'attention_mask': jnp.zeros((B, 1, 1, S), jnp.float32), 'c_attn_w': jax.random.normal(ks[2], (EMBED, 3 * EMBED), jnp.float32) * scale, 'c_attn_b': jnp.zeros((3 * EMBED,), jnp.float32), 'c_proj_w': jax.random.normal(ks[3], (EMBED, EMBED), jnp.float32) * scale, 'c_proj_b': jnp.zeros((EMBED,), jnp.float32), 'uk_w': jax.random.normal(ks[4], (EMBED, EMBED), jnp.float32) * scale, 'uk_b': jnp.zeros((EMBED,), jnp.float32), 'uv_w': jax.random.normal(ks[5], (EMBED, EMBED), jnp.float32) * scale, 'uv_b': jnp.zeros((EMBED,), jnp.float32)}
    _L1_cond_all = _L1_cond_setup()
    _L1_cond_in = {k: v for k, v in _L1_cond_all.items() if k in ('c_attn_w', 'c_attn_b', 'c_proj_w', 'c_proj_b', 'uk_w', 'uk_b', 'uv_w', 'uv_b')}
    del _L1_cond_all

    def _L1_ffn_setup():
        import jax, jax.numpy as jnp
        import numpy as np
        NHEAD = 16
        NUM_GROUPS = 4
        EXPERTS_PER_GROUP = 2
        LN_EPS = 1e-05

        def _layernorm(x, g, b):
            mu = jnp.mean(x, axis=-1, keepdims=True)
            var = jnp.mean(jnp.square(x - mu), axis=-1, keepdims=True)
            return (x - mu) * jax.lax.rsqrt(var + LN_EPS) * g + b

        def _mha(x, wi, bi, wo, bo):
            B, S, D = x.shape
            hd = D // NHEAD
            qkv = x @ wi.T + bi
            q, k, v = jnp.split(qkv, 3, axis=-1)

            def heads(t):
                return t.reshape(B, S, NHEAD, hd).transpose(0, 2, 1, 3)
            q, k, v = (heads(q), heads(k), heads(v))
            scores = jnp.einsum('bhqd,bhkd->bhqk', q, k) / jnp.sqrt(jnp.asarray(hd, x.dtype))
            attn = jax.nn.softmax(scores, axis=-1)
            o = jnp.einsum('bhqk,bhkd->bhqd', attn, v)
            o = o.transpose(0, 2, 1, 3).reshape(B, S, D)
            return o @ wo.T + bo

        def _hier_moe(x, w_group, b_group, w_expert, b_expert, w1, b1, w2, b2):
            B, S, D = x.shape
            xt = x.reshape(B * S, D)
            T = xt.shape[0]
            E = NUM_GROUPS * EXPERTS_PER_GROUP
            gp = jax.nn.softmax(xt @ w_group + b_group, axis=-1)
            g_idx = jnp.argmax(gp, axis=-1)
            g_prob = jnp.max(gp, axis=-1)
            elog = jnp.einsum('td,gde->tge', xt, w_expert) + b_expert
            ep = jax.nn.softmax(elog, axis=-1)
            ep_sel = jnp.take_along_axis(ep, g_idx[:, None, None], axis=1)[:, 0, :]
            e_idx_local = jnp.argmax(ep_sel, axis=-1)
            e_prob = jnp.max(ep_sel, axis=-1)
            flat_e = g_idx * EXPERTS_PER_GROUP + e_idx_local
            combine = jax.nn.one_hot(flat_e, E, dtype=xt.dtype) * (g_prob * e_prob)[:, None]
            h = jax.nn.relu(jnp.einsum('td,edf->etf', xt, w1) + b1[:, None, :])
            y = jnp.einsum('etf,efd->etd', h, w2) + b2[:, None, :]
            out = jnp.einsum('te,etd->td', combine, y)
            return out.reshape(B, S, D)
        key = jax.random.key(seed)
        ks = jax.random.split(key, 8)
        B, S, D, F = (2, 128, 128, 256)
        G, Epg = (NUM_GROUPS, EXPERTS_PER_GROUP)
        E = G * Epg
        sc = lambda fan: 1.0 / np.sqrt(fan)
        return {'x': jax.random.normal(ks[0], (B, S, D), jnp.float32), 'in_proj_w': jax.random.normal(ks[1], (3 * D, D), jnp.float32) * sc(D), 'in_proj_b': jnp.zeros((3 * D,), jnp.float32), 'out_proj_w': jax.random.normal(ks[2], (D, D), jnp.float32) * sc(D), 'out_proj_b': jnp.zeros((D,), jnp.float32), 'ln1_g': jnp.ones((D,), jnp.float32), 'ln1_b': jnp.zeros((D,), jnp.float32), 'ln2_g': jnp.ones((D,), jnp.float32), 'ln2_b': jnp.zeros((D,), jnp.float32), 'w_group': jax.random.normal(ks[3], (D, G), jnp.float32) * sc(D), 'b_group': jnp.zeros((G,), jnp.float32), 'w_expert': jax.random.normal(ks[4], (G, D, Epg), jnp.float32) * sc(D), 'b_expert': jnp.zeros((G, Epg), jnp.float32), 'w1': jax.random.normal(ks[5], (E, D, F), jnp.float32) * sc(D), 'b1': jnp.zeros((E, F), jnp.float32), 'w2': jax.random.normal(ks[6], (E, F, D), jnp.float32) * sc(F), 'b2': jnp.zeros((E, D), jnp.float32)}
    _L1_ffn_all = _L1_ffn_setup()
    _L1_ffn_in = {k: v for k, v in _L1_ffn_all.items() if k in ('in_proj_w', 'in_proj_b', 'out_proj_w', 'out_proj_b', 'ln1_g', 'ln1_b', 'ln2_g', 'ln2_b', 'w_group', 'b_group', 'w_expert', 'b_expert', 'w1', 'b1', 'w2', 'b2')}
    del _L1_ffn_all
    return {'x': x, 'cond_1024': cond_1024, 'mask_Bx1x1xS_ff0': mask_Bx1x1xS_ff0, 'L0_ffn_w_gate': _L0_ffn_in['w_gate'], 'L0_ffn_w_up': _L0_ffn_in['w_up'], 'L0_ffn_w_down': _L0_ffn_in['w_down'], 'L1_cond_c_attn_w': _L1_cond_in['c_attn_w'], 'L1_cond_c_attn_b': _L1_cond_in['c_attn_b'], 'L1_cond_c_proj_w': _L1_cond_in['c_proj_w'], 'L1_cond_c_proj_b': _L1_cond_in['c_proj_b'], 'L1_cond_uk_w': _L1_cond_in['uk_w'], 'L1_cond_uk_b': _L1_cond_in['uk_b'], 'L1_cond_uv_w': _L1_cond_in['uv_w'], 'L1_cond_uv_b': _L1_cond_in['uv_b'], 'L1_ffn_in_proj_w': _L1_ffn_in['in_proj_w'], 'L1_ffn_in_proj_b': _L1_ffn_in['in_proj_b'], 'L1_ffn_out_proj_w': _L1_ffn_in['out_proj_w'], 'L1_ffn_out_proj_b': _L1_ffn_in['out_proj_b'], 'L1_ffn_ln1_g': _L1_ffn_in['ln1_g'], 'L1_ffn_ln1_b': _L1_ffn_in['ln1_b'], 'L1_ffn_ln2_g': _L1_ffn_in['ln2_g'], 'L1_ffn_ln2_b': _L1_ffn_in['ln2_b'], 'L1_ffn_w_group': _L1_ffn_in['w_group'], 'L1_ffn_b_group': _L1_ffn_in['b_group'], 'L1_ffn_w_expert': _L1_ffn_in['w_expert'], 'L1_ffn_b_expert': _L1_ffn_in['b_expert'], 'L1_ffn_w1': _L1_ffn_in['w1'], 'L1_ffn_b1': _L1_ffn_in['b1'], 'L1_ffn_w2': _L1_ffn_in['w2'], 'L1_ffn_b2': _L1_ffn_in['b2']}

def reference(x, cond_1024, mask_Bx1x1xS_ff0, L0_ffn_w_gate, L0_ffn_w_up, L0_ffn_w_down, L1_cond_c_attn_w, L1_cond_c_attn_b, L1_cond_c_proj_w, L1_cond_c_proj_b, L1_cond_uk_w, L1_cond_uk_b, L1_cond_uv_w, L1_cond_uv_b, L1_ffn_in_proj_w, L1_ffn_in_proj_b, L1_ffn_out_proj_w, L1_ffn_out_proj_b, L1_ffn_ln1_g, L1_ffn_ln1_b, L1_ffn_ln2_g, L1_ffn_ln2_b, L1_ffn_w_group, L1_ffn_b_group, L1_ffn_w_expert, L1_ffn_b_expert, L1_ffn_w1, L1_ffn_b1, L1_ffn_w2, L1_ffn_b2):
    import jax
    import jax.numpy as jnp

    def _L0_cond_ref(query, values):
        import jax, jax.numpy as jnp
        import numpy as np
        D = query.shape[-1]
        weights = jnp.einsum('bd,bsd->bs', query, values) / jnp.sqrt(jnp.asarray(D, query.dtype))
        weights = jax.nn.softmax(weights, axis=0)
        return values * weights[..., None]

    def _L0_ffn_ref(x, w_gate, w_up, w_down):
        import jax, jax.numpy as jnp
        import numpy as np
        HIDDEN = 128
        INNER = 512

        def _weight_quant(w):
            scale = 1.0 / jnp.clip(jnp.mean(jnp.abs(w)), 1e-05)
            wq = jnp.clip(jnp.round(w * scale), -1.0, 1.0) / scale
            return w + jax.lax.stop_gradient(wq - w)

        def _act_quant(x):
            scale = 127.0 / jnp.clip(jnp.max(jnp.abs(x), axis=-1, keepdims=True), 1e-05)
            xq = jnp.clip(jnp.round(x * scale), -128.0, 127.0) / scale
            return x + jax.lax.stop_gradient(xq - x)

        def _bitlinear(x, w):
            return jnp.einsum('bsi,oi->bso', _act_quant(x), _weight_quant(w))
        gate = jax.nn.silu(_bitlinear(x, w_gate))
        up = _bitlinear(x, w_up)
        return _bitlinear(gate * up, w_down)

    def _L1_cond_ref(word_hidden_states, image_hidden_states, attention_mask, c_attn_w, c_attn_b, c_proj_w, c_proj_b, uk_w, uk_b, uv_w, uv_b):
        import jax, jax.numpy as jnp
        import numpy as np
        EMBED = 128
        HEADS = 16
        HDIM = EMBED // HEADS
        MASK_OUT = -10000.0

        def _split_heads(t):
            B, T, _ = t.shape
            return t.reshape(B, T, HEADS, HDIM).transpose(0, 2, 1, 3)
        B, S, _ = word_hidden_states.shape
        qkv = word_hidden_states @ c_attn_w + c_attn_b
        q_word, k_word, v_word = jnp.split(qkv, 3, axis=-1)
        img = image_hidden_states[:, None, :]
        k_img = img @ uk_w.T + uk_b
        v_img = img @ uv_w.T + uv_b
        k = jnp.concatenate([k_img, k_word], axis=1)
        v = jnp.concatenate([v_img, v_word], axis=1)
        q = _split_heads(q_word)
        k = _split_heads(k)
        v = _split_heads(v)
        scores = jnp.einsum('bhqd,bhkd->bhqk', q, k) / jnp.sqrt(jnp.float32(HDIM))
        qi = jnp.arange(S)[:, None]
        kj = jnp.arange(S + 1)[None, :]
        causal = kj <= qi + 1
        scores = jnp.where(causal[None, None], scores, jnp.float32(MASK_OUT))
        zero_col = jnp.zeros(attention_mask.shape[:-1] + (1,), attention_mask.dtype)
        mask = jnp.concatenate([zero_col, attention_mask], axis=-1)
        scores = scores + mask
        attn = jax.nn.softmax(scores, axis=-1)
        out = jnp.einsum('bhqk,bhkd->bhqd', attn, v)
        out = out.transpose(0, 2, 1, 3).reshape(B, S, EMBED)
        out = out @ c_proj_w + c_proj_b
        return out

    def _L1_ffn_ref(x, in_proj_w, in_proj_b, out_proj_w, out_proj_b, ln1_g, ln1_b, ln2_g, ln2_b, w_group, b_group, w_expert, b_expert, w1, b1, w2, b2):
        import jax, jax.numpy as jnp
        import numpy as np
        NHEAD = 16
        NUM_GROUPS = 4
        EXPERTS_PER_GROUP = 2
        LN_EPS = 1e-05

        def _layernorm(x, g, b):
            mu = jnp.mean(x, axis=-1, keepdims=True)
            var = jnp.mean(jnp.square(x - mu), axis=-1, keepdims=True)
            return (x - mu) * jax.lax.rsqrt(var + LN_EPS) * g + b

        def _mha(x, wi, bi, wo, bo):
            B, S, D = x.shape
            hd = D // NHEAD
            qkv = x @ wi.T + bi
            q, k, v = jnp.split(qkv, 3, axis=-1)

            def heads(t):
                return t.reshape(B, S, NHEAD, hd).transpose(0, 2, 1, 3)
            q, k, v = (heads(q), heads(k), heads(v))
            scores = jnp.einsum('bhqd,bhkd->bhqk', q, k) / jnp.sqrt(jnp.asarray(hd, x.dtype))
            attn = jax.nn.softmax(scores, axis=-1)
            o = jnp.einsum('bhqk,bhkd->bhqd', attn, v)
            o = o.transpose(0, 2, 1, 3).reshape(B, S, D)
            return o @ wo.T + bo

        def _hier_moe(x, w_group, b_group, w_expert, b_expert, w1, b1, w2, b2):
            B, S, D = x.shape
            xt = x.reshape(B * S, D)
            T = xt.shape[0]
            E = NUM_GROUPS * EXPERTS_PER_GROUP
            gp = jax.nn.softmax(xt @ w_group + b_group, axis=-1)
            g_idx = jnp.argmax(gp, axis=-1)
            g_prob = jnp.max(gp, axis=-1)
            elog = jnp.einsum('td,gde->tge', xt, w_expert) + b_expert
            ep = jax.nn.softmax(elog, axis=-1)
            ep_sel = jnp.take_along_axis(ep, g_idx[:, None, None], axis=1)[:, 0, :]
            e_idx_local = jnp.argmax(ep_sel, axis=-1)
            e_prob = jnp.max(ep_sel, axis=-1)
            flat_e = g_idx * EXPERTS_PER_GROUP + e_idx_local
            combine = jax.nn.one_hot(flat_e, E, dtype=xt.dtype) * (g_prob * e_prob)[:, None]
            h = jax.nn.relu(jnp.einsum('td,edf->etf', xt, w1) + b1[:, None, :])
            y = jnp.einsum('etf,efd->etd', h, w2) + b2[:, None, :]
            out = jnp.einsum('te,etd->td', combine, y)
            return out.reshape(B, S, D)
        attn_out = _mha(x, in_proj_w, in_proj_b, out_proj_w, out_proj_b)
        x = _layernorm(x + attn_out, ln1_g, ln1_b)
        moe_out = _hier_moe(x, w_group, b_group, w_expert, b_expert, w1, b1, w2, b2)
        x = _layernorm(x + moe_out, ln2_g, ln2_b)
        return x
    x = x + _L0_ffn_ref(_L0_cond_ref(cond_1024, x), L0_ffn_w_gate, L0_ffn_w_up, L0_ffn_w_down)
    x = x + _L1_ffn_ref(_L1_cond_ref(x, cond_1024, mask_Bx1x1xS_ff0, L1_cond_c_attn_w, L1_cond_c_attn_b, L1_cond_c_proj_w, L1_cond_c_proj_b, L1_cond_uk_w, L1_cond_uk_b, L1_cond_uv_w, L1_cond_uv_b), L1_ffn_in_proj_w, L1_ffn_in_proj_b, L1_ffn_out_proj_w, L1_ffn_out_proj_b, L1_ffn_ln1_g, L1_ffn_ln1_b, L1_ffn_ln2_g, L1_ffn_ln2_b, L1_ffn_w_group, L1_ffn_b_group, L1_ffn_w_expert, L1_ffn_b_expert, L1_ffn_w1, L1_ffn_b1, L1_ffn_w2, L1_ffn_b2)
    return x

_drawn_inputs = setup_inputs


def setup_inputs(seed=0):
    import zlib

    import numpy as np

    out = dict(_drawn_inputs(seed))
    spreads = {'L1_cond_c_attn_b': (0.0, 0.1),
     'L1_cond_c_proj_b': (0.0, 0.1),
     'L1_cond_uk_b': (0.0, 0.8),
     'L1_cond_uv_b': (0.0, 0.8),
     'L1_ffn_in_proj_b': (0.0, 0.1),
     'L1_ffn_out_proj_b': (0.0, 0.1),
     'L1_ffn_ln1_g': (1.0, 0.2),
     'L1_ffn_ln1_b': (0.0, 0.1),
     'L1_ffn_ln2_g': (1.0, 0.2),
     'L1_ffn_ln2_b': (0.0, 0.1),
     'L1_ffn_b_group': (0.0, 0.472),
     'L1_ffn_b_expert': (0.0, 0.8),
     'L1_ffn_b1': (0.0, 0.315),
     'L1_ffn_b2': (0.0, 0.1)}
    factors = {'L1_cond_c_attn_w': 3.075, 'L1_cond_uk_w': 8.0, 'L1_cond_uv_w': 8.0}
    for name, (base, spread) in spreads.items():
        noise = np.random.default_rng([zlib.crc32(name.encode()), seed]).standard_normal(out[name].shape)
        drawn = base * np.exp(spread * noise) if base else spread * noise
        out[name] = jnp.asarray(drawn.astype(out[name].dtype))
    for name, factor in factors.items():
        out[name] = (out[name] * factor).astype(out[name].dtype)
    return out
```

```python
import concourse.bass as bass
from concourse import mybir
from contextlib import ExitStack

P = 128
B, S, D = 2, 512, 128
NT = S // P
TILES = B * NT
INNER = 512
NC = INNER // P
HEADS = 16
HD = D // HEADS
GROUP = 4
ROUNDS = HEADS // GROUP
HC = 32
PARTS = 3
STACK = PARTS * PARTS * HD
SHIFT = STACK
MASK = SHIFT + 2
EXPERTS, NG, F = 8, 4, 256
FH = F // P
EPS = 1e-5
MAGIC = 1.5 * 2.0 ** 23
BIG = -1e30
INST = 4
LAG = 3
UNITS = 2 * HEADS


def program_order():
    order = [("setup", 0, 0)]
    for b in range(B):
        order += [("ffn_in", b, 0)]
        order += [("ffn_up", b, t) for t in range(NT)]
        order += [("ffn_down", b, t) for t in range(NT)]
        if b == 0:
            order += [("prepare", 0, 0)]
        order += [("x1t", b, 0), ("qkv", b, 0)]
    order += [("scores", 0, h) for h in range(HEADS)] + [("shift", 0, 0)]
    for i in range(HEADS + LAG):
        if i < HEADS:
            order += [("scores", 1, i)]
        if i == HEADS - 1:
            order += [("shift", 1, 0)]
        if i >= LAG:
            order += [("attend", 0, n) for n in (2 * (i - LAG), 2 * (i - LAG) + 1)]
    order += [("finish", 0, 0), ("qkv", 2, 0)]
    for i in range(HEADS + LAG):
        if i < HEADS:
            order += [("attend", 1, 2 * i), ("attend", 1, 2 * i + 1)]
        if i == HEADS - 1:
            order += [("finish", 1, 0), ("qkv", 3, 0)]
        if i >= LAG:
            order += [("scores", 2, i - LAG)]
    order += [("shift", 2, 0)]
    for i in range(HEADS + LAG):
        if i < HEADS:
            order += [("scores", 3, i)]
        if i == HEADS - 1:
            order += [("shift", 3, 0)]
        if i >= LAG:
            order += [("attend", 2, n) for n in (2 * (i - LAG), 2 * (i - LAG) + 1)]
    order += [("finish", 2, 0), ("moe_in", 0, 0)]
    for i in range(HEADS):
        order += [("attend", 3, 2 * i), ("attend", 3, 2 * i + 1)]
        if i % 2 == 1:
            order += [("expert", 0, i // 2)]
    order += [("expert", 0, EXPERTS), ("finish", 3, 0), ("moe_in", 1, 0), ("out", 0, 0)]
    order += [("expert", 1, e) for e in range(EXPERTS + 1)] + [("out", 1, 0)]
    return order


def unit(i):
    return i // (2 * GROUP), i // GROUP % 2, i % GROUP


def values_after(i):
    if i % GROUP == 1 and i > GROUP:
        return unit(i - GROUP)[:2]
    return None


def turn_back_after(i):
    if i % (2 * GROUP) == 3 and i > 2 * GROUP:
        return i // (2 * GROUP) - 1
    return None


def place_jobs(order):
    places = {n: {} for n in ("misc", "s0", "s1", "t0", "t1", "pv")}

    def add(place, *name):
        places[place][name] = len(places[place])

    for step, a, i in order:
        if step == "setup":
            add("misc", "sums"), add("t1", "ternary")
        if step == "prepare":
            add("misc", "wi"), add("t0", "turned"), add("misc", "small"), add("s0", "image_v")
        if step == "ffn_in":
            add("misc", "rt", a)
        if step == "ffn_up":
            add(f"t{i % 2}", "up", a, i)
        if step == "ffn_down":
            add(f"s{i % 2}", "r2t", a, i)
            if i == 0:
                add("pv", "down", a)
        if step == "x1t":
            add("misc", "x1t", a)
        if step == "qkv":
            for n in ("q", "k", "v"):
                add("misc", n, a)
        if step == "scores":
            for t in range(NT):
                add(f"s{t % 2}", "scores", a, i, t)
        if step == "shift":
            if a < 2:
                add("misc", "image", a)
            add("misc", "max_rows", a)
            if a < 2:
                add("misc", "image_rows", a)
        if step == "attend":
            add(f"t{i % 2}", "weights", a, i)
            if values_after(i) is not None and values_after(i)[1] == 1:
                add("pv", "values", a, values_after(i)[0])
            if turn_back_after(i) is not None:
                add("misc", "turn_back", a, turn_back_after(i))
        if step == "finish":
            add("pv", "values", a, ROUNDS - 1)
            add("misc", "turn_back", a, ROUNDS - 1)
            add("misc", "o_rows", a)
            if a < 2:
                add("misc", "x2t", a)
        if step == "moe_in":
            for n in ("sum", "x3t", "router", "combine", "bias2"):
                add("misc", n, a)
        if step == "expert":
            if i < EXPERTS:
                add("s0", "hidden", a, i), add("s1", "hidden", a, i)
            if i > 0:
                add("misc", "y", a, i - 1)
    return places


def blocks_of(a, u):
    out, col = [], 0
    for kb in (2 * u, 2 * u + 1):
        w = S - kb * P if a < 2 else S
        out.append((kb, col, w))
        col += w
    return out


def two_layers(nc, A, out):
    fp32 = mybir.dt.float32
    bf16 = mybir.dt.bfloat16
    ALU = mybir.AluOpType
    ACT = mybir.ActivationFunctionType
    AX = mybir.AxisListType.X

    ORDER = program_order()
    JOB = place_jobs(ORDER)

    def drows(ap, n, count):
        return bass.AP(tensor=ap.tensor, offset=ap.offset, ap=[[0, n], [1, count]])

    ctx = ExitStack()
    with ctx:
        def sb(name, shape, dt=fp32):
            return ctx.enter_context(nc.sbuf_tensor(name, shape, dt))

        def pb(name, shape):
            return ctx.enter_context(nc.psum_tensor(name, shape, fp32))

        def sem(name):
            return ctx.enter_context(nc.semaphore(name))

        parts_dram = [[nc.dram_tensor(f"parts_{n}{a}", (PARTS, P, S), bf16, kind="Internal").ap()
                       for n in "qk"] for a in range(INST)]
        shift_dram = [nc.dram_tensor(f"shift_{a}", (2 * HEADS, S), bf16, kind="Internal").ap()
                      for a in range(INST)]

        ident = sb("ident", [P, P])
        identb = sb("identb", [P, P], bf16)
        causal_q = sb("causal_q", [P, P], bf16)
        causal_k = sb("causal_k", [P, P], bf16)
        ones = sb("ones", [P, P])
        head_grid = sb("head_grid", [P, HD, HEADS])
        head_of = sb("head_of", [P, HEADS])
        pick = sb("pick", [2 * HEADS, HEADS], bf16)
        prior = sb("prior", [P, NT, NG])
        magic = sb("magic", [P, 1])
        halves = sb("halves", [P, NT])
        zrow = sb("zrow", [2, S], bf16)
        orow = sb("orow", [PARTS, S], bf16)

        X = sb("X", [P, TILES, D])
        Wca = sb("Wca", [P, 3 * D])
        Wcaq = sb("Wcaq", [P, 2, D])
        Wcp = sb("Wcp", [P, D])
        WinT = sb("WinT", [P, 3, D])
        WsqT = sb("WsqT", [P, 3, D])
        rows5 = sb("rows5", [5, D])
        rows5p = sb("rows5p", [5, D])
        rows17 = sb("rows17", [17, D])
        cols5 = sb("cols5", [P, 5])
        cols17 = sb("cols17", [P, 17])
        condr = sb("condr", [B, D])
        condT = sb("condT", [P, B])
        brow = sb("brow", [1, 5, D])
        Wr = sb("Wr", [P, NG + EXPERTS])
        rrow = sb("rrow", [1, NG + EXPERTS])
        B2 = sb("B2", [EXPERTS, D])
        norm_gb = sb("norm_gb", [P, 4, D])

        shared = sb("shared", [P, 7936])
        taken = {"first": 0, "later": 0}

        def part(when, shape, dt=fp32):
            n = 1
            for x in shape:
                n *= x
            words = n if dt == fp32 else n // 2
            ap = shared[:, taken[when]:taken[when] + words]
            taken[when] += words
            if dt != fp32:
                ap = ap.bitcast(dt)
            if len(shape) == 2:
                return ap.rearrange("p (a b) -> p a b", a=shape[0])
            if len(shape) == 3:
                return ap.rearrange("p (a b c) -> p a b c", a=shape[0], b=shape[1])
            return ap

        W3 = part("first", [3, INNER])
        xtmp = part("first", [TILES, D])
        R1 = part("first", [TILES, D], bf16)
        RT = part("first", [B, S], bf16)
        Wt = part("first", [3, INNER], bf16)
        WtT = part("first", [3 * NC, P], bf16)
        Win = part("first", [3, D])
        Wsq = part("first", [3, D])
        cond_all = part("first", [B, D])
        R2 = part("first", [2, INNER], bf16)
        mrow = part("first", [S])[0:B, :]
        mres = part("first", [S])[0:B, :]
        mparts = xtmp.rearrange("p t d -> p (t d)").bitcast(bf16)[0:B, 0:PARTS * S]\
            .rearrange("p (n s) -> p n s", n=PARTS)
        hid = part("later", [2, FH, S])
        acc = part("later", [B, NT, D])
        X3 = part("later", [NT, D])
        X3T = part("later", [S])
        OT = part("later", [INST, S])
        On = part("later", [NT, HEADS, HD])
        Ou = part("later", [2, S])

        wdot = sb("wdot", [P, 6, TILES])
        absum = sb("absum", [P, 3])
        wmean = sb("wmean", [P, 3])
        wscale = sb("wscale", [P, 3])
        q1 = sb("q1", [P, 5, TILES])
        q2 = sb("q2", [P, 4, TILES])
        R2T = sb("R2T", [P, 2, INNER], bf16)
        X1 = sb("X1", [P, TILES, D])

        XT = sb("XT", [P, 2, S])
        Qf = sb("Qf", [P, 2, S])
        Kf = sb("Kf", [P, S])
        qres = sb("qres", [P, S])
        kres = sb("kres", [P, S])
        Qp = sb("Qp", [P, PARTS, S], bf16)
        Kp = sb("Kp", [P, PARTS, S], bf16)
        Qs = sb("Qs", [P, 2, HEADS, S], bf16)
        Ks = sb("Ks", [P, 2, HEADS, S], bf16)
        wexp = Ks[:, 0, :, :].rearrange("p h s -> p (h s)").bitcast(fp32)
        W1 = wexp[:, 0:EXPERTS * F].rearrange("p (e f) -> p e f", e=EXPERTS)
        W2 = wexp[:, EXPERTS * F:].rearrange("p (e h d) -> p e h d", e=EXPERTS, h=FH)
        Vs = sb("Vs", [P, 2, NT, HEADS, HC])
        kimg = sb("kimg", [P, B])
        Kimg = sb("Kimg", [P, B, HEADS])
        Vimg = sb("Vimg", [HEADS, B, HEADS, HC])
        mx = sb("mx", [P, 2, NT, HEADS])
        nm = sb("nm", [P, 2, NT, 2, HEADS], bf16)
        nmT = sb("nmT", [2 * HEADS, 2, S], bf16)
        Pimg = sb("Pimg", [HEADS, 2, S])
        probs = sb("probs", [P, 2, GROUP, 2 * S])
        rden = sb("rden", [P, NT, GROUP])

        stats = sb("stats", [P, NT, 6])
        mv = sb("mv", [P, NT, 2])
        ve = sb("ve", [P, NT])
        rstd = sb("rstd", [P, NT])
        lg = sb("lg", [P, NT, NG + EXPERTS])
        dl = sb("dl", [P, NT, NG + EXPERTS])
        ex = sb("ex", [P, NT, NG + EXPERTS])
        rs = sb("rs", [P, 3, NT])
        rg = sb("rg", [P, 4, NT, NG])
        comb = sb("comb", [P, B, NT, NG, 2])
        combT = X[:, :, :].rearrange("p t d -> p (t d)")[0:EXPERTS, 0:S]

        early = probs[:, :, :, :].rearrange("p n j s -> p (n j s)")

        def H(b, t):
            return early[:, (b * NT + t) * INNER:(b * NT + t + 1) * INNER]

        def SG(t):
            return early[:, (TILES + t % 2) * INNER:(TILES + t % 2 + 1) * INNER]

        def Y(t):
            return early[:, (TILES + 2 + t % 2) * INNER:(TILES + 3 + t % 2) * INNER]

        wtmp = early[:, (TILES + 4) * INNER:(TILES + 7) * INNER].rearrange("p (n d) -> p n d", n=3)

        place = {"misc": pb("ps_misc", [P, S]), "pv": pb("ps_pv", [P, S]),
                 "s0": pb("ps_s0", [P, S]), "s1": pb("ps_s1", [P, S]),
                 "t0": pb("ps_t0", [P, 2 * S]), "t1": pb("ps_t1", [P, 2 * S])}
        full = {n: sem(f"{n}_full") for n in place}
        free = {n: sem(f"{n}_free") for n in place}

        def filled(n, *name):
            return JOB[n][name] + 1

        in_experts = sem("in_experts")
        in_x, in_w3, in_att, in_mask, in_moe = (sem(n) for n in
                                                ("in_x", "in_w3", "in_att", "in_mask", "in_moe"))
        pool_const = sem("pool_const")
        dve_step = sem("dve_step")
        pool_step = sem("pool_step")
        w_exp_in, w_exp = sem("w_exp_in"), sem("w_exp")
        r1_ready = sem("r1_ready")
        ternary_ready = sem("ternary_ready")
        setup_pe = sem("setup_pe")
        perm_ready = sem("perm_ready")
        sums_ready = sem("sums_ready")
        scale_ready = sem("scale_ready")
        silu_ready = sem("silu_ready")
        q2_ready = sem("q2_ready")
        y_ready = sem("y_ready")
        r2_ready = sem("r2_ready")
        qf_ready, kf_ready = sem("qf_ready"), sem("kf_ready")
        qhi_ready, khi_ready = sem("qhi_ready"), sem("khi_ready")
        qp_ready, kp_ready = sem("qp_ready"), sem("kp_ready")
        parts_q = [sem(f"parts_q{a}") for a in range(INST)]
        parts_k = [sem(f"parts_k{a}") for a in range(INST)]
        stacked = [sem(f"stacked{a}") for a in range(INST)]
        mparts_ready = sem("mparts_ready")
        half_done = sem("half_done")
        fixed_rows = sem("fixed_rows")
        stack_init = sem("stack_init")
        nm_ready = sem("nm_ready")
        shift_out = [sem(f"shift_out{a}") for a in range(INST)]
        shifted = [sem(f"shifted{a}") for a in range(INST)]
        ve_ready, rstd_ready = sem("ve_ready"), sem("rstd_ready")
        x3_ready, x3t_ready = sem("x3_ready"), sem("x3t_ready")
        dl_ready, ex_ready = sem("dl_ready"), sem("ex_ready")
        comb_ready, combT_ready = sem("comb_ready"), sem("combT_ready")
        hid_ready, y_read = sem("hid_ready"), sem("y_read")
        out_ready, stored = sem("out_ready"), sem("stored")

        block = ctx.enter_context(nc.Block())

        @block.sync
        def _(sp):
            for step, a, i in ORDER:
                b = a % 2
                if step == "setup":
                    sp.dma_start(cond_all[:, :, :].rearrange("p b d -> p (b d)"),
                                 drows(A["cond_1024"], P, B * D)).then_inc(in_x, 16)
                    xv = A["x"].rearrange("b (t p) d -> p (b t) d", p=P)
                    for b in range(B):
                        sp.dma_start(X[:, b * NT:(b + 1) * NT, :],
                                     xv[:, b * NT:(b + 1) * NT, :]).then_inc(in_x, 16)
                    for n, w in enumerate(("L0_ffn_w_gate", "L0_ffn_w_up")):
                        sp.dma_start(W3[:, n, :].rearrange("p (a d) -> p a d", d=D),
                                     A[w].rearrange("(a p) d -> p a d", p=P)).then_inc(in_w3, 16)
                    sp.dma_start(W3[:, 2, :], A["L0_ffn_w_down"]).then_inc(in_w3, 16)
                    sp.dma_start(mrow[:, :], A["mask_Bx1x1xS_ff0"].rearrange("b x y s -> (b x y) s"))\
                      .then_inc(in_mask, 16)
                    for dst, src in (
                            (rows5[0:2, :], A["L1_cond_c_attn_b"][0:2 * D].rearrange("(r d) -> r d", d=D)),
                            (rows5[2:4, :], A["L1_ffn_in_proj_b"][0:2 * D].rearrange("(r d) -> r d", d=D)),
                            (rows5[4:5, :], A["L1_cond_uk_b"].rearrange("(r d) -> r d", r=1)),
                            (rows17[0:16, :], A["L1_ffn_b1"].rearrange("e (h p) -> (e h) p", p=P)),
                            (rows17[16:17, :], A["L1_cond_c_proj_b"].rearrange("(r d) -> r d", r=1)),
                            (condr[:, :], A["cond_1024"]),
                            (Wca[:, :], A["L1_cond_c_attn_w"]),
                            (Wcp[:, :], A["L1_cond_c_proj_w"]),
                            (Win[:, :, :], A["L1_ffn_in_proj_w"].rearrange("(a p) d -> p a d", p=P)),
                            (Wsq[:, 0, :], A["L1_ffn_out_proj_w"]),
                            (Wsq[:, 1, :], A["L1_cond_uk_w"]),
                            (Wsq[:, 2, :], A["L1_cond_uv_w"]),
                            (brow[:, 0, :], A["L1_cond_c_attn_b"][2 * D:3 * D].rearrange("(r d) -> r d", r=1)),
                            (brow[:, 1, :], A["L1_ffn_in_proj_b"][2 * D:3 * D].rearrange("(r d) -> r d", r=1)),
                            (brow[:, 2, :], A["L1_cond_uv_b"].rearrange("(r d) -> r d", r=1)),
                            (brow[:, 3, :], A["L1_cond_c_proj_b"].rearrange("(r d) -> r d", r=1)),
                            (brow[:, 4, :], A["L1_ffn_out_proj_b"].rearrange("(r d) -> r d", r=1))):
                        sp.dma_start(dst, src).then_inc(in_att, 16)
                if step == "prepare":
                    sp.wait_ge(pool_const, 1)
                    sp.wait_ge(mparts_ready, 1)
                    for b in range(B):
                        for n in range(PARTS):
                            src = mparts[b:b + 1, n, :].unsqueeze(1).to_broadcast([1, HEADS, S])
                            sp.dma_start(Ks[MASK + n:MASK + n + 1, b, :, :], src).then_inc(fixed_rows, 16)
                        sp.dma_start(Qs[SHIFT:SHIFT + 2, b, :, :],
                                     zrow[:, :].unsqueeze(1).to_broadcast([2, HEADS, S])).then_inc(fixed_rows, 16)
                        sp.dma_start(Ks[SHIFT:SHIFT + 2, b, :, :],
                                     orow[0:2, :].unsqueeze(1).to_broadcast([2, HEADS, S])).then_inc(fixed_rows, 16)
                        sp.dma_start(Qs[MASK:MASK + PARTS, b, :, :],
                                     orow[:, :].unsqueeze(1).to_broadcast([PARTS, HEADS, S])).then_inc(fixed_rows, 16)
                if step == "qkv":
                    sp.wait_ge(qp_ready, a + 1)
                    sp.dma_start(parts_dram[a][0].rearrange("n p s -> p n s"), Qp[:, :, :]).then_inc(parts_q[a], 16)
                    sp.wait_ge(kp_ready, a + 1)
                    sp.dma_start(parts_dram[a][1].rearrange("n p s -> p n s"), Kp[:, :, :]).then_inc(parts_k[a], 16)
                    row = HEADS * S
                    sp.wait_ge(parts_q[a], 16)
                    for n in range(PARTS):
                        for m in range(PARTS):
                            r = (n * PARTS + m) * HD
                            sp.dma_start(Qs[r:r + HD, b, :, :].rearrange("p h s -> p (h s)"),
                                         parts_dram[a][0][n].rearrange("(d h) s -> d (h s)", h=HEADS))\
                              .then_inc(stacked[a], 16)
                    sp.wait_ge(parts_k[a], 16)
                    for n in range(PARTS):
                        r = n * PARTS * HD
                        sp.dma_start(Ks[r:r + PARTS * HD, b, :, :].rearrange("p h s -> p (h s)"),
                                     parts_dram[a][1].rearrange("m (d h) s -> (m d) (h s)", h=HEADS))\
                          .then_inc(stacked[a], 16)
                if step == "shift":
                    sp.wait_ge(free["misc"], filled("misc", "max_rows", a))
                    sp.dma_start(shift_dram[a], nmT[:, b, :]).then_inc(shift_out[a], 16)
                    sp.wait_ge(shift_out[a], 16)
                    sp.dma_start(Qs[SHIFT:SHIFT + 2, b, :, :].rearrange("p h s -> p (h s)"),
                                 shift_dram[a].rearrange("(n h) s -> n (h s)", h=HEADS)).then_inc(shifted[a], 16)
                if step == "finish" and a == 2:
                    sp.wait_ge(full["misc"], filled("misc", "turn_back", 2, ROUNDS - 1))
                    sp.dma_start(W1[:, :, :], A["L1_ffn_w1"].rearrange("e d f -> d e f")).then_inc(in_experts, 16)
                    sp.dma_start(W2[:, :, :, :], A["L1_ffn_w2"].rearrange("e (h p) d -> p e h d", p=P))\
                      .then_inc(in_experts, 16)
                if step == "out":
                    sp.wait_ge(out_ready, a + 1)
                    sp.dma_start(out[a].rearrange("(t p) d -> p t d", p=P), acc[:, a, :, :]).then_inc(stored, 16)
            sp.wait_ge(stored, 16 * B)

        @block.gpsimd
        def _(pool):
            done = [0]

            def then_wait(ins):
                done[0] += 1
                ins.then_inc(pool_step, 1)
                pool.wait_ge(pool_step, done[0])

            for step, a, i in ORDER:
                b = a % 2
                if step == "setup":
                    pool.memset(ident[:, :], 0.0)
                    pool.memset(identb[:, :], 0.0)
                    pool.memset(causal_q[:, :], 0.0)
                    pool.memset(causal_k[:, :], 0.0)
                    pool.memset(head_grid[:, :, :], 0.0)
                    then_wait(pool.memset(pick[:, :], 0.0))
                    pool.affine_select(out=ident[:, :], in_=ident[:, :], compare_op=ALU.not_equal, fill=1.0,
                                       base=0, pattern=[[-1, P]], channel_multiplier=1)
                    pool.affine_select(out=identb[:, :], in_=identb[:, :], compare_op=ALU.not_equal, fill=1.0,
                                       base=0, pattern=[[-1, P]], channel_multiplier=1)
                    pool.affine_select(out=causal_q[:, :], in_=causal_q[:, :], compare_op=ALU.is_ge, fill=BIG,
                                       base=0, pattern=[[-1, P]], channel_multiplier=1)
                    pool.affine_select(out=causal_k[:, :], in_=causal_k[:, :], compare_op=ALU.is_ge, fill=BIG,
                                       base=0, pattern=[[1, P]], channel_multiplier=-1)
                    pool.affine_select(out=head_grid[:, :, :], in_=head_grid[:, :, :],
                                       compare_op=ALU.not_equal, fill=1.0,
                                       base=0, pattern=[[-HEADS, HD], [-1, HEADS]], channel_multiplier=1)
                    then_wait(pool.affine_select(out=pick[:, :], in_=pick[:, :], compare_op=ALU.not_equal, fill=1.0,
                                                 base=0, pattern=[[-1, HEADS]], channel_multiplier=1))
                    pool.affine_select(out=pick[:, :], in_=pick[:, :], compare_op=ALU.not_equal, fill=1.0,
                                       base=-HEADS, pattern=[[-1, HEADS]], channel_multiplier=1)
                    pool.memset(ones[:, :], 1.0)
                    pool.memset(magic[:, :], MAGIC)
                    pool.memset(halves[:, :], -0.5)
                    for g in range(NG):
                        pool.memset(prior[:, :, g:g + 1], float(NG - g))
                    pool.memset(orow[:, :], 1.0)
                    pool.memset(zrow[:, :], 0.0).then_inc(pool_const, 1)
                    for n in range(2):
                        pool.memset(Vs[:, n, :, :, :], 0.0)
                    pool.memset(Vimg[:, :, :, :], 0.0).then_inc(pool_step, 1)
                    done[0] += 1
                    pool.wait_ge(pool_step, done[0])
                    for n in range(2):
                        pool.memset(Vs[:, n, :, :, HD:HD + 1], 1.0).then_inc(stack_init, 1)
                    for dst, src in (
                            (Wr[:, 0:NG], A["L1_ffn_w_group"]),
                            (Wr[:, NG:].rearrange("p (g e) -> p g e", e=2),
                             A["L1_ffn_w_expert"].rearrange("g d e -> d g e")),
                            (rrow[:, 0:NG], A["L1_ffn_b_group"].rearrange("(r n) -> r n", r=1)),
                            (rrow[:, NG:], A["L1_ffn_b_expert"].rearrange("(r g) e -> r (g e)", r=1)),
                            (B2[:, :], A["L1_ffn_b2"]),
                            (norm_gb[:, 0, :], drows(A["L1_ffn_ln1_g"], P, D)),
                            (norm_gb[:, 1, :], drows(A["L1_ffn_ln1_b"], P, D)),
                            (norm_gb[:, 2, :], drows(A["L1_ffn_ln2_g"], P, D)),
                            (norm_gb[:, 3, :], drows(A["L1_ffn_ln2_b"], P, D))):
                        pool.dma_start(dst, src).then_inc(in_moe, 16)
                if step == "qkv":
                    pool.wait_ge(khi_ready, a + 1)
                    then_wait(pool.tensor_tensor(kres[:, :], Kf[:, :], Kp[:, 0, :], ALU.subtract))
                    then_wait(pool.tensor_scalar(Kp[:, 1, :], kres[:, :], 1.0, None, ALU.mult))
                    pool.tensor_tensor(Kp[:, 2, :], kres[:, :], Kp[:, 1, :], ALU.subtract).then_inc(kp_ready, 1)
                if step in ("moe_in", "out"):
                    n = {("moe_in", 0): 1, ("moe_in", 1): 2, ("out", 0): 3, ("out", 1): 4}[(step, a)]
                    pool.wait_ge(ve_ready, n)
                    pool.tensor_tensor(rstd[:, :], ve[:, :], halves[:, :], ALU.pow).then_inc(rstd_ready, 1)

        @block.scalar
        def _(act):
            def take(n, *name):
                act.wait_ge(full[n], filled(n, *name))
                return place[n]

            for step, a, i in ORDER:
                b = a % 2
                if step == "setup":
                    act.wait_ge(w_exp_in, 1)
                    act.activation(wdot[:, 3, :], wdot[:, 1, :], ACT.Exp).then_inc(w_exp, 1)
                    ps = take("t1", "ternary")
                    act.activation(WtT[:, 0:8, :].rearrange("p a d -> p (a d)"),
                                   ps[:, 0:S].bitcast(bf16), ACT.Copy)
                    act.activation(WtT[:, 8:12, :].rearrange("p a d -> p (a d)"),
                                   ps[:, S:S + S // 2].bitcast(bf16), ACT.Copy).then_inc(free["t1"], 1)
                if step == "prepare":
                    ps = take("misc", "wi")
                    for n in range(3):
                        src = ps[:, n * D:(n + 1) * D]
                        if n < 2:
                            act.activation(WinT[:, n, :].rearrange("p (d h) -> p d h", h=HEADS),
                                           src.rearrange("p (h d) -> p d h", d=HD), ACT.Copy)
                        else:
                            act.activation(WinT[:, n, :], src, ACT.Copy).then_inc(free["misc"], 1)
                    ps = take("t0", "turned")
                    act.activation(WsqT[:, 0, :], ps[:, 0:D], ACT.Copy)
                    act.activation(WsqT[:, 1, :].rearrange("p (d h) -> p d h", h=HEADS),
                                   ps[:, D:2 * D].rearrange("p (h d) -> p d h", d=HD), ACT.Copy)
                    act.activation(WsqT[:, 2, :], ps[:, 2 * D:3 * D], ACT.Copy)
                    act.activation(condT[:, :], ps[:, 3 * D:3 * D + B], ACT.Copy).then_inc(free["t0"], 1)
                if step == "ffn_in":
                    ps = take("misc", "rt", a)
                    act.activation(RT[:, a, :], ps[:, 0:S // 2].bitcast(bf16), ACT.Copy).then_inc(free["misc"], 1)
                if step == "ffn_up":
                    t = a * NT + i
                    ps = take(f"t{i % 2}", "up", a, i)
                    act.wait_ge(scale_ready, 1)
                    act.activation(SG(i), ps[:, 0:INNER], ACT.Silu, scale=q1[:, 3, t:t + 1]).then_inc(silu_ready, 1)
                if step == "ffn_down":
                    t = a * NT + i
                    act.wait_ge(q2_ready, a + 1)
                    act.activation(Y(i), H(a, i), ACT.Identity, bias=magic[:, 0:1],
                                   scale=q2[:, 2, t:t + 1]).then_inc(y_ready, 1)
                    ps = take(f"s{i % 2}", "r2t", a, i)
                    act.activation(R2T[:, i % 2, :], ps[:, 0:INNER // 2].bitcast(bf16), ACT.Copy)\
                       .then_inc(free[f"s{i % 2}"], 1)
                if step == "x1t":
                    ps = take("misc", "x1t", a)
                    act.activation(XT[:, a, :], ps[:, :], ACT.Copy).then_inc(free["misc"], 1)
                if step == "qkv":
                    layer = a // 2
                    if a >= 1:
                        act.wait_ge(parts_q[a - 1], 16)
                        act.wait_ge(parts_k[a - 1], 16)
                    act.wait_ge(perm_ready, 1)
                    ps = take("misc", "q", a)
                    act.activation(Qf[:, b, :], ps[:, :], ACT.Identity, bias=cols5[:, 2 * layer:2 * layer + 1],
                                   scale=float(HD) ** -0.5).then_inc(free["misc"], 1)
                    act.wait_ge(free["misc"], filled("misc", "q", a))
                    act.activation(Qp[:, 0, :], Qf[:, b, :], ACT.Copy).then_inc(qhi_ready, 1)
                    ps = take("misc", "k", a)
                    act.activation(Kf[:, :], ps[:, :], ACT.Identity,
                                   bias=cols5[:, 2 * layer + 1:2 * layer + 2]).then_inc(free["misc"], 1)
                    act.wait_ge(free["misc"], filled("misc", "k", a))
                    act.activation(Kp[:, 0, :], Kf[:, :], ACT.Copy).then_inc(khi_ready, 1)
                if step == "shift":
                    ps = take("misc", "max_rows", a)
                    act.activation(nmT[:, b, :], ps[0:2 * HEADS, 0:S // 2].bitcast(bf16), ACT.Copy)\
                       .then_inc(free["misc"], 1)
                    if a < 2:
                        ps = take("misc", "image_rows", a)
                        act.activation(Pimg[:, b, :], ps[0:HEADS, :], ACT.Exp).then_inc(free["misc"], 1)
                if step == "attend":
                    r, u, j = unit(i)
                    half = 2 * (a * ROUNDS + r) + u
                    if j == 0 and half >= 2:
                        if u == 0:
                            act.wait_ge(half_done, half // 2)
                        else:
                            n = half // 2 - 1
                            act.wait_ge(full["pv"], filled("pv", "values", n // ROUNDS, n % ROUNDS))
                    ps = take(f"t{i % 2}", "weights", a, i)
                    w = sum(x[2] for x in blocks_of(a, u))
                    act.activation(probs[:, half % 2, j, 0:w], ps[:, 0:w], ACT.Exp).then_inc(free[f"t{i % 2}"], 1)
                if step == "finish":
                    ps = take("misc", "o_rows", a)
                    act.activation(OT[:, a, :], ps[:, :], ACT.Copy).then_inc(free["misc"], 1)
                    if a < 2:
                        ps = take("misc", "x2t", a)
                        act.activation(XT[:, a, :], ps[:, :], ACT.Identity, bias=cols17[:, 16:17])\
                           .then_inc(free["misc"], 1)
                if step == "moe_in":
                    ps = take("misc", "x3t", a)
                    act.activation(X3T[:, :], ps[:, :], ACT.Copy).then_inc(free["misc"], 1)
                    act.wait_ge(dl_ready, a + 1)
                    act.activation(ex[:, :, :], dl[:, :, :], ACT.Exp).then_inc(ex_ready, 1)

        @block.vector
        def _(dve):
            done = [0]

            def then_wait(ins):
                done[0] += 1
                ins.then_inc(dve_step, 1)
                dve.wait_ge(dve_step, done[0])

            def take(n, *name):
                dve.wait_ge(full[n], filled(n, *name))
                return place[n]

            norms = [0]

            def norm(src, dst, g):
                for t in range(NT):
                    last = dve.bn_stats(stats[:, t, :], src[:, t, :])
                then_wait(last)
                for t in range(NT):
                    last = dve.bn_aggr(mv[:, t, :], stats[:, t, :])
                then_wait(last)
                norms[0] += 1
                dve.tensor_scalar(ve[:, :], mv[:, :, 1], EPS, None, ALU.add).then_inc(ve_ready, 1)
                dve.wait_ge(rstd_ready, norms[0])
                for t in range(NT):
                    last = dve.tensor_scalar(dst[:, t, :], src[:, t, :], mv[:, t, 0:1], rstd[:, t:t + 1],
                                             ALU.subtract, ALU.mult)
                return last

            def gain(dst, g):
                gb = norm_gb[:, g:g + 1, :].to_broadcast([P, NT, D])
                bb = norm_gb[:, g + 1:g + 2, :].to_broadcast([P, NT, D])
                then_wait(dve.tensor_tensor(dst, dst, gb, ALU.mult))
                return dve.tensor_tensor(dst, dst, bb, ALU.add)

            for step, a, i in ORDER:
                b = a % 2
                if step == "setup":
                    dve.wait_ge(in_x, 16 * 3)
                    for n in range(B):
                        last = dve.tensor_tensor(
                            xtmp[:, n * NT:(n + 1) * NT, :], X[:, n * NT:(n + 1) * NT, :],
                            cond_all[:, n:n + 1, :].to_broadcast([P, NT, D]), ALU.mult)
                    then_wait(last)
                    then_wait(dve.tensor_reduce(wdot[:, 0, :], xtmp[:, :, :], AX, ALU.add))
                    then_wait(dve.tensor_scalar(wdot[:, 0, :], wdot[:, 0, :], float(D) ** -0.5, None, ALU.mult))
                    then_wait(dve.tensor_tensor(wdot[:, 5, 0:NT], wdot[:, 0, 0:NT], wdot[:, 0, NT:], ALU.max))
                    for n in range(B):
                        last = dve.tensor_tensor(wdot[:, 1, n * NT:(n + 1) * NT], wdot[:, 0, n * NT:(n + 1) * NT],
                                                 wdot[:, 5, 0:NT], ALU.subtract)
                    last.then_inc(w_exp_in, 1)
                    dve.wait_ge(in_w3, 16 * 3)
                    dve.tensor_reduce(absum[:, :], W3[:, :, :], AX, ALU.add, apply_absolute_value=True)\
                       .then_inc(sums_ready, 1)
                    dve.wait_ge(w_exp, 1)
                    then_wait(dve.tensor_tensor(wdot[:, 5, 0:NT], wdot[:, 3, 0:NT], wdot[:, 3, NT:], ALU.add))
                    then_wait(dve.reciprocal(wdot[:, 5, NT:], wdot[:, 5, 0:NT]))
                    for n in range(B):
                        last = dve.tensor_tensor(wdot[:, 0, n * NT:(n + 1) * NT], wdot[:, 3, n * NT:(n + 1) * NT],
                                                 wdot[:, 5, NT:], ALU.mult)
                    then_wait(last)
                    then_wait(dve.tensor_tensor(xtmp[:, :, :], X[:, :, :],
                                                wdot[:, 0, :].unsqueeze(2).to_broadcast([P, TILES, D]), ALU.mult))
                    then_wait(dve.tensor_reduce(q1[:, 0, :], xtmp[:, :, :], AX, ALU.max, apply_absolute_value=True))
                    then_wait(dve.tensor_scalar(q1[:, 0, :], q1[:, 0, :], 1e-5, None, ALU.max))
                    then_wait(dve.reciprocal(q1[:, 1, :], q1[:, 0, :]))
                    then_wait(dve.tensor_scalar(q1[:, 1, :], q1[:, 1, :], 127.0, None, ALU.mult))
                    then_wait(dve.tensor_tensor(xtmp[:, :, :], xtmp[:, :, :],
                                                q1[:, 1, :].unsqueeze(2).to_broadcast([P, TILES, D]), ALU.mult))
                    dve.tensor_scalar(R1[:, :, :], xtmp[:, :, :], MAGIC, MAGIC, ALU.add, ALU.subtract).then_inc(r1_ready, 1)
                    ps = take("misc", "sums")
                    then_wait(dve.tensor_scalar(wmean[:, :], ps[:, 0:3], 1.0 / (INNER * D), 1e-5, ALU.mult, ALU.max))
                    dve.reciprocal(wscale[:, :], wmean[:, :]).then_inc(free["misc"], 1)
                    dve.wait_ge(free["misc"], filled("misc", "sums"))
                    for n in range(3):
                        last = dve.tensor_scalar(wtmp[:, n, :], W3[:, n, :], wscale[:, n:n + 1], MAGIC,
                                                 ALU.mult, ALU.add)
                    then_wait(last)
                    then_wait(dve.tensor_scalar(wtmp[:, :, :], wtmp[:, :, :], MAGIC, 1.0, ALU.subtract, ALU.min))
                    dve.tensor_scalar(Wt[:, :, :], wtmp[:, :, :], -1.0, None, ALU.max).then_inc(ternary_ready, 1)
                    then_wait(dve.tensor_scalar(q1[:, 2, :], q1[:, 0, :], 1.0 / 127.0, None, ALU.mult))
                    dve.tensor_scalar(q1[:, 4, :], q1[:, 2, :], wmean[:, 1:2], None, ALU.mult)
                    dve.tensor_scalar(q1[:, 3, :], q1[:, 2, :], wmean[:, 0:1], None, ALU.mult).then_inc(scale_ready, 1)
                if step == "prepare":
                    dve.wait_ge(in_att, 16 * 17)
                    dve.tensor_copy(rows5p[:, :].rearrange("r (d h) -> r d h", h=HEADS),
                                    rows5[:, :].rearrange("r (h d) -> r d h", d=HD)).then_inc(setup_pe, 1)
                    for n in range(2):
                        last = dve.tensor_copy(Wcaq[:, n, :].rearrange("p (d h) -> p d h", h=HEADS),
                                               Wca[:, n * D:(n + 1) * D].rearrange("p (h d) -> p d h", d=HD))
                    then_wait(last)
                    dve.wait_ge(in_mask, 16)
                    then_wait(dve.tensor_copy(mparts[:, 0, :], mrow[:, :]))
                    then_wait(dve.tensor_tensor(mres[:, :], mrow[:, :], mparts[:, 0, :], ALU.subtract))
                    then_wait(dve.tensor_copy(mparts[:, 1, :], mres[:, :]))
                    dve.tensor_tensor(mparts[:, 2, :], mres[:, :], mparts[:, 1, :], ALU.subtract)\
                       .then_inc(mparts_ready, 1)
                    then_wait(dve.tensor_tensor(brow[:, 3, :], brow[:, 3, :], brow[:, 4, :], ALU.add))
                    dve.wait_ge(pool_const, 1)
                    dve.tensor_reduce(head_of[:, :], head_grid[:, :, :].rearrange("p d h -> p h d"), AX, ALU.add)
                    ps = take("misc", "small")
                    dve.tensor_copy(cols5[:, :], ps[:, 0:5])
                    then_wait(dve.tensor_copy(cols17[:, :], ps[:, 8:25]))
                    for n in range(2):
                        last = dve.tensor_scalar(cols5[:, 2 * n:2 * n + 1], cols5[:, 2 * n:2 * n + 1],
                                                 float(HD) ** -0.5, None, ALU.mult)
                    then_wait(last)
                    dve.tensor_scalar(kimg[:, :], ps[:, 32:32 + B], cols5[:, 4:5], None, ALU.add)\
                       .then_inc(free["misc"], 1)
                    dve.wait_ge(free["misc"], filled("misc", "small"))
                    for n in range(B):
                        last = dve.tensor_scalar(Kimg[:, n, :], head_of[:, :], kimg[:, n:n + 1], None, ALU.mult)
                    last.then_inc(perm_ready, 1)
                    dve.wait_ge(stack_init, 2)
                    ps = take("s0", "image_v")
                    own = ident[0:HEADS, 0:HEADS]
                    for n in range(B):
                        dve.tensor_tensor(Vimg[:, n, :, 0:HD],
                                          ps[0:HEADS, n * D:(n + 1) * D].rearrange("p (h d) -> p h d", d=HD),
                                          own.unsqueeze(2).to_broadcast([HEADS, HEADS, HD]), ALU.mult)
                        last = dve.tensor_copy(Vimg[:, n, :, HD:HD + 1], own.unsqueeze(2))
                    last.then_inc(free["s0"], 1)
                if step == "ffn_up":
                    t = a * NT + i
                    ps = take(f"t{i % 2}", "up", a, i)
                    dve.wait_ge(silu_ready, t + 1)
                    dve.tensor_tensor(H(a, i), SG(i), ps[:, INNER:2 * INNER], ALU.mult)\
                       .then_inc(free[f"t{i % 2}"], 1)
                    dve.wait_ge(free[f"t{i % 2}"], filled(f"t{i % 2}", "up", a, i))
                    last = dve.tensor_reduce(q2[:, 0, t:t + 1], H(a, i), AX, ALU.max, apply_absolute_value=True)
                    if i == NT - 1:
                        then_wait(last)
                        r = slice(a * NT, (a + 1) * NT)
                        then_wait(dve.tensor_tensor(q2[:, 0, r], q2[:, 0, r], q1[:, 4, r], ALU.mult))
                        then_wait(dve.tensor_scalar(q2[:, 0, r], q2[:, 0, r], 1e-5, None, ALU.max))
                        then_wait(dve.reciprocal(q2[:, 1, r], q2[:, 0, r]))
                        dve.tensor_scalar(q2[:, 3, r], q2[:, 0, r], wmean[:, 2:3], 1.0 / 127.0, ALU.mult, ALU.mult)
                        then_wait(dve.tensor_scalar(q2[:, 1, r], q2[:, 1, r], 127.0, None, ALU.mult))
                        dve.tensor_tensor(q2[:, 2, r], q2[:, 1, r], q1[:, 4, r], ALU.mult).then_inc(q2_ready, 1)
                if step == "ffn_down":
                    t = a * NT + i
                    dve.wait_ge(y_ready, t + 1)
                    dve.tensor_scalar(R2[:, t % 2, :], Y(i), MAGIC, None, ALU.subtract).then_inc(r2_ready, 1)
                if step == "x1t":
                    ps = take("pv", "down", a)
                    dve.wait_ge(q2_ready, a + 1)
                    for t in range(NT):
                        n = a * NT + t
                        last = dve.scalar_tensor_tensor(out=X1[:, n, :], in0=ps[:, t * D:(t + 1) * D],
                                                        scalar=q2[:, 3, n:n + 1], in1=X[:, n, :],
                                                        op0=ALU.mult, op1=ALU.add)
                    last.then_inc(free["pv"], 1)
                if step == "qkv":
                    dve.wait_ge(qhi_ready, a + 1)
                    then_wait(dve.tensor_tensor(qres[:, :], Qf[:, b, :], Qp[:, 0, :], ALU.subtract))
                    then_wait(dve.tensor_copy(Qp[:, 1, :], qres[:, :]))
                    dve.tensor_tensor(Qp[:, 2, :], qres[:, :], Qp[:, 1, :], ALU.subtract).then_inc(qp_ready, 1)
                    if a < 2:
                        dve.wait_ge(stack_init, 2)
                    ps = take("misc", "v", a)
                    dve.tensor_copy(Vs[:, b, :, :, 0:HD].rearrange("p t h d -> p (t h) d"),
                                    ps[:, :].rearrange("p (n d) -> p n d", d=HD)).then_inc(free["misc"], 1)
                if step == "scores":
                    for t in range(NT):
                        ps = take(f"s{t % 2}", "scores", a, i, t)
                        w = (t + 1) * P if a < 2 else S
                        dve.tensor_reduce(mx[:, b, t, i:i + 1], ps[:, 0:w], AX, ALU.max).then_inc(free[f"s{t % 2}"], 1)
                if step == "shift":
                    for n in range(2):
                        dve.wait_ge(free[f"s{n}"], filled(f"s{n}", "scores", a, HEADS - 1, NT - 2 + n))
                    m = mx[:, b, :, :]
                    if a < 2:
                        ps = take("misc", "image", a)
                        dve.tensor_tensor(m, ps[:, 0:NT * HEADS].rearrange("p (t h) -> p t h", h=HEADS), m, ALU.max)\
                           .then_inc(free["misc"], 1)
                        dve.wait_ge(free["misc"], filled("misc", "image", a))
                    then_wait(dve.tensor_scalar(nm[:, b, :, 0, :], m, -1.0, None, ALU.mult))
                    dve.scalar_tensor_tensor(out=nm[:, b, :, 1, :], in0=m, scalar=-1.0, in1=nm[:, b, :, 0, :],
                                             op0=ALU.mult, op1=ALU.subtract).then_inc(nm_ready, 1)
                if step in ("attend", "finish"):
                    mul = (ROUNDS - 1, 1) if step == "finish" else values_after(i)
                    back = ROUNDS - 1 if step == "finish" else turn_back_after(i)
                    if mul is not None and mul[1] == 1:
                        ps = take("pv", "values", a, mul[0])
                        dve.tensor_copy(Ou[:, mul[0] % 2, :], ps[:, :]).then_inc(free["pv"], 1)
                    if back is not None:
                        r = back
                        ps = take("misc", "turn_back", a, r)
                        tb = ps[:, :].rearrange("p (t j c) -> p t j c", j=GROUP, c=HC)
                        then_wait(dve.reciprocal(rden[:, :, :], tb[:, :, :, HD]))
                        dve.tensor_tensor(On[:, :, r * GROUP:(r + 1) * GROUP, :], tb[:, :, :, 0:HD],
                                          rden[:, :, :].unsqueeze(3).to_broadcast([P, NT, GROUP, HD]), ALU.mult)\
                           .then_inc(free["misc"], 1)
                if step == "moe_in":
                    dve.wait_ge(in_moe, 16 * 9)
                    ps = take("misc", "sum", a)
                    norm(ps[:, :].rearrange("p (t d) -> p t d", d=D), X3[:, :, :], 0).then_inc(free["misc"], 1)
                    dve.wait_ge(free["misc"], filled("misc", "sum", a))
                    gain(X3[:, :, :], 0).then_inc(x3_ready, 1)
                    ps = take("misc", "router", a)
                    dve.tensor_copy(lg[:, :, :], ps[:, 0:NT * (NG + EXPERTS)]
                                    .rearrange("p (t n) -> p t n", t=NT)).then_inc(free["misc"], 1)
                    dve.wait_ge(free["misc"], filled("misc", "router", a))
                    pair = lg[:, :, NG:].rearrange("p t (g e) -> p t g e", e=2)
                    dve.tensor_reduce(rs[:, 0, :], lg[:, :, 0:NG], AX, ALU.max)
                    then_wait(dve.tensor_tensor(rg[:, 0, :, :], pair[:, :, :, 0], pair[:, :, :, 1], ALU.max))
                    dve.tensor_tensor(dl[:, :, 0:NG], lg[:, :, 0:NG],
                                      rs[:, 0, :].unsqueeze(2).to_broadcast([P, NT, NG]), ALU.subtract)
                    then_wait(dve.tensor_tensor(dl[:, :, NG:].rearrange("p t (g e) -> p t g e", e=2), pair,
                                                rg[:, 0, :, :].unsqueeze(3).to_broadcast([P, NT, NG, 2]),
                                                ALU.subtract))
                    dve.scalar_tensor_tensor(out=rg[:, 1, :, :], in0=dl[:, :, 0:NG], scalar=0.0,
                                             in1=prior[:, :, :], op0=ALU.is_equal, op1=ALU.mult).then_inc(dl_ready, 1)
                    dve.wait_ge(dl_ready, a + 1)
                    then_wait(dve.tensor_reduce(rs[:, 1, :], rg[:, 1, :, :], AX, ALU.max))
                    dve.tensor_tensor(rg[:, 2, :, :], rg[:, 1, :, :],
                                      rs[:, 1, :].unsqueeze(2).to_broadcast([P, NT, NG]), ALU.is_equal)
                    dve.wait_ge(ex_ready, a + 1)
                    pex = ex[:, :, NG:].rearrange("p t (g e) -> p t g e", e=2)
                    dve.tensor_reduce(rs[:, 2, :], ex[:, :, 0:NG], AX, ALU.add)
                    then_wait(dve.tensor_tensor(rg[:, 3, :, :], pex[:, :, :, 0], pex[:, :, :, 1], ALU.add))
                    then_wait(dve.tensor_tensor(rg[:, 3, :, :], rg[:, 3, :, :],
                                                rs[:, 2, :].unsqueeze(2).to_broadcast([P, NT, NG]), ALU.mult))
                    then_wait(dve.reciprocal(rg[:, 0, :, :], rg[:, 3, :, :]))
                    then_wait(dve.tensor_tensor(rg[:, 0, :, :], rg[:, 0, :, :], rg[:, 2, :, :], ALU.mult))
                    dpair = dl[:, :, NG:].rearrange("p t (g e) -> p t g e", e=2)
                    then_wait(dve.scalar_tensor_tensor(out=comb[:, a, :, :, 0], in0=dpair[:, :, :, 0], scalar=0.0,
                                                       in1=rg[:, 0, :, :], op0=ALU.is_equal, op1=ALU.mult))
                    dve.tensor_tensor(comb[:, a, :, :, 1], rg[:, 0, :, :], comb[:, a, :, :, 0], ALU.subtract)\
                       .then_inc(comb_ready, 1)
                    dve.wait_ge(comb_ready, a + 1)
                    ps = take("misc", "combine", a)
                    dve.tensor_copy(combT[:, :], ps[0:EXPERTS, :]).then_inc(free["misc"], 1)
                    ps = take("misc", "bias2", a)
                    dve.tensor_tensor(acc[:, a, :, :], ps[:, :].rearrange("p (t d) -> p t d", d=D),
                                      X3[:, :, :], ALU.add).then_inc(free["misc"], 1)
                if step == "expert":
                    if i < EXPERTS:
                        for h in range(FH):
                            ps = take(f"s{h}", "hidden", a, i)
                            dve.tensor_scalar(hid[:, i % 2, h, :], ps[:, :], cols17[:, 2 * i + h:2 * i + h + 1], 0.0,
                                              ALU.add, ALU.max).then_inc(free[f"s{h}"], 1)
                    if i > 0:
                        if i == 1:
                            dve.wait_ge(free["misc"], filled("misc", "bias2", a))
                        else:
                            dve.wait_ge(free["misc"], filled("misc", "y", a, i - 2))
                        e = i - 1
                        ps = take("misc", "y", a, e)
                        for t in range(NT):
                            last = dve.scalar_tensor_tensor(
                                out=acc[:, a, t, :], in0=ps[:, t * D:(t + 1) * D],
                                scalar=comb[:, a, t, e // 2, e % 2:e % 2 + 1], in1=acc[:, a, t, :],
                                op0=ALU.mult, op1=ALU.add)
                        last.then_inc(free["misc"], 1)
                if step == "out":
                    dve.wait_ge(free["misc"], filled("misc", "y", a, EXPERTS - 1))
                    then_wait(norm(acc[:, a, :, :], acc[:, a, :, :], 2))
                    then_wait(gain(acc[:, a, :, :], 2))
                    dve.tensor_tensor(acc[:, a, :, :], acc[:, a, :, :], X1[:, a * NT:(a + 1) * NT, :], ALU.add)\
                       .then_inc(out_ready, 1)

        @block.tensor
        def _(pe):
            def put(n, *name):
                if JOB[n][name] > 0:
                    pe.wait_ge(free[n], JOB[n][name])
                return place[n]

            def times_values(a, r, u):
                b, half = a % 2, 2 * (a * ROUNDS + r) + u
                ps = put("pv", "values", a, r) if u == 0 else place["pv"]
                for i in (2 * GROUP * r + GROUP * u + 2, 2 * GROUP * r + GROUP * u + 3):
                    pe.wait_ge(free[f"t{i % 2}"], filled(f"t{i % 2}", "weights", a, i))
                for kb, col, w in blocks_of(a, u):
                    for j in range(GROUP):
                        mm = pe.matmul(ps[j * HC:(j + 1) * HC, S - w:S], Vs[:, b, kb, r * GROUP + j, :],
                                       probs[:, half % 2, j, col:col + w], start=(kb == 0),
                                       stop=(kb == NT - 1 and a >= 2))
                if u == 0:
                    mm.then_inc(half_done, 1)
                    return
                if a < 2:
                    if r == 0:
                        pe.wait_ge(free["misc"], filled("misc", "image_rows", a))
                    for j in range(GROUP):
                        mm = pe.matmul(ps[j * HC:(j + 1) * HC, :], Vimg[:, b, r * GROUP + j, :],
                                       Pimg[:, b, :], start=False, stop=True)
                mm.then_inc(full["pv"], 1)

            def turn_back(a, r):
                pe.wait_ge(free["pv"], filled("pv", "values", a, r))
                ps = put("misc", "turn_back", a, r)
                for t in range(NT):
                    mm = pe.transpose(ps[:, t * P:(t + 1) * P], Ou[:, r % 2, t * P:(t + 1) * P], ident[:, :])
                mm.then_inc(full["misc"], 1)

            for step, a, i in ORDER:
                b = a % 2
                if step == "setup":
                    pe.wait_ge(pool_const, 1)
                    pe.wait_ge(sums_ready, 1)
                    ps = put("misc", "sums")
                    pe.matmul(ps[:, 0:3], ones[:, :], absum[:, :], start=True, stop=True).then_inc(full["misc"], 1)
                    pe.wait_ge(ternary_ready, 1)
                    ps = put("t1", "ternary")
                    for n in range(8):
                        pe.transpose(ps[:, n * P // 2:(n + 1) * P // 2].bitcast(bf16),
                                     Wt[:, n // NC, (n % NC) * P:(n % NC + 1) * P], identb[:, :])
                    for n in range(NC):
                        mm = pe.transpose(ps[:, S + n * P // 2:S + (n + 1) * P // 2].bitcast(bf16),
                                          Wt[:, 2, n * P:(n + 1) * P], identb[:, :])
                    mm.then_inc(full["t1"], 1)
                if step == "prepare":
                    pe.wait_ge(in_att, 16 * 17)
                    ps = put("misc", "wi")
                    for n in range(3):
                        mm = pe.transpose(ps[:, n * D:(n + 1) * D], Win[:, n, :], ident[:, :])
                    mm.then_inc(full["misc"], 1)
                    ps = put("t0", "turned")
                    for n in range(3):
                        pe.transpose(ps[:, n * D:(n + 1) * D], Wsq[:, n, :], ident[:, :])
                    pe.transpose(ps[:, 3 * D:3 * D + B], condr[:, :], ident[0:B, 0:B]).then_inc(full["t0"], 1)
                    pe.wait_ge(setup_pe, 1)
                    ps = put("misc", "small")
                    pe.transpose(ps[:, 0:5], rows5p[:, :], ident[0:5, 0:5])
                    pe.transpose(ps[:, 8:25], rows17[:, :], ident[0:17, 0:17])
                    pe.wait_ge(free["t0"], filled("t0", "turned"))
                    pe.matmul(ps[:, 32:32 + B], WsqT[:, 1, :], condT[:, :], start=True, stop=True)\
                      .then_inc(full["misc"], 1)
                    ps = put("s0", "image_v")
                    for n in range(B):
                        pe.matmul(ps[0:HEADS, n * D:(n + 1) * D], condT[:, n:n + 1].to_broadcast([P, HEADS]),
                                  WsqT[:, 2, :], start=True, stop=False)
                        mm = pe.matmul(ps[0:HEADS, n * D:(n + 1) * D], ones[0:1, 0:HEADS], brow[:, 2, :],
                                       start=False, stop=True)
                    mm.then_inc(full["s0"], 1)
                if step == "ffn_in":
                    pe.wait_ge(r1_ready, 1)
                    ps = put("misc", "rt", a)
                    for t in range(NT):
                        mm = pe.transpose(ps[:, t * P // 2:(t + 1) * P // 2].bitcast(bf16),
                                          R1[:, a * NT + t, :], identb[:, :])
                    mm.then_inc(full["misc"], 1)
                if step == "ffn_up":
                    if i == 0:
                        pe.wait_ge(free["misc"], filled("misc", "rt", a))
                        pe.wait_ge(free["t1"], filled("t1", "ternary"))
                    ps = put(f"t{i % 2}", "up", a, i)
                    for n in range(2):
                        mm = pe.matmul(ps[:, n * INNER:(n + 1) * INNER], RT[:, a, i * P:(i + 1) * P],
                                       WtT[:, n * NC:(n + 1) * NC, :].rearrange("p a d -> p (a d)"),
                                       start=True, stop=True)
                    mm.then_inc(full[f"t{i % 2}"], 1)
                if step == "ffn_down":
                    t = a * NT + i
                    pe.wait_ge(r2_ready, t + 1)
                    ps = put(f"s{i % 2}", "r2t", a, i)
                    for c in range(NC):
                        mm = pe.transpose(ps[:, c * P // 2:(c + 1) * P // 2].bitcast(bf16),
                                          R2[:, t % 2, c * P:(c + 1) * P], identb[:, :])
                    mm.then_inc(full[f"s{i % 2}"], 1)
                    pe.wait_ge(free[f"s{i % 2}"], filled(f"s{i % 2}", "r2t", a, i))
                    if i == 0:
                        put("pv", "down", a)
                    for c in range(NC):
                        mm = pe.matmul(place["pv"][:, i * D:(i + 1) * D], R2T[:, i % 2, c * P:(c + 1) * P],
                                       WtT[:, 2 * NC + c, :], start=(c == 0), stop=(c == NC - 1))
                    if i == NT - 1:
                        mm.then_inc(full["pv"], 1)
                if step == "x1t":
                    pe.wait_ge(free["pv"], filled("pv", "down", a))
                    ps = put("misc", "x1t", a)
                    for t in range(NT):
                        mm = pe.transpose(ps[:, t * P:(t + 1) * P], X1[:, a * NT + t, :], ident[:, :])
                    mm.then_inc(full["misc"], 1)
                if step == "qkv":
                    if a < 2:
                        pe.wait_ge(perm_ready, 1)
                        pe.wait_ge(free["misc"], filled("misc", "x1t", a))
                    else:
                        pe.wait_ge(free["misc"], filled("misc", "x2t", a - 2))
                    wq, wk = (Wcaq[:, 0, :], Wcaq[:, 1, :]) if a < 2 else (WinT[:, 0, :], WinT[:, 1, :])
                    wv = Wca[:, 2 * D:3 * D] if a < 2 else WinT[:, 2, :]
                    ps = put("misc", "q", a)
                    pe.matmul(ps[:, :], wq, XT[:, b, :], start=True, stop=True).then_inc(full["misc"], 1)
                    ps = put("misc", "k", a)
                    pe.matmul(ps[:, :], wk, XT[:, b, :], start=True, stop=True).then_inc(full["misc"], 1)
                    ps = put("misc", "v", a)
                    for t in range(NT):
                        pe.matmul(ps[:, t * D:(t + 1) * D], XT[:, b, t * P:(t + 1) * P], wv, start=True, stop=False)
                        mm = pe.matmul(ps[:, t * D:(t + 1) * D], ones[0:1, :], brow[:, a // 2, :],
                                       start=False, stop=True)
                    mm.then_inc(full["misc"], 1)
                if step == "scores":
                    if i == 0:
                        pe.wait_ge(stacked[a], 16 * 12)
                        if a < 2:
                            pe.wait_ge(fixed_rows, 16 * 2 * (PARTS + 3))
                    rows = MASK + PARTS if a < 2 else STACK
                    for t in range(NT):
                        ps = put(f"s{t % 2}", "scores", a, i, t)
                        w = (t + 1) * P if a < 2 else S
                        mm = pe.matmul(ps[:, 0:w], Qs[0:rows, b, i, t * P:(t + 1) * P], Ks[0:rows, b, i, 0:w],
                                       start=True, stop=(a >= 2))
                        if a < 2:
                            mm = pe.matmul(ps[:, w - P:w], identb[:, :], causal_q[:, :], start=False, stop=True)
                        mm.then_inc(full[f"s{t % 2}"], 1)
                if step == "shift":
                    if a < 2:
                        ps = put("misc", "image", a)
                        for t in range(NT):
                            mm = pe.matmul(ps[:, t * HEADS:(t + 1) * HEADS], Qf[:, b, t * P:(t + 1) * P],
                                           Kimg[:, b, :], start=True, stop=True)
                        mm.then_inc(full["misc"], 1)
                    pe.wait_ge(nm_ready, a + 1)
                    ps = put("misc", "max_rows", a)
                    for t in range(NT):
                        mm = pe.transpose(ps[0:2 * HEADS, t * P // 2:(t + 1) * P // 2].bitcast(bf16),
                                          nm[:, b, t, :, :].rearrange("p n h -> p (n h)"), identb[:, :])
                    mm.then_inc(full["misc"], 1)
                    if a < 2:
                        pe.wait_ge(free["misc"], filled("misc", "max_rows", a))
                        ps = put("misc", "image_rows", a)
                        pe.matmul(ps[0:HEADS, :], Kimg[:, b, :], Qf[:, b, :], start=True, stop=False)
                        pe.matmul(ps[0:HEADS, :], pick[:, :], nmT[:, b, :], start=False, stop=True)\
                          .then_inc(full["misc"], 1)
                if step == "attend":
                    if i == 0:
                        pe.wait_ge(shifted[a], 16)
                    rows = MASK + PARTS if a < 2 else MASK
                    r, u, j = unit(i)
                    h = r * GROUP + j
                    ps = put(f"t{i % 2}", "weights", a, i)
                    for kb, col, w in blocks_of(a, u):
                        mm = pe.matmul(ps[:, col:col + w], Ks[0:rows, b, h, kb * P:(kb + 1) * P],
                                       Qs[0:rows, b, h, S - w:S], start=True, stop=(a >= 2))
                        if a < 2:
                            mm = pe.matmul(ps[:, col:col + P], identb[:, :], causal_k[:, :],
                                           start=False, stop=True)
                    mm.then_inc(full[f"t{i % 2}"], 1)
                    if values_after(i) is not None:
                        times_values(a, *values_after(i))
                    if turn_back_after(i) is not None:
                        turn_back(a, turn_back_after(i))
                if step == "finish":
                    times_values(a, ROUNDS - 1, 1)
                    turn_back(a, ROUNDS - 1)
                    pe.wait_ge(free["misc"], filled("misc", "turn_back", a, ROUNDS - 1))
                    ps = put("misc", "o_rows", a)
                    for t in range(NT):
                        mm = pe.transpose(ps[:, t * P:(t + 1) * P],
                                          On[:, t, :, :].rearrange("p h d -> p (h d)"), ident[:, :])
                    mm.then_inc(full["misc"], 1)
                    if a < 2:
                        pe.wait_ge(free["misc"], filled("misc", "o_rows", a))
                        ps = put("misc", "x2t", a)
                        pe.matmul(ps[:, :], Wcp[:, :], OT[:, a, :], start=True, stop=True).then_inc(full["misc"], 1)
                if step == "moe_in":
                    pe.wait_ge(free["misc"], filled("misc", "o_rows", 2 + a))
                    ps = put("misc", "sum", a)
                    for t in range(NT):
                        o = ps[:, t * D:(t + 1) * D]
                        pe.matmul(o, OT[:, a, t * P:(t + 1) * P], Wcp[:, :], start=True, stop=False)
                        pe.matmul(o, OT[:, 2 + a, t * P:(t + 1) * P], WsqT[:, 0, :], start=False, stop=False)
                        mm = pe.matmul(o, ones[0:1, :], brow[:, 3, :], start=False, stop=True)
                    mm.then_inc(full["misc"], 1)
                    pe.wait_ge(x3_ready, a + 1)
                    ps = put("misc", "x3t", a)
                    for t in range(NT):
                        mm = pe.transpose(ps[:, t * P:(t + 1) * P], X3[:, t, :], ident[:, :])
                    mm.then_inc(full["misc"], 1)
                    pe.wait_ge(in_moe, 16 * 9)
                    pe.wait_ge(free["misc"], filled("misc", "x3t", a))
                    ps = put("misc", "router", a)
                    n = NG + EXPERTS
                    for t in range(NT):
                        pe.matmul(ps[:, t * n:(t + 1) * n], X3T[:, t * P:(t + 1) * P], Wr[:, :],
                                  start=True, stop=False)
                        mm = pe.matmul(ps[:, t * n:(t + 1) * n], ones[0:1, :], rrow[:, :], start=False, stop=True)
                    mm.then_inc(full["misc"], 1)
                    pe.wait_ge(comb_ready, a + 1)
                    ps = put("misc", "combine", a)
                    for t in range(NT):
                        mm = pe.transpose(ps[0:EXPERTS, t * P:(t + 1) * P],
                                          comb[:, a, t, :, :].rearrange("p g e -> p (g e)"), ident[:, :])
                    mm.then_inc(full["misc"], 1)
                    pe.wait_ge(free["misc"], filled("misc", "combine", a))
                    ps = put("misc", "bias2", a)
                    for t in range(NT):
                        mm = pe.matmul(ps[:, t * D:(t + 1) * D], combT[:, t * P:(t + 1) * P], B2[:, :],
                                       start=True, stop=True)
                    mm.then_inc(full["misc"], 1)
                if step == "expert":
                    if a == 0 and i == 0:
                        pe.wait_ge(in_experts, 16 * 2)
                    if i < EXPERTS:
                        for h in range(FH):
                            ps = put(f"s{h}", "hidden", a, i)
                            pe.matmul(ps[:, :], W1[:, i, h * P:(h + 1) * P], X3T[:, :], start=True, stop=True)\
                              .then_inc(full[f"s{h}"], 1)
                    if i > 0:
                        e = i - 1
                        for h in range(FH):
                            pe.wait_ge(free[f"s{h}"], filled(f"s{h}", "hidden", a, e))
                        ps = put("misc", "y", a, e)
                        for t in range(NT):
                            for h in range(FH):
                                mm = pe.matmul(ps[:, t * D:(t + 1) * D], hid[:, e % 2, h, t * P:(t + 1) * P],
                                               W2[:, e, h, :], start=(h == 0), stop=(h == FH - 1))
                        mm.then_inc(full["misc"], 1)


INPUTS = [
    "x", "cond_1024", "mask_Bx1x1xS_ff0", "L0_ffn_w_gate", "L0_ffn_w_up", "L0_ffn_w_down",
    "L1_cond_c_attn_w", "L1_cond_c_attn_b", "L1_cond_c_proj_w", "L1_cond_c_proj_b", "L1_cond_uk_w",
    "L1_cond_uk_b", "L1_cond_uv_w", "L1_cond_uv_b", "L1_ffn_in_proj_w", "L1_ffn_in_proj_b",
    "L1_ffn_out_proj_w", "L1_ffn_out_proj_b", "L1_ffn_ln1_g", "L1_ffn_ln1_b", "L1_ffn_ln2_g",
    "L1_ffn_ln2_b", "L1_ffn_w_group", "L1_ffn_b_group", "L1_ffn_w_expert", "L1_ffn_b_expert",
    "L1_ffn_w1", "L1_ffn_b1", "L1_ffn_w2", "L1_ffn_b2",
]


def kernel(**inputs):
    import numpy as _np
    import concourse.bacc as _bacc
    from concourse import mybir as _mybir
    from concourse.bass_utils import run_bass_kernel_spmd as _run

    nc = _bacc.Bacc("TRN2", target_bir_lowering=False, num_devices=1)
    arrays, aps = {}, {}
    for name in INPUTS:
        a = _np.ascontiguousarray(inputs[name])
        arrays[f"in_{name}"] = a
        aps[name] = nc.dram_tensor(f"in_{name}", a.shape, _mybir.dt.from_np(a.dtype), kind="ExternalInput").ap()
    out = nc.dram_tensor("out_x", (B, S, D), _mybir.dt.float32, kind="ExternalOutput").ap()
    two_layers(nc, aps, out)
    r = _run(nc, [arrays], core_ids=[0])
    return r.results[0]["out_x"]
```

```python
import concourse.bass as bass
from concourse import mybir
from contextlib import ExitStack

P = 128
B, S, D = 2, 512, 128
NT = S // P
TILES = B * NT
INNER = 512
NC = INNER // P
HEADS = 16
HD = D // HEADS
GROUP = 4
ROUNDS = HEADS // GROUP
HC = 32
PARTS = 3
STACK = PARTS * PARTS * HD
SHIFT = STACK
MASK = SHIFT + 2
EXPERTS, NG, F = 8, 4, 256
FH = F // P
EPS = 1e-5
MAGIC = 1.5 * 2.0 ** 23
BIG = -1e30
INST = 4
UNITS = 2 * HEADS


def spread(steps, begin, end):
    return [(begin + (end - begin) * n / len(steps), step) for n, step in enumerate(steps)]


def attention(a):
    steps = []
    for i in range(UNITS + 2 * GROUP):
        if i < UNITS:
            steps += [("attend", a, i)]
        if i > GROUP and i % GROUP in (1, 2) and (i - GROUP) // GROUP * 2 < ROUNDS * NT:
            steps += [("values", a, (i - GROUP) // GROUP * 2 + i % GROUP - 1)]
        if i > 2 * GROUP and i % (2 * GROUP) == 4:
            steps += [("turn_back", a, i // (2 * GROUP) - 1)]
    n = steps.index(("attend", a, UNITS - 1)) + 1
    return steps[:n], steps[n:] + [("o_rows", a, 0)]


def program_order():
    scores = [[("scores", a, n) for n in range(HEADS * NT)] for a in range(INST)]
    units, ends = zip(*(attention(a) for a in range(INST)))
    qkv = [[("q", a, 0), ("k", a, 0), ("v", a, 0)] for a in range(INST)]
    shift = [[("max", a, 0), ("max_rows", a, 0)] + [("image_rows", a, 0)] * (a < 2) for a in range(INST)]
    ffn_up = [[("ffn_in", b, 0)] + [("ffn_up", b, t) for t in range(NT)] for b in range(B)]
    ffn_down = [[("ffn_down", b, t) for t in range(NT)] + [("x1t", b, 0)] for b in range(B)]
    moe_in = [[(n, b, 0) for n in ("sum", "x3t", "router", "route", "combine", "bias2")]
              for b in range(B)]
    experts = [[("expert", b, e) for e in range(EXPERTS + 1)] for b in range(B)]
    plan = []
    for steps, begin, end in (
            ([("setup", 0, 0)] + ffn_up[0] + [("turn_weights", 0, 0)] + ffn_down[0][:-1]
             + [("prepare", 0, 0)] + ffn_down[0][-1:] + qkv[0] + ffn_up[1], 0, 50),
            (scores[0], 51, 80), (ffn_down[1], 52, 60), (qkv[1], 61, 65), (shift[0], 81, 84),
            (scores[1], 80, 135), (units[0], 88, 135), (shift[1], 136, 139),
            (ends[0] + [("x2t", 0, 0)] + qkv[2], 136, 150), (units[1], 142, 190), (scores[2], 170, 220),
            (ends[1] + [("x2t", 1, 0)] + qkv[3], 191, 202), (shift[2], 221, 224),
            (scores[3], 220, 275), (units[2], 228, 275), ([("load_experts", 0, 0)], 275.5, 276),
            (shift[3], 277, 280),
            (ends[2], 276, 282), (units[3], 284, 350), (moe_in[0], 286, 300), (experts[0], 302, 375),
            (ends[3], 351, 357), (moe_in[1], 358, 372), ([("out", 0, 0)], 380, 381),
            (experts[1], 375.5, 400), ([("out", 1, 0)], 401, 402)):
        plan += spread(steps, begin, end)
    plan.sort(key=lambda x: x[0])
    return [step for _, step in plan]


def unit(i):
    return i // (2 * GROUP), i // GROUP % 2, i % GROUP


def place_jobs(order):
    places = {n: {} for n in ("misc", "s0", "s1", "t0", "t1", "pv")}

    def add(place, *name):
        places[place][name] = len(places[place])

    for step, a, i in order:
        if step == "setup":
            add("misc", "sums"), add("t1", "ternary")
        if step == "turn_weights":
            add("misc", "wi"), add("t0", "turned")
        if step == "prepare":
            add("misc", "small"), add("s0", "image_v")
        if step == "ffn_in":
            add("misc", "rt", a)
        if step == "ffn_up":
            add(f"t{i % 2}", "up", a, i)
        if step == "ffn_down":
            add(f"s{i % 2}", "r2t", a, i)
            if i == 0:
                add("pv", "down", a)
        if step in ("x1t", "q", "k", "v", "max_rows", "image_rows", "o_rows", "x2t",
                    "sum", "x3t", "router", "combine", "bias2"):
            add("misc", step, a)
        if step == "scores":
            add(f"s{i % 2}", "scores", a, i)
        if step == "max" and a < 2:
            add("misc", "image", a)
        if step == "attend":
            add(f"t{i % 2}", "weights", a, i)
        if step == "values" and i % NT == 0:
            add("pv", "values", a, i // NT)
        if step == "turn_back":
            add("misc", "turn_back", a, i)
        if step == "expert":
            if i < EXPERTS:
                add("s0", "hidden", a, i), add("s1", "hidden", a, i)
            if i > 0:
                add("misc", "y", a, i - 1)
    return places


def blocks_of(a, u):
    out, col = [], 0
    for kb in (2 * u, 2 * u + 1):
        w = S - kb * P if a < 2 else S
        out.append((kb, col, w))
        col += w
    return out


def two_layers(nc, A, out):
    fp32 = mybir.dt.float32
    bf16 = mybir.dt.bfloat16
    ALU = mybir.AluOpType
    ACT = mybir.ActivationFunctionType
    AX = mybir.AxisListType.X

    ORDER = program_order()
    JOB = place_jobs(ORDER)

    def drows(ap, n, count):
        return bass.AP(tensor=ap.tensor, offset=ap.offset, ap=[[0, n], [1, count]])

    ctx = ExitStack()
    with ctx:
        def sb(name, shape, dt=fp32):
            return ctx.enter_context(nc.sbuf_tensor(name, shape, dt))

        def pb(name, shape):
            return ctx.enter_context(nc.psum_tensor(name, shape, fp32))

        def sem(name):
            return ctx.enter_context(nc.semaphore(name))

        parts_dram = [[nc.dram_tensor(f"parts_{n}{a}", (PARTS, P, S), bf16, kind="Internal").ap()
                       for n in "qk"] for a in range(INST)]
        shift_dram = [nc.dram_tensor(f"shift_{a}", (2 * HEADS, S), bf16, kind="Internal").ap()
                      for a in range(INST)]

        ident = sb("ident", [P, P])
        identb = sb("identb", [P, P], bf16)
        causal_q = sb("causal_q", [P, P], bf16)
        causal_k = sb("causal_k", [P, P], bf16)
        ones = sb("ones", [P, P])
        head_grid = sb("head_grid", [P, HD, HEADS])
        head_of = sb("head_of", [P, HEADS])
        pick = sb("pick", [2 * HEADS, HEADS], bf16)
        prior = sb("prior", [P, NT, NG])
        magic = sb("magic", [P, 1])
        halves = sb("halves", [P, NT])
        zrow = sb("zrow", [2, S], bf16)
        orow = sb("orow", [PARTS, S], bf16)

        X = sb("X", [P, TILES, D])
        Wca = sb("Wca", [P, 3 * D])
        Wcaq = sb("Wcaq", [P, 2, D])
        Wcp = sb("Wcp", [P, D])
        WinT = sb("WinT", [P, 3, D])
        WsqT = sb("WsqT", [P, 3, D])
        rows5 = sb("rows5", [5, D])
        rows5p = sb("rows5p", [5, D])
        rows17 = sb("rows17", [17, D])
        cols5 = sb("cols5", [P, 5])
        cols17 = sb("cols17", [P, 17])
        condr = sb("condr", [B, D])
        condT = sb("condT", [P, B])
        brow = sb("brow", [1, 5, D])
        Wr = sb("Wr", [P, NG + EXPERTS])
        rrow = sb("rrow", [1, NG + EXPERTS])
        B2 = sb("B2", [EXPERTS, D])
        norm_gb = sb("norm_gb", [P, 4, D])

        shared = sb("shared", [P, 7936])
        taken = {"first": 0, "later": 0}

        def part(when, shape, dt=fp32):
            n = 1
            for x in shape:
                n *= x
            words = n if dt == fp32 else n // 2
            ap = shared[:, taken[when]:taken[when] + words]
            taken[when] += words
            if dt != fp32:
                ap = ap.bitcast(dt)
            if len(shape) == 2:
                return ap.rearrange("p (a b) -> p a b", a=shape[0])
            if len(shape) == 3:
                return ap.rearrange("p (a b c) -> p a b c", a=shape[0], b=shape[1])
            return ap

        W3 = part("first", [3, INNER])
        xtmp = part("first", [TILES, D])
        R1 = part("first", [TILES, D], bf16)
        RT = part("first", [B, S], bf16)
        Wt = part("first", [3, INNER], bf16)
        WtT = part("first", [3 * NC, P], bf16)
        Win = part("first", [3, D])
        Wsq = part("first", [3, D])
        cond_all = part("first", [B, D])
        R2 = part("first", [2, INNER], bf16)
        mrow = part("first", [S])[0:B, :]
        mres = part("first", [S])[0:B, :]
        mparts = xtmp.rearrange("p t d -> p (t d)").bitcast(bf16)[0:B, 0:PARTS * S]\
            .rearrange("p (n s) -> p n s", n=PARTS)
        hid = part("later", [2, FH, S])
        acc = part("later", [B, NT, D])
        X3 = part("later", [NT, D])
        OT = part("later", [INST, S])
        On = part("later", [NT, HEADS, HD])
        Ou = part("later", [2, S])

        wdot = sb("wdot", [P, 6, TILES])
        absum = sb("absum", [P, 3])
        wmean = sb("wmean", [P, 3])
        wscale = sb("wscale", [P, 3])
        q1 = sb("q1", [P, 5, TILES])
        q2 = sb("q2", [P, 4, TILES])
        R2T = sb("R2T", [P, 2, INNER], bf16)
        X1 = sb("X1", [P, TILES, D])

        XT = sb("XT", [P, 2, S])
        Qf = sb("Qf", [P, 2, S])
        Kf = sb("Kf", [P, S])
        X3T = Qf
        qres = sb("qres", [P, S])
        kres = sb("kres", [P, S])
        Qp = sb("Qp", [P, PARTS, S], bf16)
        Kp = sb("Kp", [P, PARTS, S], bf16)
        Qs = sb("Qs", [P, 2, HEADS, S], bf16)
        Ks = sb("Ks", [P, 2, HEADS, S], bf16)
        wexp = Ks[:, 0, :, :].rearrange("p h s -> p (h s)").bitcast(fp32)
        W1 = wexp[:, 0:EXPERTS * F].rearrange("p (e f) -> p e f", e=EXPERTS)
        W2 = wexp[:, EXPERTS * F:].rearrange("p (e h d) -> p e h d", e=EXPERTS, h=FH)
        Vs = sb("Vs", [P, 2, NT, HEADS, HC])
        kimg = sb("kimg", [P, B])
        Kimg = sb("Kimg", [P, B, HEADS])
        Vimg = sb("Vimg", [HEADS, B, HEADS, HC])
        mx = sb("mx", [P, 2, NT, HEADS])
        nm = sb("nm", [P, 2, NT, 2, HEADS], bf16)
        nmT = sb("nmT", [2 * HEADS, 2, S], bf16)
        Pimg = sb("Pimg", [HEADS, 2, S])
        probs = sb("probs", [P, 2, GROUP, 2 * S])
        rden = sb("rden", [P, NT, GROUP])

        stats = sb("stats", [P, NT, 6])
        mv = sb("mv", [P, NT, 2])
        ve = sb("ve", [P, NT])
        rstd = sb("rstd", [P, NT])
        lg = sb("lg", [P, NT, NG + EXPERTS])
        dl = sb("dl", [P, NT, NG + EXPERTS])
        ex = sb("ex", [P, NT, NG + EXPERTS])
        rs = sb("rs", [P, 3, NT])
        rg = sb("rg", [P, 4, NT, NG])
        comb = sb("comb", [P, B, NT, NG, 2])
        combT = X[:, :, :].rearrange("p t d -> p (t d)")[0:EXPERTS, 0:S]

        early = probs[:, :, :, :].rearrange("p n j s -> p (n j s)")

        def H(b, t):
            return early[:, (b * NT + t) * INNER:(b * NT + t + 1) * INNER]

        def SG(t):
            return early[:, (TILES + t % 2) * INNER:(TILES + t % 2 + 1) * INNER]

        def Y(t):
            return early[:, (TILES + 2 + t % 2) * INNER:(TILES + 3 + t % 2) * INNER]

        wtmp = early[:, (TILES + 4) * INNER:(TILES + 7) * INNER].rearrange("p (n d) -> p n d", n=3)

        place = {"misc": pb("ps_misc", [P, S]), "pv": pb("ps_pv", [P, S]),
                 "s0": pb("ps_s0", [P, S]), "s1": pb("ps_s1", [P, S]),
                 "t0": pb("ps_t0", [P, 2 * S]), "t1": pb("ps_t1", [P, 2 * S])}
        full = {n: sem(f"{n}_full") for n in place}
        free = {n: sem(f"{n}_free") for n in place}

        def filled(n, *name):
            return JOB[n][name] + 1

        in_experts = sem("in_experts")
        in_x, in_w3, in_att, in_mask, in_moe = (sem(n) for n in
                                                ("in_x", "in_w3", "in_att", "in_mask", "in_moe"))
        pool_const = sem("pool_const")
        dve_step = sem("dve_step")
        pool_step = sem("pool_step")
        w_exp_in, w_exp = sem("w_exp_in"), sem("w_exp")
        r1_ready = sem("r1_ready")
        ternary_ready = sem("ternary_ready")
        setup_pe = sem("setup_pe")
        perm_ready, wcaq_ready = sem("perm_ready"), sem("wcaq_ready")
        sums_ready = sem("sums_ready")
        scale_ready = sem("scale_ready")
        silu_ready = sem("silu_ready")
        q2_ready = sem("q2_ready")
        y_ready = sem("y_ready")
        r2_ready = sem("r2_ready")
        qf_ready, kf_ready = sem("qf_ready"), sem("kf_ready")
        qhi_ready, khi_ready = sem("qhi_ready"), sem("khi_ready")
        qp_ready, kp_ready = sem("qp_ready"), sem("kp_ready")
        parts_q = [sem(f"parts_q{a}") for a in range(INST)]
        parts_k = [sem(f"parts_k{a}") for a in range(INST)]
        stacked = [sem(f"stacked{a}") for a in range(INST)]
        mparts_ready, bias_ready = sem("mparts_ready"), sem("bias_ready")
        half_done = sem("half_done")
        fixed_rows = sem("fixed_rows")
        stack_init = sem("stack_init")
        nm_ready = sem("nm_ready")
        shift_out = [sem(f"shift_out{a}") for a in range(INST)]
        shifted = [sem(f"shifted{a}") for a in range(INST)]
        ve_ready, rstd_ready = sem("ve_ready"), sem("rstd_ready")
        x3_ready, x3t_ready = sem("x3_ready"), sem("x3t_ready")
        dl_ready, ex_ready = sem("dl_ready"), sem("ex_ready")
        comb_ready, combT_ready = sem("comb_ready"), sem("combT_ready")
        hid_ready, y_read = sem("hid_ready"), sem("y_read")
        out_ready, stored = sem("out_ready"), sem("stored")

        block = ctx.enter_context(nc.Block())

        @block.sync
        def _(sp):
            for step, a, i in ORDER:
                b = a % 2
                if step == "setup":
                    sp.dma_start(cond_all[:, :, :].rearrange("p b d -> p (b d)"),
                                 drows(A["cond_1024"], P, B * D)).then_inc(in_x, 16)
                    xv = A["x"].rearrange("b (t p) d -> p (b t) d", p=P)
                    for b in range(B):
                        sp.dma_start(X[:, b * NT:(b + 1) * NT, :],
                                     xv[:, b * NT:(b + 1) * NT, :]).then_inc(in_x, 16)
                    for n, w in enumerate(("L0_ffn_w_gate", "L0_ffn_w_up")):
                        sp.dma_start(W3[:, n, :].rearrange("p (a d) -> p a d", d=D),
                                     A[w].rearrange("(a p) d -> p a d", p=P)).then_inc(in_w3, 16)
                    sp.dma_start(W3[:, 2, :], A["L0_ffn_w_down"]).then_inc(in_w3, 16)
                    sp.dma_start(mrow[:, :], A["mask_Bx1x1xS_ff0"].rearrange("b x y s -> (b x y) s"))\
                      .then_inc(in_mask, 16)
                    for dst, src in (
                            (rows5[0:2, :], A["L1_cond_c_attn_b"][0:2 * D].rearrange("(r d) -> r d", d=D)),
                            (rows5[2:4, :], A["L1_ffn_in_proj_b"][0:2 * D].rearrange("(r d) -> r d", d=D)),
                            (rows5[4:5, :], A["L1_cond_uk_b"].rearrange("(r d) -> r d", r=1)),
                            (rows17[0:16, :], A["L1_ffn_b1"].rearrange("e (h p) -> (e h) p", p=P)),
                            (rows17[16:17, :], A["L1_cond_c_proj_b"].rearrange("(r d) -> r d", r=1)),
                            (condr[:, :], A["cond_1024"]),
                            (Wca[:, :], A["L1_cond_c_attn_w"]),
                            (Wcp[:, :], A["L1_cond_c_proj_w"]),
                            (Win[:, :, :], A["L1_ffn_in_proj_w"].rearrange("(a p) d -> p a d", p=P)),
                            (Wsq[:, 0, :], A["L1_ffn_out_proj_w"]),
                            (Wsq[:, 1, :], A["L1_cond_uk_w"]),
                            (Wsq[:, 2, :], A["L1_cond_uv_w"]),
                            (brow[:, 0, :], A["L1_cond_c_attn_b"][2 * D:3 * D].rearrange("(r d) -> r d", r=1)),
                            (brow[:, 1, :], A["L1_ffn_in_proj_b"][2 * D:3 * D].rearrange("(r d) -> r d", r=1)),
                            (brow[:, 2, :], A["L1_cond_uv_b"].rearrange("(r d) -> r d", r=1)),
                            (brow[:, 3, :], A["L1_cond_c_proj_b"].rearrange("(r d) -> r d", r=1)),
                            (brow[:, 4, :], A["L1_ffn_out_proj_b"].rearrange("(r d) -> r d", r=1))):
                        sp.dma_start(dst, src).then_inc(in_att, 16)
                if step == "prepare":
                    sp.wait_ge(pool_const, 1)
                    sp.wait_ge(mparts_ready, 1)
                    for b in range(B):
                        for n in range(PARTS):
                            src = mparts[b:b + 1, n, :].unsqueeze(1).to_broadcast([1, HEADS, S])
                            sp.dma_start(Ks[MASK + n:MASK + n + 1, b, :, :], src).then_inc(fixed_rows, 16)
                        sp.dma_start(Qs[SHIFT:SHIFT + 2, b, :, :],
                                     zrow[:, :].unsqueeze(1).to_broadcast([2, HEADS, S])).then_inc(fixed_rows, 16)
                        sp.dma_start(Ks[SHIFT:SHIFT + 2, b, :, :],
                                     orow[0:2, :].unsqueeze(1).to_broadcast([2, HEADS, S])).then_inc(fixed_rows, 16)
                        sp.dma_start(Qs[MASK:MASK + PARTS, b, :, :],
                                     orow[:, :].unsqueeze(1).to_broadcast([PARTS, HEADS, S])).then_inc(fixed_rows, 16)
                if step == "v":
                    sp.wait_ge(qp_ready, a + 1)
                    sp.dma_start(parts_dram[a][0].rearrange("n p s -> p n s"), Qp[:, :, :]).then_inc(parts_q[a], 16)
                    sp.wait_ge(kp_ready, a + 1)
                    sp.dma_start(parts_dram[a][1].rearrange("n p s -> p n s"), Kp[:, :, :]).then_inc(parts_k[a], 16)
                    row = HEADS * S
                    sp.wait_ge(parts_q[a], 16)
                    for n in range(PARTS):
                        for m in range(PARTS):
                            r = (n * PARTS + m) * HD
                            sp.dma_start(Qs[r:r + HD, b, :, :].rearrange("p h s -> p (h s)"),
                                         parts_dram[a][0][n].rearrange("(d h) s -> d (h s)", h=HEADS))\
                              .then_inc(stacked[a], 16)
                    sp.wait_ge(parts_k[a], 16)
                    for n in range(PARTS):
                        r = n * PARTS * HD
                        sp.dma_start(Ks[r:r + PARTS * HD, b, :, :].rearrange("p h s -> p (h s)"),
                                     parts_dram[a][1].rearrange("m (d h) s -> (m d) (h s)", h=HEADS))\
                          .then_inc(stacked[a], 16)
                if step == "max_rows":
                    sp.wait_ge(free["misc"], filled("misc", "max_rows", a))
                    sp.dma_start(shift_dram[a], nmT[:, b, :]).then_inc(shift_out[a], 16)
                    sp.wait_ge(shift_out[a], 16)
                    sp.dma_start(Qs[SHIFT:SHIFT + 2, b, :, :].rearrange("p h s -> p (h s)"),
                                 shift_dram[a].rearrange("(n h) s -> n (h s)", h=HEADS)).then_inc(shifted[a], 16)
                if step == "load_experts":
                    sp.wait_ge(full["t1"], filled("t1", "weights", 2, UNITS - 1))
                    sp.dma_start(W1[:, :, :], A["L1_ffn_w1"].rearrange("e d f -> d e f")).then_inc(in_experts, 16)
                    sp.dma_start(W2[:, :, :, :], A["L1_ffn_w2"].rearrange("e (h p) d -> p e h d", p=P))\
                      .then_inc(in_experts, 16)
                if step == "out":
                    sp.wait_ge(out_ready, a + 1)
                    sp.dma_start(out[a].rearrange("(t p) d -> p t d", p=P), acc[:, a, :, :]).then_inc(stored, 16)
            sp.wait_ge(stored, 16 * B)

        @block.gpsimd
        def _(pool):
            done = [0]
            norms = 0

            def then_wait(ins):
                done[0] += 1
                ins.then_inc(pool_step, 1)
                pool.wait_ge(pool_step, done[0])

            for step, a, i in ORDER:
                b = a % 2
                if step == "setup":
                    pool.memset(ident[:, :], 0.0)
                    pool.memset(identb[:, :], 0.0)
                    pool.memset(causal_q[:, :], 0.0)
                    pool.memset(causal_k[:, :], 0.0)
                    pool.memset(head_grid[:, :, :], 0.0)
                    then_wait(pool.memset(pick[:, :], 0.0))
                    pool.affine_select(out=ident[:, :], in_=ident[:, :], compare_op=ALU.not_equal, fill=1.0,
                                       base=0, pattern=[[-1, P]], channel_multiplier=1)
                    pool.affine_select(out=identb[:, :], in_=identb[:, :], compare_op=ALU.not_equal, fill=1.0,
                                       base=0, pattern=[[-1, P]], channel_multiplier=1)
                    pool.affine_select(out=causal_q[:, :], in_=causal_q[:, :], compare_op=ALU.is_ge, fill=BIG,
                                       base=0, pattern=[[-1, P]], channel_multiplier=1)
                    pool.affine_select(out=causal_k[:, :], in_=causal_k[:, :], compare_op=ALU.is_ge, fill=BIG,
                                       base=0, pattern=[[1, P]], channel_multiplier=-1)
                    pool.affine_select(out=head_grid[:, :, :], in_=head_grid[:, :, :],
                                       compare_op=ALU.not_equal, fill=1.0,
                                       base=0, pattern=[[-HEADS, HD], [-1, HEADS]], channel_multiplier=1)
                    then_wait(pool.affine_select(out=pick[:, :], in_=pick[:, :], compare_op=ALU.not_equal, fill=1.0,
                                                 base=0, pattern=[[-1, HEADS]], channel_multiplier=1))
                    pool.affine_select(out=pick[:, :], in_=pick[:, :], compare_op=ALU.not_equal, fill=1.0,
                                       base=-HEADS, pattern=[[-1, HEADS]], channel_multiplier=1)
                    pool.memset(ones[:, :], 1.0)
                    pool.memset(magic[:, :], MAGIC)
                    pool.memset(halves[:, :], -0.5)
                    for g in range(NG):
                        pool.memset(prior[:, :, g:g + 1], float(NG - g))
                    pool.memset(orow[:, :], 1.0)
                    pool.memset(zrow[:, :], 0.0).then_inc(pool_const, 1)
                    for n in range(2):
                        pool.memset(Vs[:, n, :, :, :], 0.0)
                    pool.memset(Vimg[:, :, :, :], 0.0).then_inc(pool_step, 1)
                    done[0] += 1
                    pool.wait_ge(pool_step, done[0])
                    for n in range(2):
                        pool.memset(Vs[:, n, :, :, HD:HD + 1], 1.0).then_inc(stack_init, 1)
                    for dst, src in (
                            (Wr[:, 0:NG], A["L1_ffn_w_group"]),
                            (Wr[:, NG:].rearrange("p (g e) -> p g e", e=2),
                             A["L1_ffn_w_expert"].rearrange("g d e -> d g e")),
                            (rrow[:, 0:NG], A["L1_ffn_b_group"].rearrange("(r n) -> r n", r=1)),
                            (rrow[:, NG:], A["L1_ffn_b_expert"].rearrange("(r g) e -> r (g e)", r=1)),
                            (B2[:, :], A["L1_ffn_b2"]),
                            (norm_gb[:, 0, :], drows(A["L1_ffn_ln1_g"], P, D)),
                            (norm_gb[:, 1, :], drows(A["L1_ffn_ln1_b"], P, D)),
                            (norm_gb[:, 2, :], drows(A["L1_ffn_ln2_g"], P, D)),
                            (norm_gb[:, 3, :], drows(A["L1_ffn_ln2_b"], P, D))):
                        pool.dma_start(dst, src).then_inc(in_moe, 16)
                if step == "turn_weights":
                    pool.wait_ge(r1_ready, 1)
                    pool.wait_ge(in_mask, 16)
                    then_wait(pool.tensor_scalar(mparts[:, 0, :], mrow[:, :], 1.0, None, ALU.mult))
                    then_wait(pool.tensor_tensor(mres[:, :], mrow[:, :], mparts[:, 0, :], ALU.subtract))
                    then_wait(pool.tensor_scalar(mparts[:, 1, :], mres[:, :], 1.0, None, ALU.mult))
                    pool.tensor_tensor(mparts[:, 2, :], mres[:, :], mparts[:, 1, :], ALU.subtract)\
                        .then_inc(mparts_ready, 1)
                    pool.wait_ge(in_att, 16 * 17)
                    pool.tensor_tensor(brow[:, 3, :], brow[:, 3, :], brow[:, 4, :], ALU.add)\
                        .then_inc(bias_ready, 1)
                if step == "k":
                    pool.wait_ge(khi_ready, a + 1)
                    then_wait(pool.tensor_tensor(kres[:, :], Kf[:, :], Kp[:, 0, :], ALU.subtract))
                    then_wait(pool.tensor_scalar(Kp[:, 1, :], kres[:, :], 1.0, None, ALU.mult))
                    pool.tensor_tensor(Kp[:, 2, :], kres[:, :], Kp[:, 1, :], ALU.subtract).then_inc(kp_ready, 1)
                if step in ("sum", "out"):
                    norms += 1
                    pool.wait_ge(ve_ready, norms)
                    pool.tensor_tensor(rstd[:, :], ve[:, :], halves[:, :], ALU.pow).then_inc(rstd_ready, 1)

        @block.scalar
        def _(act):
            def take(n, *name):
                act.wait_ge(full[n], filled(n, *name))
                return place[n]

            for step, a, i in ORDER:
                b = a % 2
                if step == "setup":
                    act.wait_ge(w_exp_in, 1)
                    act.activation(wdot[:, 3, :], wdot[:, 1, :], ACT.Exp).then_inc(w_exp, 1)
                    ps = take("t1", "ternary")
                    act.activation(WtT[:, 0:8, :].rearrange("p a d -> p (a d)"),
                                   ps[:, 0:S].bitcast(bf16), ACT.Copy)
                    act.activation(WtT[:, 8:12, :].rearrange("p a d -> p (a d)"),
                                   ps[:, S:S + S // 2].bitcast(bf16), ACT.Copy).then_inc(free["t1"], 1)
                if step == "turn_weights":
                    ps = take("misc", "wi")
                    for n in range(3):
                        src = ps[:, n * D:(n + 1) * D]
                        if n < 2:
                            act.activation(WinT[:, n, :].rearrange("p (d h) -> p d h", h=HEADS),
                                           src.rearrange("p (h d) -> p d h", d=HD), ACT.Copy)
                        else:
                            act.activation(WinT[:, n, :], src, ACT.Copy).then_inc(free["misc"], 1)
                    ps = take("t0", "turned")
                    act.activation(WsqT[:, 0, :], ps[:, 0:D], ACT.Copy)
                    act.activation(WsqT[:, 1, :].rearrange("p (d h) -> p d h", h=HEADS),
                                   ps[:, D:2 * D].rearrange("p (h d) -> p d h", d=HD), ACT.Copy)
                    act.activation(WsqT[:, 2, :], ps[:, 2 * D:3 * D], ACT.Copy)
                    act.activation(condT[:, :], ps[:, 3 * D:3 * D + B], ACT.Copy).then_inc(free["t0"], 1)
                    act.wait_ge(in_att, 16 * 17)
                    for n in range(2):
                        last = act.activation(Wcaq[:, n, :].rearrange("p (d h) -> p d h", h=HEADS),
                                              Wca[:, n * D:(n + 1) * D].rearrange("p (h d) -> p d h", d=HD),
                                              ACT.Copy)
                    last.then_inc(wcaq_ready, 1)
                if step == "ffn_in":
                    ps = take("misc", "rt", a)
                    act.activation(RT[:, a, :], ps[:, 0:S // 2].bitcast(bf16), ACT.Copy).then_inc(free["misc"], 1)
                if step == "ffn_up":
                    t = a * NT + i
                    ps = take(f"t{i % 2}", "up", a, i)
                    act.wait_ge(scale_ready, 1)
                    act.activation(SG(i), ps[:, 0:INNER], ACT.Silu, scale=q1[:, 3, t:t + 1]).then_inc(silu_ready, 1)
                if step == "ffn_down":
                    t = a * NT + i
                    act.wait_ge(q2_ready, a + 1)
                    act.activation(Y(i), H(a, i), ACT.Identity, bias=magic[:, 0:1],
                                   scale=q2[:, 2, t:t + 1]).then_inc(y_ready, 1)
                    ps = take(f"s{i % 2}", "r2t", a, i)
                    act.activation(R2T[:, i % 2, :], ps[:, 0:INNER // 2].bitcast(bf16), ACT.Copy)\
                       .then_inc(free[f"s{i % 2}"], 1)
                if step == "x1t":
                    ps = take("misc", "x1t", a)
                    act.activation(XT[:, a, :], ps[:, :], ACT.Copy).then_inc(free["misc"], 1)
                if step == "q":
                    layer = a // 2
                    if a >= 1:
                        act.wait_ge(parts_q[a - 1], 16)
                        act.wait_ge(parts_k[a - 1], 16)
                    act.wait_ge(perm_ready, 1)
                    ps = take("misc", "q", a)
                    act.activation(Qf[:, b, :], ps[:, :], ACT.Identity, bias=cols5[:, 2 * layer:2 * layer + 1],
                                   scale=float(HD) ** -0.5).then_inc(free["misc"], 1)
                    act.wait_ge(free["misc"], filled("misc", "q", a))
                    act.activation(Qp[:, 0, :], Qf[:, b, :], ACT.Copy).then_inc(qhi_ready, 1)
                if step == "k":
                    layer = a // 2
                    ps = take("misc", "k", a)
                    act.activation(Kf[:, :], ps[:, :], ACT.Identity,
                                   bias=cols5[:, 2 * layer + 1:2 * layer + 2]).then_inc(free["misc"], 1)
                    act.wait_ge(free["misc"], filled("misc", "k", a))
                    act.activation(Kp[:, 0, :], Kf[:, :], ACT.Copy).then_inc(khi_ready, 1)
                if step == "max_rows":
                    ps = take("misc", "max_rows", a)
                    act.activation(nmT[:, b, :], ps[0:2 * HEADS, 0:S // 2].bitcast(bf16), ACT.Copy)\
                       .then_inc(free["misc"], 1)
                if step == "image_rows":
                    ps = take("misc", "image_rows", a)
                    act.activation(Pimg[:, b, :], ps[0:HEADS, :], ACT.Exp).then_inc(free["misc"], 1)
                if step == "attend":
                    r, u, j = unit(i)
                    half = 2 * (a * ROUNDS + r) + u
                    if j == 0 and half >= 2:
                        if u == 0:
                            act.wait_ge(half_done, half // 2)
                        else:
                            n = half // 2 - 1
                            act.wait_ge(full["pv"], filled("pv", "values", n // ROUNDS, n % ROUNDS))
                    ps = take(f"t{i % 2}", "weights", a, i)
                    w = sum(x[2] for x in blocks_of(a, u))
                    act.activation(probs[:, half % 2, j, 0:w], ps[:, 0:w], ACT.Exp).then_inc(free[f"t{i % 2}"], 1)
                if step == "o_rows":
                    ps = take("misc", "o_rows", a)
                    act.activation(OT[:, a, :], ps[:, :], ACT.Copy).then_inc(free["misc"], 1)
                if step == "x2t":
                    ps = take("misc", "x2t", a)
                    act.activation(XT[:, a, :], ps[:, :], ACT.Identity, bias=cols17[:, 16:17])\
                       .then_inc(free["misc"], 1)
                if step == "x3t":
                    ps = take("misc", "x3t", a)
                    act.activation(X3T[:, a, :], ps[:, :], ACT.Copy).then_inc(free["misc"], 1)
                if step == "route":
                    act.wait_ge(dl_ready, a + 1)
                    act.activation(ex[:, :, :], dl[:, :, :], ACT.Exp).then_inc(ex_ready, 1)

        @block.vector
        def _(dve):
            done = [0]

            def then_wait(ins):
                done[0] += 1
                ins.then_inc(dve_step, 1)
                dve.wait_ge(dve_step, done[0])

            def take(n, *name):
                dve.wait_ge(full[n], filled(n, *name))
                return place[n]

            norms = [0]

            def norm_stats(src):
                for t in range(NT):
                    last = dve.bn_stats(stats[:, t, :], src[:, t, :])
                then_wait(last)
                for t in range(NT):
                    last = dve.bn_aggr(mv[:, t, :], stats[:, t, :])
                then_wait(last)
                norms[0] += 1
                dve.tensor_scalar(ve[:, :], mv[:, :, 1], EPS, None, ALU.add).then_inc(ve_ready, 1)

            def norm(src, dst):
                dve.wait_ge(rstd_ready, norms[0])
                for t in range(NT):
                    last = dve.tensor_scalar(dst[:, t, :], src[:, t, :], mv[:, t, 0:1], rstd[:, t:t + 1],
                                             ALU.subtract, ALU.mult)
                return last

            def gain(dst, g):
                gb = norm_gb[:, g:g + 1, :].to_broadcast([P, NT, D])
                bb = norm_gb[:, g + 1:g + 2, :].to_broadcast([P, NT, D])
                then_wait(dve.tensor_tensor(dst, dst, gb, ALU.mult))
                return dve.tensor_tensor(dst, dst, bb, ALU.add)

            for step, a, i in ORDER:
                b = a % 2
                if step == "setup":
                    dve.wait_ge(in_x, 16 * 3)
                    for n in range(B):
                        last = dve.tensor_tensor(
                            xtmp[:, n * NT:(n + 1) * NT, :], X[:, n * NT:(n + 1) * NT, :],
                            cond_all[:, n:n + 1, :].to_broadcast([P, NT, D]), ALU.mult)
                    then_wait(last)
                    then_wait(dve.tensor_reduce(wdot[:, 0, :], xtmp[:, :, :], AX, ALU.add))
                    then_wait(dve.tensor_scalar(wdot[:, 0, :], wdot[:, 0, :], float(D) ** -0.5, None, ALU.mult))
                    then_wait(dve.tensor_tensor(wdot[:, 5, 0:NT], wdot[:, 0, 0:NT], wdot[:, 0, NT:], ALU.max))
                    for n in range(B):
                        last = dve.tensor_tensor(wdot[:, 1, n * NT:(n + 1) * NT], wdot[:, 0, n * NT:(n + 1) * NT],
                                                 wdot[:, 5, 0:NT], ALU.subtract)
                    last.then_inc(w_exp_in, 1)
                    dve.wait_ge(in_w3, 16 * 3)
                    dve.tensor_reduce(absum[:, :], W3[:, :, :], AX, ALU.add, apply_absolute_value=True)\
                       .then_inc(sums_ready, 1)
                    dve.wait_ge(w_exp, 1)
                    then_wait(dve.tensor_tensor(wdot[:, 5, 0:NT], wdot[:, 3, 0:NT], wdot[:, 3, NT:], ALU.add))
                    then_wait(dve.reciprocal(wdot[:, 5, NT:], wdot[:, 5, 0:NT]))
                    for n in range(B):
                        last = dve.tensor_tensor(wdot[:, 0, n * NT:(n + 1) * NT], wdot[:, 3, n * NT:(n + 1) * NT],
                                                 wdot[:, 5, NT:], ALU.mult)
                    then_wait(last)
                    then_wait(dve.tensor_tensor(xtmp[:, :, :], X[:, :, :],
                                                wdot[:, 0, :].unsqueeze(2).to_broadcast([P, TILES, D]), ALU.mult))
                    then_wait(dve.tensor_reduce(q1[:, 0, :], xtmp[:, :, :], AX, ALU.max, apply_absolute_value=True))
                    then_wait(dve.tensor_scalar(q1[:, 0, :], q1[:, 0, :], 1e-5, None, ALU.max))
                    then_wait(dve.reciprocal(q1[:, 1, :], q1[:, 0, :]))
                    then_wait(dve.tensor_scalar(q1[:, 1, :], q1[:, 1, :], 127.0, None, ALU.mult))
                    then_wait(dve.tensor_tensor(xtmp[:, :, :], xtmp[:, :, :],
                                                q1[:, 1, :].unsqueeze(2).to_broadcast([P, TILES, D]), ALU.mult))
                    dve.tensor_scalar(R1[:, :, :], xtmp[:, :, :], MAGIC, MAGIC, ALU.add, ALU.subtract).then_inc(r1_ready, 1)
                    ps = take("misc", "sums")
                    then_wait(dve.tensor_scalar(wmean[:, :], ps[:, 0:3], 1.0 / (INNER * D), 1e-5, ALU.mult, ALU.max))
                    dve.reciprocal(wscale[:, :], wmean[:, :]).then_inc(free["misc"], 1)
                    dve.wait_ge(free["misc"], filled("misc", "sums"))
                    for n in range(3):
                        last = dve.tensor_scalar(wtmp[:, n, :], W3[:, n, :], wscale[:, n:n + 1], MAGIC,
                                                 ALU.mult, ALU.add)
                    then_wait(last)
                    then_wait(dve.tensor_scalar(wtmp[:, :, :], wtmp[:, :, :], MAGIC, 1.0, ALU.subtract, ALU.min))
                    dve.tensor_scalar(Wt[:, :, :], wtmp[:, :, :], -1.0, None, ALU.max).then_inc(ternary_ready, 1)
                    then_wait(dve.tensor_scalar(q1[:, 2, :], q1[:, 0, :], 1.0 / 127.0, None, ALU.mult))
                    dve.tensor_scalar(q1[:, 4, :], q1[:, 2, :], wmean[:, 1:2], None, ALU.mult)
                    dve.tensor_scalar(q1[:, 3, :], q1[:, 2, :], wmean[:, 0:1], None, ALU.mult).then_inc(scale_ready, 1)
                if step == "prepare":
                    dve.wait_ge(in_att, 16 * 17)
                    dve.tensor_copy(rows5p[:, :].rearrange("r (d h) -> r d h", h=HEADS),
                                    rows5[:, :].rearrange("r (h d) -> r d h", d=HD)).then_inc(setup_pe, 1)
                    dve.wait_ge(pool_const, 1)
                    dve.tensor_reduce(head_of[:, :], head_grid[:, :, :].rearrange("p d h -> p h d"), AX, ALU.add)
                    ps = take("misc", "small")
                    dve.tensor_copy(cols5[:, :], ps[:, 0:5])
                    then_wait(dve.tensor_copy(cols17[:, :], ps[:, 8:25]))
                    for n in range(2):
                        last = dve.tensor_scalar(cols5[:, 2 * n:2 * n + 1], cols5[:, 2 * n:2 * n + 1],
                                                 float(HD) ** -0.5, None, ALU.mult)
                    then_wait(last)
                    dve.tensor_scalar(kimg[:, :], ps[:, 32:32 + B], cols5[:, 4:5], None, ALU.add)\
                       .then_inc(free["misc"], 1)
                    dve.wait_ge(free["misc"], filled("misc", "small"))
                    for n in range(B):
                        last = dve.tensor_scalar(Kimg[:, n, :], head_of[:, :], kimg[:, n:n + 1], None, ALU.mult)
                    last.then_inc(perm_ready, 1)
                    dve.wait_ge(stack_init, 2)
                    ps = take("s0", "image_v")
                    own = ident[0:HEADS, 0:HEADS]
                    for n in range(B):
                        dve.tensor_tensor(Vimg[:, n, :, 0:HD],
                                          ps[0:HEADS, n * D:(n + 1) * D].rearrange("p (h d) -> p h d", d=HD),
                                          own.unsqueeze(2).to_broadcast([HEADS, HEADS, HD]), ALU.mult)
                        last = dve.tensor_copy(Vimg[:, n, :, HD:HD + 1], own.unsqueeze(2))
                    last.then_inc(free["s0"], 1)
                if step == "ffn_up":
                    t = a * NT + i
                    ps = take(f"t{i % 2}", "up", a, i)
                    dve.wait_ge(silu_ready, t + 1)
                    dve.tensor_tensor(H(a, i), SG(i), ps[:, INNER:2 * INNER], ALU.mult)\
                       .then_inc(free[f"t{i % 2}"], 1)
                    dve.wait_ge(free[f"t{i % 2}"], filled(f"t{i % 2}", "up", a, i))
                    last = dve.tensor_reduce(q2[:, 0, t:t + 1], H(a, i), AX, ALU.max, apply_absolute_value=True)
                    if i == NT - 1:
                        then_wait(last)
                        r = slice(a * NT, (a + 1) * NT)
                        then_wait(dve.tensor_tensor(q2[:, 0, r], q2[:, 0, r], q1[:, 4, r], ALU.mult))
                        then_wait(dve.tensor_scalar(q2[:, 0, r], q2[:, 0, r], 1e-5, None, ALU.max))
                        then_wait(dve.reciprocal(q2[:, 1, r], q2[:, 0, r]))
                        dve.tensor_scalar(q2[:, 3, r], q2[:, 0, r], wmean[:, 2:3], 1.0 / 127.0, ALU.mult, ALU.mult)
                        then_wait(dve.tensor_scalar(q2[:, 1, r], q2[:, 1, r], 127.0, None, ALU.mult))
                        dve.tensor_tensor(q2[:, 2, r], q2[:, 1, r], q1[:, 4, r], ALU.mult).then_inc(q2_ready, 1)
                if step == "ffn_down":
                    t = a * NT + i
                    dve.wait_ge(y_ready, t + 1)
                    dve.tensor_scalar(R2[:, t % 2, :], Y(i), MAGIC, None, ALU.subtract).then_inc(r2_ready, 1)
                if step == "x1t":
                    ps = take("pv", "down", a)
                    dve.wait_ge(q2_ready, a + 1)
                    for t in range(NT):
                        n = a * NT + t
                        last = dve.scalar_tensor_tensor(out=X1[:, n, :], in0=ps[:, t * D:(t + 1) * D],
                                                        scalar=q2[:, 3, n:n + 1], in1=X[:, n, :],
                                                        op0=ALU.mult, op1=ALU.add)
                    last.then_inc(free["pv"], 1)
                if step == "q":
                    dve.wait_ge(qhi_ready, a + 1)
                    then_wait(dve.tensor_tensor(qres[:, :], Qf[:, b, :], Qp[:, 0, :], ALU.subtract))
                    then_wait(dve.tensor_copy(Qp[:, 1, :], qres[:, :]))
                    dve.tensor_tensor(Qp[:, 2, :], qres[:, :], Qp[:, 1, :], ALU.subtract).then_inc(qp_ready, 1)
                if step == "v":
                    if a < 2:
                        dve.wait_ge(stack_init, 2)
                    ps = take("misc", "v", a)
                    dve.tensor_copy(Vs[:, b, :, :, 0:HD].rearrange("p t h d -> p (t h) d"),
                                    ps[:, :].rearrange("p (n d) -> p n d", d=HD)).then_inc(free["misc"], 1)
                if step == "scores":
                    h, t = i // NT, i % NT
                    ps = take(f"s{i % 2}", "scores", a, i)
                    w = (t + 1) * P if a < 2 else S
                    dve.tensor_reduce(mx[:, b, t, h:h + 1], ps[:, 0:w], AX, ALU.max).then_inc(free[f"s{i % 2}"], 1)
                if step == "max":
                    for n in range(2):
                        dve.wait_ge(free[f"s{n}"], filled(f"s{n}", "scores", a, HEADS * NT - 2 + n))
                    m = mx[:, b, :, :]
                    if a < 2:
                        ps = take("misc", "image", a)
                        dve.tensor_tensor(m, ps[:, 0:NT * HEADS].rearrange("p (t h) -> p t h", h=HEADS), m, ALU.max)\
                           .then_inc(free["misc"], 1)
                        dve.wait_ge(free["misc"], filled("misc", "image", a))
                    then_wait(dve.tensor_scalar(nm[:, b, :, 0, :], m, -1.0, None, ALU.mult))
                    dve.scalar_tensor_tensor(out=nm[:, b, :, 1, :], in0=m, scalar=-1.0, in1=nm[:, b, :, 0, :],
                                             op0=ALU.mult, op1=ALU.subtract).then_inc(nm_ready, 1)
                if step == "values" and i % NT == NT - 1:
                    ps = take("pv", "values", a, i // NT)
                    dve.tensor_copy(Ou[:, i // NT % 2, :], ps[:, :]).then_inc(free["pv"], 1)
                if step == "turn_back":
                    ps = take("misc", "turn_back", a, i)
                    tb = ps[:, :].rearrange("p (t j c) -> p t j c", j=GROUP, c=HC)
                    then_wait(dve.reciprocal(rden[:, :, :], tb[:, :, :, HD]))
                    dve.tensor_tensor(On[:, :, i * GROUP:(i + 1) * GROUP, :], tb[:, :, :, 0:HD],
                                      rden[:, :, :].unsqueeze(3).to_broadcast([P, NT, GROUP, HD]), ALU.mult)\
                       .then_inc(free["misc"], 1)
                if step == "sum":
                    dve.wait_ge(in_moe, 16 * 9)
                    norm_stats(take("misc", "sum", a)[:, :].rearrange("p (t d) -> p t d", d=D))
                    norm(place["misc"][:, :].rearrange("p (t d) -> p t d", d=D), X3[:, :, :])\
                        .then_inc(free["misc"], 1)
                    dve.wait_ge(free["misc"], filled("misc", "sum", a))
                    gain(X3[:, :, :], 0).then_inc(x3_ready, 1)
                if step == "router":
                    ps = take("misc", "router", a)
                    dve.tensor_copy(lg[:, :, :], ps[:, 0:NT * (NG + EXPERTS)]
                                    .rearrange("p (t n) -> p t n", t=NT)).then_inc(free["misc"], 1)
                    dve.wait_ge(free["misc"], filled("misc", "router", a))
                    pair = lg[:, :, NG:].rearrange("p t (g e) -> p t g e", e=2)
                    dve.tensor_reduce(rs[:, 0, :], lg[:, :, 0:NG], AX, ALU.max)
                    then_wait(dve.tensor_tensor(rg[:, 0, :, :], pair[:, :, :, 0], pair[:, :, :, 1], ALU.max))
                    dve.tensor_tensor(dl[:, :, 0:NG], lg[:, :, 0:NG],
                                      rs[:, 0, :].unsqueeze(2).to_broadcast([P, NT, NG]), ALU.subtract)
                    then_wait(dve.tensor_tensor(dl[:, :, NG:].rearrange("p t (g e) -> p t g e", e=2), pair,
                                                rg[:, 0, :, :].unsqueeze(3).to_broadcast([P, NT, NG, 2]),
                                                ALU.subtract))
                    dve.scalar_tensor_tensor(out=rg[:, 1, :, :], in0=dl[:, :, 0:NG], scalar=0.0,
                                             in1=prior[:, :, :], op0=ALU.is_equal, op1=ALU.mult).then_inc(dl_ready, 1)
                if step == "route":
                    dve.wait_ge(dl_ready, a + 1)
                    then_wait(dve.tensor_reduce(rs[:, 1, :], rg[:, 1, :, :], AX, ALU.max))
                    dve.tensor_tensor(rg[:, 2, :, :], rg[:, 1, :, :],
                                      rs[:, 1, :].unsqueeze(2).to_broadcast([P, NT, NG]), ALU.is_equal)
                    dve.wait_ge(ex_ready, a + 1)
                    pex = ex[:, :, NG:].rearrange("p t (g e) -> p t g e", e=2)
                    dve.tensor_reduce(rs[:, 2, :], ex[:, :, 0:NG], AX, ALU.add)
                    then_wait(dve.tensor_tensor(rg[:, 3, :, :], pex[:, :, :, 0], pex[:, :, :, 1], ALU.add))
                    then_wait(dve.tensor_tensor(rg[:, 3, :, :], rg[:, 3, :, :],
                                                rs[:, 2, :].unsqueeze(2).to_broadcast([P, NT, NG]), ALU.mult))
                    then_wait(dve.reciprocal(rg[:, 0, :, :], rg[:, 3, :, :]))
                    then_wait(dve.tensor_tensor(rg[:, 0, :, :], rg[:, 0, :, :], rg[:, 2, :, :], ALU.mult))
                    dpair = dl[:, :, NG:].rearrange("p t (g e) -> p t g e", e=2)
                    then_wait(dve.scalar_tensor_tensor(out=comb[:, a, :, :, 0], in0=dpair[:, :, :, 0], scalar=0.0,
                                                       in1=rg[:, 0, :, :], op0=ALU.is_equal, op1=ALU.mult))
                    dve.tensor_tensor(comb[:, a, :, :, 1], rg[:, 0, :, :], comb[:, a, :, :, 0], ALU.subtract)\
                       .then_inc(comb_ready, 1)
                if step == "combine":
                    dve.wait_ge(comb_ready, a + 1)
                    ps = take("misc", "combine", a)
                    dve.tensor_copy(combT[:, :], ps[0:EXPERTS, :]).then_inc(free["misc"], 1)
                if step == "bias2":
                    ps = take("misc", "bias2", a)
                    dve.tensor_tensor(acc[:, a, :, :], ps[:, :].rearrange("p (t d) -> p t d", d=D),
                                      X3[:, :, :], ALU.add).then_inc(free["misc"], 1)
                if step == "expert":
                    if i < EXPERTS:
                        for h in range(FH):
                            ps = take(f"s{h}", "hidden", a, i)
                            dve.tensor_scalar(hid[:, i % 2, h, :], ps[:, :], cols17[:, 2 * i + h:2 * i + h + 1], 0.0,
                                              ALU.add, ALU.max).then_inc(free[f"s{h}"], 1)
                    if i > 0:
                        if i == 1:
                            dve.wait_ge(free["misc"], filled("misc", "bias2", a))
                        else:
                            dve.wait_ge(free["misc"], filled("misc", "y", a, i - 2))
                        e = i - 1
                        ps = take("misc", "y", a, e)
                        for t in range(NT):
                            last = dve.scalar_tensor_tensor(
                                out=acc[:, a, t, :], in0=ps[:, t * D:(t + 1) * D],
                                scalar=comb[:, a, t, e // 2, e % 2:e % 2 + 1], in1=acc[:, a, t, :],
                                op0=ALU.mult, op1=ALU.add)
                        last.then_inc(free["misc"], 1)
                if step == "out":
                    dve.wait_ge(free["misc"], filled("misc", "y", a, EXPERTS - 1))
                    norm_stats(acc[:, a, :, :])
                    then_wait(norm(acc[:, a, :, :], acc[:, a, :, :]))
                    then_wait(gain(acc[:, a, :, :], 2))
                    dve.tensor_tensor(acc[:, a, :, :], acc[:, a, :, :], X1[:, a * NT:(a + 1) * NT, :], ALU.add)\
                       .then_inc(out_ready, 1)

        @block.tensor
        def _(pe):
            def put(n, *name):
                if JOB[n][name] > 0:
                    pe.wait_ge(free[n], JOB[n][name])
                return place[n]

            for step, a, i in ORDER:
                b = a % 2
                if step == "setup":
                    pe.wait_ge(pool_const, 1)
                    pe.wait_ge(sums_ready, 1)
                    ps = put("misc", "sums")
                    pe.matmul(ps[:, 0:3], ones[:, :], absum[:, :], start=True, stop=True).then_inc(full["misc"], 1)
                    pe.wait_ge(ternary_ready, 1)
                    ps = put("t1", "ternary")
                    for n in range(8):
                        pe.transpose(ps[:, n * P // 2:(n + 1) * P // 2].bitcast(bf16),
                                     Wt[:, n // NC, (n % NC) * P:(n % NC + 1) * P], identb[:, :])
                    for n in range(NC):
                        mm = pe.transpose(ps[:, S + n * P // 2:S + (n + 1) * P // 2].bitcast(bf16),
                                          Wt[:, 2, n * P:(n + 1) * P], identb[:, :])
                    mm.then_inc(full["t1"], 1)
                if step == "turn_weights":
                    pe.wait_ge(in_att, 16 * 17)
                    ps = put("misc", "wi")
                    for n in range(3):
                        mm = pe.transpose(ps[:, n * D:(n + 1) * D], Win[:, n, :], ident[:, :])
                    mm.then_inc(full["misc"], 1)
                    ps = put("t0", "turned")
                    for n in range(3):
                        pe.transpose(ps[:, n * D:(n + 1) * D], Wsq[:, n, :], ident[:, :])
                    pe.transpose(ps[:, 3 * D:3 * D + B], condr[:, :], ident[0:B, 0:B]).then_inc(full["t0"], 1)
                if step == "prepare":
                    pe.wait_ge(setup_pe, 1)
                    ps = put("misc", "small")
                    pe.transpose(ps[:, 0:5], rows5p[:, :], ident[0:5, 0:5])
                    pe.transpose(ps[:, 8:25], rows17[:, :], ident[0:17, 0:17])
                    pe.wait_ge(free["t0"], filled("t0", "turned"))
                    pe.matmul(ps[:, 32:32 + B], WsqT[:, 1, :], condT[:, :], start=True, stop=True)\
                      .then_inc(full["misc"], 1)
                    ps = put("s0", "image_v")
                    for n in range(B):
                        pe.matmul(ps[0:HEADS, n * D:(n + 1) * D], condT[:, n:n + 1].to_broadcast([P, HEADS]),
                                  WsqT[:, 2, :], start=True, stop=False)
                        mm = pe.matmul(ps[0:HEADS, n * D:(n + 1) * D], ones[0:1, 0:HEADS], brow[:, 2, :],
                                       start=False, stop=True)
                    mm.then_inc(full["s0"], 1)
                if step == "ffn_in":
                    pe.wait_ge(r1_ready, 1)
                    ps = put("misc", "rt", a)
                    for t in range(NT):
                        mm = pe.transpose(ps[:, t * P // 2:(t + 1) * P // 2].bitcast(bf16),
                                          R1[:, a * NT + t, :], identb[:, :])
                    mm.then_inc(full["misc"], 1)
                if step == "ffn_up":
                    if i == 0:
                        pe.wait_ge(free["misc"], filled("misc", "rt", a))
                        pe.wait_ge(free["t1"], filled("t1", "ternary"))
                    ps = put(f"t{i % 2}", "up", a, i)
                    for n in range(2):
                        mm = pe.matmul(ps[:, n * INNER:(n + 1) * INNER], RT[:, a, i * P:(i + 1) * P],
                                       WtT[:, n * NC:(n + 1) * NC, :].rearrange("p a d -> p (a d)"),
                                       start=True, stop=True)
                    mm.then_inc(full[f"t{i % 2}"], 1)
                if step == "ffn_down":
                    t = a * NT + i
                    pe.wait_ge(r2_ready, t + 1)
                    ps = put(f"s{i % 2}", "r2t", a, i)
                    for c in range(NC):
                        mm = pe.transpose(ps[:, c * P // 2:(c + 1) * P // 2].bitcast(bf16),
                                          R2[:, t % 2, c * P:(c + 1) * P], identb[:, :])
                    mm.then_inc(full[f"s{i % 2}"], 1)
                    pe.wait_ge(free[f"s{i % 2}"], filled(f"s{i % 2}", "r2t", a, i))
                    if i == 0:
                        put("pv", "down", a)
                    for c in range(NC):
                        mm = pe.matmul(place["pv"][:, i * D:(i + 1) * D], R2T[:, i % 2, c * P:(c + 1) * P],
                                       WtT[:, 2 * NC + c, :], start=(c == 0), stop=(c == NC - 1))
                    if i == NT - 1:
                        mm.then_inc(full["pv"], 1)
                if step == "x1t":
                    pe.wait_ge(free["pv"], filled("pv", "down", a))
                    ps = put("misc", "x1t", a)
                    for t in range(NT):
                        mm = pe.transpose(ps[:, t * P:(t + 1) * P], X1[:, a * NT + t, :], ident[:, :])
                    mm.then_inc(full["misc"], 1)
                if step == "q":
                    if a < 2:
                        pe.wait_ge(perm_ready, 1)
                        pe.wait_ge(wcaq_ready, 1)
                        pe.wait_ge(free["misc"], filled("misc", "x1t", a))
                    else:
                        pe.wait_ge(free["misc"], filled("misc", "x2t", a - 2))
                    ps = put("misc", "q", a)
                    pe.matmul(ps[:, :], Wcaq[:, 0, :] if a < 2 else WinT[:, 0, :], XT[:, b, :],
                              start=True, stop=True).then_inc(full["misc"], 1)
                if step == "k":
                    ps = put("misc", "k", a)
                    pe.matmul(ps[:, :], Wcaq[:, 1, :] if a < 2 else WinT[:, 1, :], XT[:, b, :],
                              start=True, stop=True).then_inc(full["misc"], 1)
                if step == "v":
                    wv = Wca[:, 2 * D:3 * D] if a < 2 else WinT[:, 2, :]
                    ps = put("misc", "v", a)
                    for t in range(NT):
                        pe.matmul(ps[:, t * D:(t + 1) * D], XT[:, b, t * P:(t + 1) * P], wv, start=True, stop=False)
                        mm = pe.matmul(ps[:, t * D:(t + 1) * D], ones[0:1, :], brow[:, a // 2, :],
                                       start=False, stop=True)
                    mm.then_inc(full["misc"], 1)
                if step == "scores":
                    if i == 0:
                        pe.wait_ge(stacked[a], 16 * 12)
                        if a < 2:
                            pe.wait_ge(fixed_rows, 16 * 2 * (PARTS + 3))
                    rows = MASK + PARTS if a < 2 else STACK
                    h, t = i // NT, i % NT
                    ps = put(f"s{i % 2}", "scores", a, i)
                    w = (t + 1) * P if a < 2 else S
                    mm = pe.matmul(ps[:, 0:w], Qs[0:rows, b, h, t * P:(t + 1) * P], Ks[0:rows, b, h, 0:w],
                                   start=True, stop=(a >= 2))
                    if a < 2:
                        mm = pe.matmul(ps[:, w - P:w], identb[:, :], causal_q[:, :], start=False, stop=True)
                    mm.then_inc(full[f"s{i % 2}"], 1)
                if step == "max" and a < 2:
                    ps = put("misc", "image", a)
                    for t in range(NT):
                        mm = pe.matmul(ps[:, t * HEADS:(t + 1) * HEADS], Qf[:, b, t * P:(t + 1) * P],
                                       Kimg[:, b, :], start=True, stop=True)
                    mm.then_inc(full["misc"], 1)
                if step == "max_rows":
                    pe.wait_ge(nm_ready, a + 1)
                    ps = put("misc", "max_rows", a)
                    for t in range(NT):
                        mm = pe.transpose(ps[0:2 * HEADS, t * P // 2:(t + 1) * P // 2].bitcast(bf16),
                                          nm[:, b, t, :, :].rearrange("p n h -> p (n h)"), identb[:, :])
                    mm.then_inc(full["misc"], 1)
                if step == "image_rows":
                    pe.wait_ge(free["misc"], filled("misc", "max_rows", a))
                    ps = put("misc", "image_rows", a)
                    pe.matmul(ps[0:HEADS, :], Kimg[:, b, :], Qf[:, b, :], start=True, stop=False)
                    pe.matmul(ps[0:HEADS, :], pick[:, :], nmT[:, b, :], start=False, stop=True)\
                      .then_inc(full["misc"], 1)
                if step == "attend":
                    if i == 0:
                        pe.wait_ge(shifted[a], 16)
                    rows = MASK + PARTS if a < 2 else MASK
                    r, u, j = unit(i)
                    h = r * GROUP + j
                    ps = put(f"t{i % 2}", "weights", a, i)
                    for kb, col, w in blocks_of(a, u):
                        mm = pe.matmul(ps[:, col:col + w], Ks[0:rows, b, h, kb * P:(kb + 1) * P],
                                       Qs[0:rows, b, h, S - w:S], start=True, stop=(a >= 2))
                        if a < 2:
                            mm = pe.matmul(ps[:, col:col + P], identb[:, :], causal_k[:, :],
                                           start=False, stop=True)
                    mm.then_inc(full[f"t{i % 2}"], 1)
                if step == "values":
                    r, kb = i // NT, i % NT
                    u = kb // 2
                    half = 2 * (a * ROUNDS + r) + u
                    ps = put("pv", "values", a, r) if kb == 0 else place["pv"]
                    if kb % 2 == 0:
                        for n in (2 * GROUP * r + GROUP * u + 2, 2 * GROUP * r + GROUP * u + 3):
                            pe.wait_ge(free[f"t{n % 2}"], filled(f"t{n % 2}", "weights", a, n))
                    _, col, w = blocks_of(a, u)[kb % 2]
                    for j in range(GROUP):
                        mm = pe.matmul(ps[j * HC:(j + 1) * HC, S - w:S], Vs[:, b, kb, r * GROUP + j, :],
                                       probs[:, half % 2, j, col:col + w], start=(kb == 0),
                                       stop=(kb == NT - 1 and a >= 2))
                    if kb == 1:
                        mm.then_inc(half_done, 1)
                    if kb == NT - 1:
                        if a < 2:
                            if r == 0:
                                pe.wait_ge(free["misc"], filled("misc", "image_rows", a))
                            for j in range(GROUP):
                                mm = pe.matmul(ps[j * HC:(j + 1) * HC, :], Vimg[:, b, r * GROUP + j, :],
                                               Pimg[:, b, :], start=False, stop=True)
                        mm.then_inc(full["pv"], 1)
                if step == "turn_back":
                    pe.wait_ge(free["pv"], filled("pv", "values", a, i))
                    ps = put("misc", "turn_back", a, i)
                    for t in range(NT):
                        mm = pe.transpose(ps[:, t * P:(t + 1) * P], Ou[:, i % 2, t * P:(t + 1) * P], ident[:, :])
                    mm.then_inc(full["misc"], 1)
                if step == "o_rows":
                    pe.wait_ge(free["misc"], filled("misc", "turn_back", a, ROUNDS - 1))
                    ps = put("misc", "o_rows", a)
                    for t in range(NT):
                        mm = pe.transpose(ps[:, t * P:(t + 1) * P],
                                          On[:, t, :, :].rearrange("p h d -> p (h d)"), ident[:, :])
                    mm.then_inc(full["misc"], 1)
                if step == "x2t":
                    pe.wait_ge(free["misc"], filled("misc", "o_rows", a))
                    ps = put("misc", "x2t", a)
                    pe.matmul(ps[:, :], Wcp[:, :], OT[:, a, :], start=True, stop=True).then_inc(full["misc"], 1)
                if step == "sum":
                    pe.wait_ge(bias_ready, 1)
                    pe.wait_ge(free["misc"], filled("misc", "o_rows", 2 + a))
                    ps = put("misc", "sum", a)
                    for t in range(NT):
                        o = ps[:, t * D:(t + 1) * D]
                        pe.matmul(o, OT[:, a, t * P:(t + 1) * P], Wcp[:, :], start=True, stop=False)
                        pe.matmul(o, OT[:, 2 + a, t * P:(t + 1) * P], WsqT[:, 0, :], start=False, stop=False)
                        mm = pe.matmul(o, ones[0:1, :], brow[:, 3, :], start=False, stop=True)
                    mm.then_inc(full["misc"], 1)
                if step == "x3t":
                    pe.wait_ge(x3_ready, a + 1)
                    ps = put("misc", "x3t", a)
                    for t in range(NT):
                        mm = pe.transpose(ps[:, t * P:(t + 1) * P], X3[:, t, :], ident[:, :])
                    mm.then_inc(full["misc"], 1)
                if step == "router":
                    pe.wait_ge(in_moe, 16 * 9)
                    pe.wait_ge(free["misc"], filled("misc", "x3t", a))
                    ps = put("misc", "router", a)
                    n = NG + EXPERTS
                    for t in range(NT):
                        pe.matmul(ps[:, t * n:(t + 1) * n], X3T[:, a, t * P:(t + 1) * P], Wr[:, :],
                                  start=True, stop=False)
                        mm = pe.matmul(ps[:, t * n:(t + 1) * n], ones[0:1, :], rrow[:, :], start=False, stop=True)
                    mm.then_inc(full["misc"], 1)
                if step == "combine":
                    pe.wait_ge(comb_ready, a + 1)
                    ps = put("misc", "combine", a)
                    for t in range(NT):
                        mm = pe.transpose(ps[0:EXPERTS, t * P:(t + 1) * P],
                                          comb[:, a, t, :, :].rearrange("p g e -> p (g e)"), ident[:, :])
                    mm.then_inc(full["misc"], 1)
                if step == "bias2":
                    pe.wait_ge(free["misc"], filled("misc", "combine", a))
                    ps = put("misc", "bias2", a)
                    for t in range(NT):
                        mm = pe.matmul(ps[:, t * D:(t + 1) * D], combT[:, t * P:(t + 1) * P], B2[:, :],
                                       start=True, stop=True)
                    mm.then_inc(full["misc"], 1)
                if step == "expert":
                    if a == 0 and i == 0:
                        pe.wait_ge(in_experts, 16 * 2)
                    if i < EXPERTS:
                        for h in range(FH):
                            ps = put(f"s{h}", "hidden", a, i)
                            pe.matmul(ps[:, :], W1[:, i, h * P:(h + 1) * P], X3T[:, a, :], start=True, stop=True)\
                              .then_inc(full[f"s{h}"], 1)
                    if i > 0:
                        e = i - 1
                        for h in range(FH):
                            pe.wait_ge(free[f"s{h}"], filled(f"s{h}", "hidden", a, e))
                        ps = put("misc", "y", a, e)
                        for t in range(NT):
                            for h in range(FH):
                                mm = pe.matmul(ps[:, t * D:(t + 1) * D], hid[:, e % 2, h, t * P:(t + 1) * P],
                                               W2[:, e, h, :], start=(h == 0), stop=(h == FH - 1))
                        mm.then_inc(full["misc"], 1)


INPUTS = [
    "x", "cond_1024", "mask_Bx1x1xS_ff0", "L0_ffn_w_gate", "L0_ffn_w_up", "L0_ffn_w_down",
    "L1_cond_c_attn_w", "L1_cond_c_attn_b", "L1_cond_c_proj_w", "L1_cond_c_proj_b", "L1_cond_uk_w",
    "L1_cond_uk_b", "L1_cond_uv_w", "L1_cond_uv_b", "L1_ffn_in_proj_w", "L1_ffn_in_proj_b",
    "L1_ffn_out_proj_w", "L1_ffn_out_proj_b", "L1_ffn_ln1_g", "L1_ffn_ln1_b", "L1_ffn_ln2_g",
    "L1_ffn_ln2_b", "L1_ffn_w_group", "L1_ffn_b_group", "L1_ffn_w_expert", "L1_ffn_b_expert",
    "L1_ffn_w1", "L1_ffn_b1", "L1_ffn_w2", "L1_ffn_b2",
]


def kernel(**inputs):
    import numpy as _np
    import concourse.bacc as _bacc
    from concourse import mybir as _mybir
    from concourse.bass_utils import run_bass_kernel_spmd as _run

    nc = _bacc.Bacc("TRN2", target_bir_lowering=False, num_devices=1)
    arrays, aps = {}, {}
    for name in INPUTS:
        a = _np.ascontiguousarray(inputs[name])
        arrays[f"in_{name}"] = a
        aps[name] = nc.dram_tensor(f"in_{name}", a.shape, _mybir.dt.from_np(a.dtype), kind="ExternalInput").ap()
    out = nc.dram_tensor("out_x", (B, S, D), _mybir.dt.float32, kind="ExternalOutput").ap()
    two_layers(nc, aps, out)
    r = _run(nc, [arrays], core_ids=[0])
    return r.results[0]["out_x"]
```

```python
import concourse.bass as bass
from concourse import mybir
from contextlib import ExitStack

P = 128
B, S, D = 2, 512, 128
NT = S // P
TILES = B * NT
INNER = 512
NC = INNER // P
HEADS = 16
HD = D // HEADS
GROUP = 4
ROUNDS = HEADS // GROUP
HALF = HEADS // 2
HC = 32
PARTS = 3
STACK = PARTS * PARTS * HD
SHIFT = STACK
MASK = SHIFT + 2
EXPERTS, NG, F = 8, 4, 256
FH = F // P
EPS = 1e-5
MAGIC = 1.5 * 2.0 ** 23
BIG = -1e30
INST = 4
UNITS = 2 * HEADS


def spread(steps, begin, middle, end):
    half = len(steps) / 2
    return [(begin + (middle - begin) * n / half if n < half else middle + (end - middle) * (n / half - 1), step)
            for n, step in enumerate(steps)]


def in_two(steps):
    return steps[:(len(steps) + 1) // 2], steps[(len(steps) + 1) // 2:]


def attention(a):
    steps = []
    for i in range(UNITS + 2 * GROUP):
        if i < UNITS:
            steps += [("attend", a, i)]
        if i > GROUP and i % GROUP in (1, 2) and (i - GROUP) // GROUP * 2 < ROUNDS * NT:
            steps += [("values", a, (i - GROUP) // GROUP * 2 + i % GROUP - 1)]
        if i > 2 * GROUP and i % (2 * GROUP) == 4:
            steps += [("turn_back", a, i // (2 * GROUP) - 1)]
    n = steps.index(("attend", a, UNITS - 1)) + 1
    return steps[:n], steps[n:] + [("o_rows", a, 0)]


def program_order():
    scores = [in_two([("scores", a, n) for n in range(HEADS * NT)]) for a in range(INST)]
    units, ends = zip(*(attention(a) for a in range(INST)))
    units = [in_two(steps) for steps in units]
    qkv = [[("x1t", a, 0)] * (a < B) + [(n, a, 0) for n in ("q", "k", "v")] for a in range(INST)]
    shift = [[[("max", a, g), ("max_rows", a, g)] for g in range(2)] for a in range(INST)]
    ffn_up = [[("ffn_in", b, 0)] + [("ffn_up", b, t) for t in range(NT)] for b in range(B)]
    ffn_down = [[("r2t", b, 0)] + [x for t in range(1, NT) for x in (("r2t", b, t), ("down", b, t - 1))]
                + [("down", b, NT - 1)] for b in range(B)]
    moe_in = [[(n, b, 0) for n in ("sum", "x3t", "router", "route", "combine", "bias2")]
              for b in range(B)]
    first_hidden = [[("hidden", b, 0), ("hidden", b, 1)] for b in range(B)]
    experts = [in_two([x for e in range(2, EXPERTS) for x in (("y", b, e - 2), ("hidden", b, e))]
               + [("y", b, EXPERTS - 2), ("y", b, EXPERTS - 1)]) for b in range(B)]
    setup = [("setup", 0, 0)] + ffn_up[0]
    turn_weights, prepare = [("turn_weights", 0, 0)], [("prepare", 0, 0)]
    load_experts = [("load_experts", 0, 0)]
    out = [[("out", b, 0)] for b in range(B)]
    plan = []
    for steps, begin, middle, end in (
            (setup, 0, 10, 20),
            (turn_weights, 26.24, 33.3, 41.72),
            (ffn_down[0], 22.74, 23.37, 30.88),
            (prepare, 29.36, 41.28, 48.56),
            (qkv[0], 41.77, 45.87, 52.36),
            (ffn_up[1], 48.17, 48.17, 48.17),
            (scores[0][0], 57.97, 72.83, 72.84),
            (scores[0][1], 60.15, 87.6, 108.61),
            (ffn_down[1], 52.56, 52.56, 52.56),
            (qkv[1], 56.22, 65.93, 83.35),
            (shift[0][0], 94.68, 97.14, 97.14),
            (shift[0][1], 107.92, 109.07, 116.48),
            (scores[1][0], 99.43, 105.75, 114.01),
            (scores[1][1], 109.88, 122.35, 146.27),
            (units[0][0], 102.43, 110.74, 118.03),
            (units[0][1], 121.17, 130.52, 151.68),
            (shift[1][0], 117.12, 120.82, 123.01),
            (shift[1][1], 146.13, 152.72, 158.28),
            (ends[0], 152.5, 152.5, 159.59),
            (qkv[2], 158.42, 161.31, 162.66),
            (units[1][0], 156.71, 164.44, 172.18),
            (units[1][1], 171.44, 174.14, 176.83),
            (scores[2][0], 169.16, 176.32, 182.85),
            (scores[2][1], 181.22, 207.36, 221.88),
            (ends[1], 177.4, 179.05, 180.7),
            (qkv[3], 210.52, 211.49, 213.04),
            (shift[2][0], 186.89, 189.48, 191.54),
            (shift[2][1], 221.37, 222.53, 225.43),
            (scores[3][0], 221.72, 227.94, 242.74),
            (scores[3][1], 243.94, 255.44, 267.91),
            (units[2][0], 209.04, 218.48, 228.48),
            (units[2][1], 227.79, 238.41, 248.76),
            (load_experts, 267.85, 269.64, 273.37),
            (shift[3][0], 244.53, 246.49, 248.28),
            (shift[3][1], 269.03, 269.03, 273.09),
            (ends[2], 249.03, 253.8, 257.71),
            (units[3][0], 252.59, 264.96, 275.97),
            (units[3][1], 279.06, 293.52, 307),
            (moe_in[0][:3], 260.33, 263.76, 270.59),
            (moe_in[0][3:], 270.67, 275.49, 280.31),
            (first_hidden[0], 274.03, 283.01, 286.69),
            (experts[0][0], 279.99, 301.12, 311.06),
            (experts[0][1], 310.64, 325.47, 336.83),
            (ends[3], 308.48, 308.48, 308.48),
            (moe_in[1][:3], 314.56, 317.6, 325.11),
            (moe_in[1][3:], 327.58, 336.28, 345.43),
            (out[0], 350.49, 404.01, 406.73),
            (first_hidden[1], 332.56, 335.02, 335.23),
            (experts[1][0], 376.02, 381.61, 384.47),
            (experts[1][1], 393.26, 425.86, 425.86),
            (out[1], 441.45, 442.55, 443.65)):
        plan += spread(steps, begin, middle, end)
    plan.sort(key=lambda x: x[0])
    return [step for _, step in plan]


def unit(i):
    return i // (2 * GROUP), i // GROUP % 2, i % GROUP


def scores_places(order):
    others = [n for n, (step, _, _) in enumerate(order) if step in ("attend", "ffn_up", "r2t", "down")]
    where, turn = {}, 0
    for n, (step, a, i) in enumerate(order):
        if step == "scores":
            alone = all(abs(n - m) > 8 for m in others)
            where[a, i] = ("s0", "s1", "t0", "t1")[turn % 4] if alone else f"s{turn % 2}"
            turn += 1
    return where


def place_jobs(order):
    where, waiting = scores_places(order), 0
    places = {n: {} for n in ("misc", "s0", "s1", "t0", "t1", "pv")}

    def add(place, *name):
        places[place][name] = len(places[place])

    for step, a, i in order:
        if step == "setup":
            add("misc", "sums"), add("t1", "ternary")
        if step == "turn_weights":
            add("misc", "wi"), add("t0", "turned"), add("t1", "projection")
        if step == "prepare":
            add("misc", "small"), add("s0", "image_v"), add("s1", "joined")
        if step == "ffn_in":
            add("misc", "rt", a)
        if step == "ffn_up":
            add(f"t{i % 2}", "up", a, i)
        if step == "r2t":
            add(f"t{i % 2}", "r2t", a, i)
        if step == "down" and i == 0:
            add("pv", "down", a)
        if step in ("x1t", "q", "k", "v", "o_rows",
                    "sum", "x3t", "router", "combine", "bias2"):
            add("misc", step, a)
        if step == "scores":
            add(where[a, i], "scores", a, i)
        if step == "max" and a < 2:
            add("misc", "image", a, i)
        if step == "max_rows":
            add("misc", "max_rows", a, i)
        if step == "attend":
            add(f"t{i % 2}", "weights", a, i)
        if step == "values" and i % NT == 0:
            add("pv", "values", a, i // NT)
        if step == "turn_back":
            add("misc", "turn_back", a, i)
        if step == "hidden":
            assert waiting < 2
            waiting += 1
            add("s0", "hidden", a, i), add("s1", "hidden", a, i)
        if step == "y":
            waiting -= 1
            add("misc", "y", a, i)
    return places


def blocks_of(a, u):
    out, col = [], 0
    for kb in (2 * u, 2 * u + 1):
        w = S - kb * P if a < 2 else S
        out.append((kb, col, w))
        col += w
    return out


def two_layers(nc, A, out):
    fp32 = mybir.dt.float32
    bf16 = mybir.dt.bfloat16
    ALU = mybir.AluOpType
    ACT = mybir.ActivationFunctionType
    AX = mybir.AxisListType.X

    ORDER = program_order()
    JOB = place_jobs(ORDER)
    SCORES = scores_places(ORDER)
    NTH = {x: sum(y[0] == x[0] for y in ORDER[:n + 1]) for n, x in enumerate(ORDER)}

    def drows(ap, n, count):
        return bass.AP(tensor=ap.tensor, offset=ap.offset, ap=[[0, n], [1, count]])

    ctx = ExitStack()
    with ctx:
        def sb(name, shape, dt=fp32):
            return ctx.enter_context(nc.sbuf_tensor(name, shape, dt))

        def pb(name, shape):
            return ctx.enter_context(nc.psum_tensor(name, shape, fp32))

        def sem(name):
            return ctx.enter_context(nc.semaphore(name))

        parts_dram = [[nc.dram_tensor(f"parts_{n}{a}", (PARTS, P, S), bf16, kind="Internal").ap()
                       for n in "qk"] for a in range(INST)]
        shift_dram = [nc.dram_tensor(f"shift_{a}", (2, HEADS, S), bf16, kind="Internal").ap()
                      for a in range(INST)]

        ident = sb("ident", [P, P])
        identb = sb("identb", [P, P], bf16)
        causal_q = sb("causal_q", [P, P], bf16)
        causal_k = sb("causal_k", [P, P], bf16)
        ones = sb("ones", [P, P])
        head_grid = sb("head_grid", [P, HD, HEADS])
        head_of = sb("head_of", [P, HEADS])
        prior = sb("prior", [P, NT, NG])
        magic = sb("magic", [P, 1])
        silu_of_one = sb("silu_of_one", [P, 1])
        halves = sb("halves", [P, NT])
        zrow = sb("zrow", [2, S], bf16)
        orow = sb("orow", [PARTS, S], bf16)

        X = sb("X", [P, TILES, D])
        Wca = sb("Wca", [P, 3 * D])
        Wcaq = sb("Wcaq", [P, 2, D])
        Wcp = sb("Wcp", [P, D])
        WinT = sb("WinT", [P, 3, D])
        WcpT = sb("WcpT", [P, D])
        Wjoin = sb("Wjoin", [P, 3, D])
        bjoin = sb("bjoin", [P, 2])
        vbias = sb("vbias", [P, 2, D])
        WsqT = sb("WsqT", [P, 3, D])
        rows5 = sb("rows5", [5, D])
        rows5p = sb("rows5p", [5, D])
        rows17 = sb("rows17", [17, D])
        cols5 = sb("cols5", [P, 5])
        cols17 = sb("cols17", [P, 17])
        condr = sb("condr", [B, D])
        condT = sb("condT", [P, B])
        brow = sb("brow", [1, 4, D])
        Wr = sb("Wr", [P, NG + EXPERTS])
        rbias = sb("rbias", [P, NG + EXPERTS])
        B2 = sb("B2", [EXPERTS, D])
        norm_gb = sb("norm_gb", [P, 4, D])

        shared = sb("shared", [P, 7936])
        taken = {"first": 0, "later": 0}

        def part(when, shape, dt=fp32):
            n = 1
            for x in shape:
                n *= x
            words = n if dt == fp32 else n // 2
            ap = shared[:, taken[when]:taken[when] + words]
            taken[when] += words
            if dt != fp32:
                ap = ap.bitcast(dt)
            if len(shape) == 2:
                return ap.rearrange("p (a b) -> p a b", a=shape[0])
            if len(shape) == 3:
                return ap.rearrange("p (a b c) -> p a b c", a=shape[0], b=shape[1])
            return ap

        W3 = part("first", [3, INNER])
        xtmp = part("first", [TILES, D])
        R1 = part("first", [TILES, D], bf16)
        RT = part("first", [B, S], bf16)
        Wt = part("first", [3, INNER], bf16)
        WtT = part("first", [3 * NC, P], bf16)
        Win = part("first", [3, D])
        Wsq = part("first", [3, D])
        cond_all = part("first", [B, D])
        R2 = part("first", [2, INNER], bf16)
        mrow = part("first", [S])[0:B, :]
        mres = part("first", [S])[0:B, :]
        mparts = xtmp.rearrange("p t d -> p (t d)").bitcast(bf16)[0:B, 0:PARTS * S]\
            .rearrange("p (n s) -> p n s", n=PARTS)
        hid = part("later", [2, FH, S])
        acc = part("later", [B, NT, D])
        X3 = part("later", [NT, D])
        OT = part("later", [INST, S])
        On = part("later", [NT, HEADS, HD])
        Ou = part("later", [2, S])

        wdot = sb("wdot", [P, 6, TILES])
        absum = sb("absum", [P, 3])
        wmean = sb("wmean", [P, 3])
        wscale = sb("wscale", [P, 3])
        q1 = sb("q1", [P, 5, TILES])
        q2 = sb("q2", [P, 4, TILES])
        R2T = sb("R2T", [P, 2, INNER], bf16)
        X1 = sb("X1", [P, TILES, D])

        XT = sb("XT", [P, 2, S])
        Qf = sb("Qf", [P, 2, S])
        Kf = sb("Kf", [P, S])
        X3T = Qf
        qres = sb("qres", [P, S])
        kres = sb("kres", [P, S])
        Qp = sb("Qp", [P, PARTS, S], bf16)
        Kp = sb("Kp", [P, PARTS, S], bf16)
        Qs = sb("Qs", [P, 2, HEADS, S], bf16)
        Ks = sb("Ks", [P, 2, HEADS, S], bf16)
        wexp = Ks[:, 0, :, :].rearrange("p h s -> p (h s)").bitcast(fp32)
        W1 = wexp[:, 0:EXPERTS * F].rearrange("p (e f) -> p e f", e=EXPERTS)
        W2 = wexp[:, EXPERTS * F:].rearrange("p (e h d) -> p e h d", e=EXPERTS, h=FH)
        Vs = sb("Vs", [P, 2, NT, HEADS, HC])
        kimg = sb("kimg", [P, B])
        Kimg = sb("Kimg", [P, B, HEADS])
        Vimg = sb("Vimg", [P, B, HEADS, HD + 1])
        mx = sb("mx", [P, 2, NT, HEADS])
        nm = sb("nm", [P, 2, NT, 2, 2, HALF], bf16)
        nmT = sb("nmT", [HEADS, 2, 2, S], bf16)
        simg = sb("simg", [P, B, NT, HEADS])
        Pimg = sb("Pimg", [P, B, NT, HEADS])
        Zimg = sb("Zimg", [P, B, NT, HEADS, HD + 1])
        sums = sb("sums", [P, NT, GROUP, HD + 1])
        probs = sb("probs", [P, 2, GROUP, 2 * S])
        rden = sb("rden", [P, NT, GROUP])

        stats = sb("stats", [P, NT, 6])
        mv = sb("mv", [P, NT, 2])
        ve = sb("ve", [P, NT])
        rstd = sb("rstd", [P, NT])
        lg = sb("lg", [P, NT, NG + EXPERTS])
        dl = sb("dl", [P, NT, NG + EXPERTS])
        ex = sb("ex", [P, NT, NG + EXPERTS])
        rs = sb("rs", [P, 3, NT])
        rg = sb("rg", [P, 4, NT, NG])
        comb = sb("comb", [P, B, NT, NG, 2])
        combT = X[:, :, :].rearrange("p t d -> p (t d)")[0:EXPERTS, 0:S]

        early = probs[:, :, :, :].rearrange("p n j s -> p (n j s)")

        def H(b, t):
            return early[:, (b * NT + t) * INNER:(b * NT + t + 1) * INNER]

        def SG(t):
            return early[:, (TILES + t % 2) * INNER:(TILES + t % 2 + 1) * INNER]

        def Y(t):
            return early[:, (TILES + 2 + t % 2) * INNER:(TILES + 3 + t % 2) * INNER]

        wtmp = early[:, (TILES + 4) * INNER:(TILES + 7) * INNER].rearrange("p (n d) -> p n d", n=3)

        place = {"misc": pb("ps_misc", [P, S]), "pv": pb("ps_pv", [P, S]),
                 "s0": pb("ps_s0", [P, S]), "s1": pb("ps_s1", [P, S]),
                 "t0": pb("ps_t0", [P, 2 * S]), "t1": pb("ps_t1", [P, 2 * S])}
        full = {n: sem(f"{n}_full") for n in place}
        free = {n: sem(f"{n}_free") for n in place}

        def filled(n, *name):
            return JOB[n][name] + 1

        in_experts = sem("in_experts")
        in_x, in_w3, in_att, in_mask, in_moe = (sem(n) for n in
                                                ("in_x", "in_w3", "in_att", "in_mask", "in_moe"))
        pool_const = sem("pool_const")
        dve_step = sem("dve_step")
        pool_step = sem("pool_step")
        w_exp_in, w_exp = sem("w_exp_in"), sem("w_exp")
        r1_ready = sem("r1_ready")
        ternary_ready = sem("ternary_ready")
        setup_pe = sem("setup_pe")
        perm_ready, wcaq_ready = sem("perm_ready"), sem("wcaq_ready")
        sums_ready, wscaled_ready = sem("sums_ready"), sem("wscaled_ready")
        scale_ready = sem("scale_ready")
        silu_ready = sem("silu_ready")
        q2_ready = sem("q2_ready")
        y_ready = sem("y_ready")
        r2_ready = sem("r2_ready")
        qhi_ready, khi_ready = sem("qhi_ready"), sem("khi_ready")
        qp_ready, kp_ready = sem("qp_ready"), sem("kp_ready")
        parts_q = [sem(f"parts_q{a}") for a in range(INST)]
        parts_k = [sem(f"parts_k{a}") for a in range(INST)]
        stacked = [[sem(f"stacked{a}_{n}") for n in range(2)] for a in range(INST)]
        mparts_ready, bias_ready = sem("mparts_ready"), sem("bias_ready")
        half_done = sem("half_done")
        fixed_rows = sem("fixed_rows")
        stack_init = sem("stack_init")
        nm_ready = sem("nm_ready")
        simg_ready, pimg_ready, zimg_ready = sem("simg_ready"), sem("pimg_ready"), sem("zimg_ready")
        turned_ready, residual_ready = sem("turned_ready"), sem("residual_ready")
        shift_out = [sem(f"shift_out{a}") for a in range(INST)]
        shifted = [[sem(f"shifted{a}_{g}") for g in range(2)] for a in range(INST)]
        ve_ready, rstd_ready, gained = sem("ve_ready"), sem("rstd_ready"), sem("gained")
        x3_ready = sem("x3_ready")
        dl_ready, ex_ready = sem("dl_ready"), sem("ex_ready")
        comb_ready = sem("comb_ready")
        out_ready, stored = sem("out_ready"), sem("stored")

        block = ctx.enter_context(nc.Block())

        @block.sync
        def _(sp):
            for step, a, i in ORDER:
                b = a % 2
                if step == "setup":
                    sp.dma_start(cond_all[:, :, :].rearrange("p b d -> p (b d)"),
                                 drows(A["cond_1024"], P, B * D)).then_inc(in_x, 16)
                    xv = A["x"].rearrange("b (t p) d -> p (b t) d", p=P)
                    for b in range(B):
                        sp.dma_start(X[:, b * NT:(b + 1) * NT, :],
                                     xv[:, b * NT:(b + 1) * NT, :]).then_inc(in_x, 16)
                    for n, w in enumerate(("L0_ffn_w_gate", "L0_ffn_w_up")):
                        sp.dma_start(W3[:, n, :].rearrange("p (a d) -> p a d", d=D),
                                     A[w].rearrange("(a p) d -> p a d", p=P)).then_inc(in_w3, 16)
                    sp.dma_start(W3[:, 2, :], A["L0_ffn_w_down"]).then_inc(in_w3, 16)
                    sp.dma_start(mrow[:, :], A["mask_Bx1x1xS_ff0"].rearrange("b x y s -> (b x y) s"))\
                      .then_inc(in_mask, 16)
                    for dst, src in (
                            (rows5[0:2, :], A["L1_cond_c_attn_b"][0:2 * D].rearrange("(r d) -> r d", d=D)),
                            (rows5[2:4, :], A["L1_ffn_in_proj_b"][0:2 * D].rearrange("(r d) -> r d", d=D)),
                            (rows5[4:5, :], A["L1_cond_uk_b"].rearrange("(r d) -> r d", r=1)),
                            (rows17[0:16, :], A["L1_ffn_b1"].rearrange("e (h p) -> (e h) p", p=P)),
                            (rows17[16:17, :], A["L1_cond_c_proj_b"].rearrange("(r d) -> r d", r=1)),
                            (condr[:, :], A["cond_1024"]),
                            (Wca[:, :], A["L1_cond_c_attn_w"]),
                            (Wcp[:, :], A["L1_cond_c_proj_w"]),
                            (Win[:, :, :], A["L1_ffn_in_proj_w"].rearrange("(a p) d -> p a d", p=P)),
                            (Wsq[:, 0, :], A["L1_ffn_out_proj_w"]),
                            (Wsq[:, 1, :], A["L1_cond_uk_w"]),
                            (Wsq[:, 2, :], A["L1_cond_uv_w"]),
                            (vbias[:, 0, :], drows(A["L1_cond_c_attn_b"][2 * D:3 * D], P, D)),
                            (brow[:, 0, :], A["L1_ffn_in_proj_b"][2 * D:3 * D].rearrange("(r d) -> r d", r=1)),
                            (brow[:, 1, :], A["L1_cond_uv_b"].rearrange("(r d) -> r d", r=1)),
                            (brow[:, 2, :], A["L1_cond_c_proj_b"].rearrange("(r d) -> r d", r=1)),
                            (brow[:, 3, :], A["L1_ffn_out_proj_b"].rearrange("(r d) -> r d", r=1))):
                        sp.dma_start(dst, src).then_inc(in_att, 16)
                if step == "prepare":
                    sp.wait_ge(pool_const, 1)
                    sp.wait_ge(mparts_ready, 1)
                    for b in range(B):
                        for n in range(PARTS):
                            src = mparts[b:b + 1, n, :].unsqueeze(1).to_broadcast([1, HEADS, S])
                            sp.dma_start(Ks[MASK + n:MASK + n + 1, b, :, :], src).then_inc(fixed_rows, 16)
                        sp.dma_start(Qs[SHIFT:SHIFT + 2, b, :, :],
                                     zrow[:, :].unsqueeze(1).to_broadcast([2, HEADS, S])).then_inc(fixed_rows, 16)
                        sp.dma_start(Ks[SHIFT:SHIFT + 2, b, :, :],
                                     orow[0:2, :].unsqueeze(1).to_broadcast([2, HEADS, S])).then_inc(fixed_rows, 16)
                        sp.dma_start(Qs[MASK:MASK + PARTS, b, :, :],
                                     orow[:, :].unsqueeze(1).to_broadcast([PARTS, HEADS, S])).then_inc(fixed_rows, 16)
                if step == "v":
                    sp.wait_ge(qp_ready, a + 1)
                    sp.dma_start(parts_dram[a][0].rearrange("n p s -> p n s"), Qp[:, :, :]).then_inc(parts_q[a], 16)
                    sp.wait_ge(kp_ready, a + 1)
                    sp.dma_start(parts_dram[a][1].rearrange("n p s -> p n s"), Kp[:, :, :]).then_inc(parts_k[a], 16)
                    row, count = HEADS * S, HEADS // 2 * S
                    for half in range(2):
                        heads = slice(half * HEADS // 2, (half + 1) * HEADS // 2)
                        sp.wait_ge(parts_q[a], 16)
                        for n in range(PARTS):
                            r = n * PARTS * HD
                            src = parts_dram[a][0][n]
                            sp.dma_start(Qs[r:r + PARTS * HD, b, heads, :].rearrange("p h s -> p (h s)"),
                                         bass.AP(tensor=src.tensor, offset=src.offset + half * count,
                                                 ap=[[0, PARTS], [row, HD], [1, count]])).then_inc(stacked[a][half], 16)
                        sp.wait_ge(parts_k[a], 16)
                        src = parts_dram[a][1]
                        for n in range(PARTS):
                            r = n * PARTS * HD
                            sp.dma_start(Ks[r:r + PARTS * HD, b, heads, :].rearrange("p h s -> p (h s)"),
                                         bass.AP(tensor=src.tensor, offset=src.offset + half * count,
                                                 ap=[[row, PARTS * HD], [1, count]])).then_inc(stacked[a][half], 16)
                if step == "max_rows":
                    sp.wait_ge(free["misc"], filled("misc", "max_rows", a, i))
                    sp.dma_start(shift_dram[a][i], nmT[:, b, i, :]).then_inc(shift_out[a], 16)
                    sp.wait_ge(shift_out[a], 16 * (i + 1))
                    sp.dma_start(Qs[SHIFT:SHIFT + 2, b, i * HALF:(i + 1) * HALF, :].rearrange("p h s -> p (h s)"),
                                 shift_dram[a][i].rearrange("(n h) s -> n (h s)", h=HALF)).then_inc(shifted[a][i], 16)
                if step == "load_experts":
                    sp.wait_ge(full["t1"], filled("t1", "weights", 2, UNITS - 1))
                    sp.dma_start(W1[:, :, :], A["L1_ffn_w1"].rearrange("e d f -> d e f")).then_inc(in_experts, 16)
                    sp.dma_start(W2[:, :, :, :], A["L1_ffn_w2"].rearrange("e (h p) d -> p e h d", p=P))\
                      .then_inc(in_experts, 16)
                if step == "out":
                    sp.wait_ge(out_ready, a + 1)
                    sp.dma_start(out[a].rearrange("(t p) d -> p t d", p=P), acc[:, a, :, :]).then_inc(stored, 16)
            sp.wait_ge(stored, 16 * B)

        @block.gpsimd
        def _(pool):
            done = [0]
            norms = 0

            def then_wait(ins):
                done[0] += 1
                ins.then_inc(pool_step, 1)
                pool.wait_ge(pool_step, done[0])

            for step, a, i in ORDER:
                b = a % 2
                if step == "setup":
                    pool.memset(ident[:, :], 0.0)
                    pool.memset(identb[:, :], 0.0)
                    pool.memset(causal_q[:, :], 0.0)
                    pool.memset(causal_k[:, :], 0.0)
                    pool.memset(head_grid[:, :, :], 0.0)
                    then_wait(pool.memset(Vimg[:, :, :, HD:HD + 1], 1.0))
                    pool.affine_select(out=ident[:, :], in_=ident[:, :], compare_op=ALU.not_equal, fill=1.0,
                                       base=0, pattern=[[-1, P]], channel_multiplier=1)
                    pool.affine_select(out=identb[:, :], in_=identb[:, :], compare_op=ALU.not_equal, fill=1.0,
                                       base=0, pattern=[[-1, P]], channel_multiplier=1)
                    pool.affine_select(out=causal_q[:, :], in_=causal_q[:, :], compare_op=ALU.is_ge, fill=BIG,
                                       base=0, pattern=[[-1, P]], channel_multiplier=1)
                    pool.affine_select(out=causal_k[:, :], in_=causal_k[:, :], compare_op=ALU.is_ge, fill=BIG,
                                       base=0, pattern=[[1, P]], channel_multiplier=-1)
                    pool.affine_select(out=head_grid[:, :, :], in_=head_grid[:, :, :],
                                       compare_op=ALU.not_equal, fill=1.0,
                                       base=0, pattern=[[-HEADS, HD], [-1, HEADS]], channel_multiplier=1)
                    pool.memset(ones[:, :], 1.0)
                    pool.memset(magic[:, :], MAGIC)
                    pool.memset(halves[:, :], -0.5)
                    for g in range(NG):
                        pool.memset(prior[:, :, g:g + 1], float(NG - g))
                    pool.memset(orow[:, :], 1.0)
                    pool.memset(zrow[:, :], 0.0).then_inc(pool_const, 1)
                    pool.memset(Vs[:, 0, :, :, :], 0.0)
                    then_wait(pool.memset(Vs[:, 1, :, :, :], 0.0))
                    for n in range(2):
                        pool.memset(Vs[:, n, :, :, HD:HD + 1], 1.0).then_inc(stack_init, 1)
                    for dst, src in (
                            (Wr[:, 0:NG], A["L1_ffn_w_group"]),
                            (Wr[:, NG:].rearrange("p (g e) -> p g e", e=2),
                             A["L1_ffn_w_expert"].rearrange("g d e -> d g e")),
                            (rbias[:, 0:NG], drows(A["L1_ffn_b_group"], P, NG)),
                            (rbias[:, NG:], drows(A["L1_ffn_b_expert"], P, EXPERTS)),
                            (B2[:, :], A["L1_ffn_b2"]),
                            (norm_gb[:, 0, :], drows(A["L1_ffn_ln1_g"], P, D)),
                            (norm_gb[:, 1, :], drows(A["L1_ffn_ln1_b"], P, D)),
                            (norm_gb[:, 2, :], drows(A["L1_ffn_ln2_g"], P, D)),
                            (norm_gb[:, 3, :], drows(A["L1_ffn_ln2_b"], P, D))):
                        pool.dma_start(dst, src).then_inc(in_moe, 16)
                if step == "turn_weights":
                    pool.wait_ge(r1_ready, 1)
                    pool.wait_ge(in_mask, 16)
                    then_wait(pool.tensor_scalar(mparts[:, 0, :], mrow[:, :], 1.0, None, ALU.mult))
                    then_wait(pool.tensor_tensor(mres[:, :], mrow[:, :], mparts[:, 0, :], ALU.subtract))
                    then_wait(pool.tensor_scalar(mparts[:, 1, :], mres[:, :], 1.0, None, ALU.mult))
                    pool.tensor_tensor(mparts[:, 2, :], mres[:, :], mparts[:, 1, :], ALU.subtract)\
                        .then_inc(mparts_ready, 1)
                    pool.wait_ge(in_att, 16 * 17)
                    pool.tensor_tensor(brow[:, 2, :], brow[:, 2, :], brow[:, 3, :], ALU.add)\
                        .then_inc(bias_ready, 1)
                if step == "max_rows" and a < 2:
                    pool.wait_ge(pimg_ready, NTH[step, a, i])
                    pool.wait_ge(perm_ready, 1)
                    pool.wait_ge(free["s0"], filled("s0", "image_v"))
                    heads, shape = slice(i * HALF, (i + 1) * HALF), [P, NT, HALF, HD + 1]
                    pool.tensor_tensor(Zimg[:, b, :, heads, :], Vimg[:, b, heads, :].unsqueeze(1).to_broadcast(shape),
                                       Pimg[:, b, :, heads].unsqueeze(3).to_broadcast(shape),
                                       ALU.mult).then_inc(zimg_ready, 1)
                if step in ("sum", "out"):
                    norms += 1
                    pool.wait_ge(ve_ready, norms)
                    pool.tensor_tensor(rstd[:, :], ve[:, :], halves[:, :], ALU.pow).then_inc(rstd_ready, 1)
                if step == "sum":
                    pool.wait_ge(in_moe, 16 * 9)
                    x1 = X1[:, a * NT:(a + 1) * NT, :]
                    pool.tensor_tensor(x1, x1, norm_gb[:, 3:4, :].to_broadcast([P, NT, D]), ALU.add)\
                        .then_inc(residual_ready, 1)

        @block.scalar
        def _(act):
            def take(n, *name):
                act.wait_ge(full[n], filled(n, *name))
                return place[n]

            for step, a, i in ORDER:
                b = a % 2
                if step == "setup":
                    act.wait_ge(w_exp_in, 1)
                    act.activation(wdot[:, 3, :], wdot[:, 1, :], ACT.Exp).then_inc(w_exp, 1)
                    act.wait_ge(in_w3, 16 * 3)
                    for n in range(3):
                        last = act.activation(wtmp[:, n, :], W3[:, n, :], ACT.Abs, accum_out=absum[:, n:n + 1])
                    last.then_inc(sums_ready, 1)
                    act.wait_ge(sums_ready, 1)
                    act.wait_ge(pool_const, 1)
                    act.wait_ge(free["misc"], filled("misc", "sums"))
                    for n in range(3):
                        last = act.activation(wtmp[:, n, :], W3[:, n, :], ACT.Identity, bias=magic[:, 0:1],
                                              scale=wscale[:, n:n + 1])
                    last.then_inc(wscaled_ready, 1)
                    act.activation(silu_of_one[:, :], magic[:, :], ACT.Silu)
                    ps = take("t1", "ternary")
                    act.activation(WtT[:, 0:8, :].rearrange("p a d -> p (a d)"),
                                   ps[:, 0:S].bitcast(bf16), ACT.Copy)
                    act.activation(WtT[:, 8:12, :].rearrange("p a d -> p (a d)"),
                                   ps[:, S:S + S // 2].bitcast(bf16), ACT.Copy).then_inc(free["t1"], 1)
                if step == "turn_weights":
                    ps = take("misc", "wi")
                    for n in range(3):
                        src = ps[:, n * D:(n + 1) * D]
                        if n < 2:
                            act.activation(WinT[:, n, :].rearrange("p (d h) -> p d h", h=HEADS),
                                           src.rearrange("p (h d) -> p d h", d=HD), ACT.Copy)
                        else:
                            act.activation(WinT[:, n, :], src, ACT.Copy).then_inc(free["misc"], 1)
                    ps = take("t0", "turned")
                    act.activation(WsqT[:, 0, :], ps[:, 0:D], ACT.Copy)
                    act.activation(WsqT[:, 1, :].rearrange("p (d h) -> p d h", h=HEADS),
                                   ps[:, D:2 * D].rearrange("p (h d) -> p d h", d=HD), ACT.Copy)
                    act.activation(WsqT[:, 2, :], ps[:, 2 * D:3 * D], ACT.Copy)
                    act.activation(condT[:, :], ps[:, 3 * D:3 * D + B], ACT.Copy).then_inc(free["t0"], 1)
                    ps = take("t1", "projection")
                    act.activation(WcpT[:, :], ps[:, 0:D], ACT.Copy).then_inc(free["t1"], 1)
                    act.wait_ge(in_att, 16 * 17)
                    for n in range(2):
                        last = act.activation(Wcaq[:, n, :].rearrange("p (d h) -> p d h", h=HEADS),
                                              Wca[:, n * D:(n + 1) * D].rearrange("p (h d) -> p d h", d=HD),
                                              ACT.Copy)
                    last.then_inc(wcaq_ready, 1)
                if step == "ffn_in":
                    ps = take("misc", "rt", a)
                    act.activation(RT[:, a, :], ps[:, 0:S // 2].bitcast(bf16), ACT.Copy).then_inc(free["misc"], 1)
                if step == "ffn_up":
                    t = a * NT + i
                    ps = take(f"t{i % 2}", "up", a, i)
                    act.wait_ge(scale_ready, 1)
                    act.activation(SG(i), ps[:, 0:INNER], ACT.Silu, scale=q1[:, 3, t:t + 1]).then_inc(silu_ready, 1)
                if step == "r2t":
                    t = a * NT + i
                    act.wait_ge(q2_ready, a + 1)
                    if t >= 2:
                        act.wait_ge(r2_ready, t - 1)
                    act.activation(Y(i), H(a, i), ACT.Identity, bias=magic[:, 0:1],
                                   scale=q2[:, 2, t:t + 1]).then_inc(y_ready, 1)
                if step == "prepare":
                    ps = take("s1", "joined")
                    act.activation(Wjoin[:, :, :].rearrange("p n d -> p (n d)"), ps[:, 0:3 * D], ACT.Copy)\
                       .then_inc(free["s1"], 1)
                if step == "x1t":
                    ps = take("misc", "x1t", a)
                    act.activation(XT[:, a, :], ps[:, :], ACT.Copy).then_inc(free["misc"], 1)
                if step == "q":
                    if a >= 1:
                        act.wait_ge(parts_q[a - 1], 16)
                        act.wait_ge(parts_k[a - 1], 16)
                    act.wait_ge(perm_ready, 1)
                    ps = take("misc", "q", a)
                    act.activation(Qf[:, b, :], ps[:, :], ACT.Identity, bias=cols5[:, 0:1] if a < 2 else bjoin[:, 0:1],
                                   scale=float(HD) ** -0.5).then_inc(free["misc"], 1)
                    act.wait_ge(free["misc"], filled("misc", "q", a))
                    act.activation(Qp[:, 0, :], Qf[:, b, :], ACT.Copy).then_inc(qhi_ready, 1)
                if step == "k":
                    ps = take("misc", "k", a)
                    act.activation(Kf[:, :], ps[:, :], ACT.Identity,
                                   bias=cols5[:, 1:2] if a < 2 else bjoin[:, 1:2]).then_inc(free["misc"], 1)
                    act.wait_ge(free["misc"], filled("misc", "k", a))
                    act.activation(Kp[:, 0, :], Kf[:, :], ACT.Copy).then_inc(khi_ready, 1)
                if step == "max_rows":
                    ps = take("misc", "max_rows", a, i)
                    act.activation(nmT[:, b, i, :], ps[0:HEADS, 0:S // 2].bitcast(bf16), ACT.Copy)\
                       .then_inc(free["misc"], 1)
                    if a < 2:
                        heads = slice(i * HALF, (i + 1) * HALF)
                        act.wait_ge(simg_ready, NTH[step, a, i])
                        act.activation(Pimg[:, b, :, heads], simg[:, b, :, heads], ACT.Exp).then_inc(pimg_ready, 1)
                if step == "values" and i % NT == NT - 1:
                    ps = take("pv", "values", a, i // NT)
                    act.activation(Ou[:, i // NT % 2, :], ps[:, :], ACT.Copy).then_inc(free["pv"], 1)
                if step == "hidden":
                    ps = take("s1", "hidden", a, i)
                    act.activation(hid[:, i % 2, 1, :], ps[:, :], ACT.Relu, bias=cols17[:, 2 * i + 1:2 * i + 2])\
                       .then_inc(free["s1"], 1)
                if step == "attend":
                    r, u, j = unit(i)
                    half = 2 * (a * ROUNDS + r) + u
                    if j == 0 and half >= 2:
                        if u == 0:
                            act.wait_ge(half_done, half // 2)
                        else:
                            n = half // 2 - 1
                            act.wait_ge(full["pv"], filled("pv", "values", n // ROUNDS, n % ROUNDS))
                    ps = take(f"t{i % 2}", "weights", a, i)
                    w = sum(x[2] for x in blocks_of(a, u))
                    act.activation(probs[:, half % 2, j, 0:w], ps[:, 0:w], ACT.Exp).then_inc(free[f"t{i % 2}"], 1)
                if step == "o_rows":
                    ps = take("misc", "o_rows", a)
                    act.activation(OT[:, a, :], ps[:, :], ACT.Copy).then_inc(free["misc"], 1)
                if step == "x3t":
                    ps = take("misc", "x3t", a)
                    act.activation(X3T[:, a, :], ps[:, :], ACT.Copy).then_inc(free["misc"], 1)
                if step == "combine":
                    ps = take("misc", "combine", a)
                    act.activation(combT[:, :], ps[0:EXPERTS, :], ACT.Copy).then_inc(free["misc"], 1)
                if step == "route":
                    act.wait_ge(dl_ready, a + 1)
                    act.activation(ex[:, :, :], dl[:, :, :], ACT.Exp).then_inc(ex_ready, 1)

        @block.vector
        def _(dve):
            done = [0]

            def then_wait(ins):
                done[0] += 1
                ins.then_inc(dve_step, 1)
                dve.wait_ge(dve_step, done[0])

            def take(n, *name):
                dve.wait_ge(full[n], filled(n, *name))
                return place[n]

            norms = [0]

            def norm_stats(src):
                for t in range(NT):
                    last = dve.bn_stats(stats[:, t, :], src[:, t, :])
                then_wait(last)
                for t in range(NT):
                    last = dve.bn_aggr(mv[:, t, :], stats[:, t, :])
                then_wait(last)
                norms[0] += 1
                dve.tensor_scalar(ve[:, :], mv[:, :, 1], EPS, None, ALU.add).then_inc(ve_ready, 1)

            def norm(src, dst, gain, more, read_out, count):
                for t in range(NT):
                    read = dve.scalar_tensor_tensor(out=dst[:, t, :], in0=src[:, t, :], scalar=mv[:, t, 0:1],
                                                    in1=norm_gb[:, gain, :], op0=ALU.subtract, op1=ALU.mult)
                read.then_inc(read_out, 1)
                dve.wait_ge(read_out, count)
                dve.wait_ge(rstd_ready, norms[0])
                for t in range(NT):
                    last = dve.scalar_tensor_tensor(out=dst[:, t, :], in0=dst[:, t, :], scalar=rstd[:, t:t + 1],
                                                    in1=more(t), op0=ALU.mult, op1=ALU.add)
                return last

            for step, a, i in ORDER:
                b = a % 2
                if step == "setup":
                    dve.wait_ge(in_x, 16 * 3)
                    for n in range(B):
                        last = dve.tensor_tensor(
                            xtmp[:, n * NT:(n + 1) * NT, :], X[:, n * NT:(n + 1) * NT, :],
                            cond_all[:, n:n + 1, :].to_broadcast([P, NT, D]), ALU.mult)
                    then_wait(last)
                    then_wait(dve.tensor_reduce(wdot[:, 0, :], xtmp[:, :, :], AX, ALU.add))
                    then_wait(dve.tensor_scalar(wdot[:, 0, :], wdot[:, 0, :], float(D) ** -0.5, None, ALU.mult))
                    then_wait(dve.tensor_tensor(wdot[:, 5, 0:NT], wdot[:, 0, 0:NT], wdot[:, 0, NT:], ALU.max))
                    for n in range(B):
                        last = dve.tensor_tensor(wdot[:, 1, n * NT:(n + 1) * NT], wdot[:, 0, n * NT:(n + 1) * NT],
                                                 wdot[:, 5, 0:NT], ALU.subtract)
                    last.then_inc(w_exp_in, 1)
                    dve.tensor_reduce(q1[:, 0, :], X[:, :, :], AX, ALU.max, apply_absolute_value=True)
                    dve.wait_ge(w_exp, 1)
                    then_wait(dve.tensor_tensor(wdot[:, 5, 0:NT], wdot[:, 3, 0:NT], wdot[:, 3, NT:], ALU.add))
                    then_wait(dve.reciprocal(wdot[:, 5, NT:], wdot[:, 5, 0:NT]))
                    for n in range(B):
                        last = dve.tensor_tensor(wdot[:, 0, n * NT:(n + 1) * NT], wdot[:, 3, n * NT:(n + 1) * NT],
                                                 wdot[:, 5, NT:], ALU.mult)
                    then_wait(last)
                    then_wait(dve.tensor_tensor(q1[:, 0, :], q1[:, 0, :], wdot[:, 0, :], ALU.mult))
                    then_wait(dve.tensor_scalar(q1[:, 0, :], q1[:, 0, :], 1e-5, None, ALU.max))
                    then_wait(dve.reciprocal(q1[:, 1, :], q1[:, 0, :]))
                    then_wait(dve.tensor_scalar(q1[:, 1, :], q1[:, 1, :], 127.0, None, ALU.mult))
                    ps = take("misc", "sums")
                    then_wait(dve.tensor_scalar(wmean[:, :], ps[:, 0:3], 1.0 / (INNER * D), 1e-5, ALU.mult, ALU.max))
                    dve.reciprocal(wscale[:, :], wmean[:, :]).then_inc(free["misc"], 1)
                    for t in range(TILES):
                        last = dve.tensor_scalar(xtmp[:, t, :], X[:, t, :], wdot[:, 0, t:t + 1], q1[:, 1, t:t + 1],
                                                 ALU.mult, ALU.mult)
                    then_wait(last)
                    dve.tensor_scalar(R1[:, :, :], xtmp[:, :, :], MAGIC, MAGIC, ALU.add, ALU.subtract)\
                       .then_inc(r1_ready, 1)
                    dve.wait_ge(wscaled_ready, 1)
                    then_wait(dve.tensor_scalar(wtmp[:, :, :], wtmp[:, :, :], MAGIC, 1.0, ALU.subtract, ALU.min))
                    dve.tensor_scalar(Wt[:, :, :], wtmp[:, :, :], -1.0, None, ALU.max).then_inc(ternary_ready, 1)
                    then_wait(dve.tensor_scalar(q1[:, 2, :], q1[:, 0, :], 1.0 / 127.0, None, ALU.mult))
                    dve.tensor_scalar(q1[:, 4, :], q1[:, 2, :], wmean[:, 1:2], None, ALU.mult)
                    dve.tensor_scalar(q1[:, 3, :], q1[:, 2, :], wmean[:, 0:1], None, ALU.mult).then_inc(scale_ready, 1)
                if step == "prepare":
                    dve.wait_ge(in_att, 16 * 17)
                    dve.tensor_copy(rows5p[:, :].rearrange("r (d h) -> r d h", h=HEADS),
                                    rows5[:, :].rearrange("r (h d) -> r d h", d=HD)).then_inc(setup_pe, 1)
                    dve.wait_ge(pool_const, 1)
                    dve.tensor_reduce(head_of[:, :], head_grid[:, :, :].rearrange("p d h -> p h d"), AX, ALU.add)
                    ps = take("misc", "small")
                    dve.tensor_copy(cols5[:, :], ps[:, 0:5])
                    then_wait(dve.tensor_copy(cols17[:, :], ps[:, 8:25]))
                    for n in range(2):
                        last = dve.tensor_scalar(cols5[:, 2 * n:2 * n + 1], cols5[:, 2 * n:2 * n + 1],
                                                 float(HD) ** -0.5, None, ALU.mult)
                    then_wait(last)
                    dve.tensor_scalar(kimg[:, :], ps[:, 32:32 + B], cols5[:, 4:5], None, ALU.add)\
                       .then_inc(free["misc"], 1)
                    dve.wait_ge(free["misc"], filled("misc", "small"))
                    for n in range(B):
                        last = dve.tensor_scalar(Kimg[:, n, :], head_of[:, :], kimg[:, n:n + 1], None, ALU.mult)
                    last.then_inc(perm_ready, 1)
                    ps = take("s0", "image_v")
                    for n in range(B):
                        last = dve.tensor_copy(Vimg[:, n, :, 0:HD],
                                               ps[:, n * D:(n + 1) * D].rearrange("p (h d) -> p h d", d=HD))
                    dve.tensor_copy(vbias[:, 1, :], ps[:, B * D:(B + 1) * D])
                    for n, scale in enumerate((float(HD) ** -0.5, 1.0)):
                        last = dve.tensor_scalar(bjoin[:, n:n + 1], ps[:, (B + 1) * D + n:(B + 1) * D + n + 1],
                                                 scale, cols5[:, 2 + n:3 + n], ALU.mult, ALU.add)
                    last.then_inc(free["s0"], 1)
                if step == "ffn_up":
                    t = a * NT + i
                    ps = take(f"t{i % 2}", "up", a, i)
                    dve.wait_ge(silu_ready, t + 1)
                    dve.tensor_tensor(H(a, i), SG(i), ps[:, INNER:2 * INNER], ALU.mult)\
                       .then_inc(free[f"t{i % 2}"], 1)
                    dve.wait_ge(free[f"t{i % 2}"], filled(f"t{i % 2}", "up", a, i))
                    last = dve.tensor_reduce(q2[:, 0, t:t + 1], H(a, i), AX, ALU.max, apply_absolute_value=True)
                    if i == NT - 1:
                        then_wait(last)
                        r = slice(a * NT, (a + 1) * NT)
                        then_wait(dve.tensor_tensor(q2[:, 0, r], q2[:, 0, r], q1[:, 4, r], ALU.mult))
                        then_wait(dve.tensor_scalar(q2[:, 0, r], q2[:, 0, r], 1e-5, None, ALU.max))
                        then_wait(dve.reciprocal(q2[:, 1, r], q2[:, 0, r]))
                        dve.tensor_scalar(q2[:, 3, r], q2[:, 0, r], wmean[:, 2:3], 1.0 / 127.0, ALU.mult, ALU.mult)
                        then_wait(dve.tensor_scalar(q2[:, 1, r], q2[:, 1, r], 127.0, None, ALU.mult))
                        dve.tensor_tensor(q2[:, 2, r], q2[:, 1, r], q1[:, 4, r], ALU.mult).then_inc(q2_ready, 1)
                if step == "r2t":
                    t = a * NT + i
                    dve.wait_ge(y_ready, t + 1)
                    dve.tensor_scalar(R2[:, t % 2, :], Y(i), MAGIC, None, ALU.subtract).then_inc(r2_ready, 1)
                if step == "down":
                    ps = take(f"t{i % 2}", "r2t", a, i)
                    dve.tensor_copy(R2T[:, i % 2, :], ps[:, 0:INNER // 2].bitcast(bf16))\
                       .then_inc(free[f"t{i % 2}"], 1)
                if step == "x1t":
                    ps = take("pv", "down", a)
                    dve.wait_ge(q2_ready, a + 1)
                    for t in range(NT):
                        n = a * NT + t
                        last = dve.scalar_tensor_tensor(out=X1[:, n, :], in0=ps[:, t * D:(t + 1) * D],
                                                        scalar=q2[:, 3, n:n + 1], in1=X[:, n, :],
                                                        op0=ALU.mult, op1=ALU.add)
                    last.then_inc(free["pv"], 1)
                if step == "q":
                    dve.wait_ge(qhi_ready, a + 1)
                    then_wait(dve.tensor_tensor(qres[:, :], Qf[:, b, :], Qp[:, 0, :], ALU.subtract))
                    then_wait(dve.tensor_copy(Qp[:, 1, :], qres[:, :]))
                    dve.tensor_tensor(Qp[:, 2, :], qres[:, :], Qp[:, 1, :], ALU.subtract).then_inc(qp_ready, 1)
                if step == "k":
                    dve.wait_ge(khi_ready, a + 1)
                    then_wait(dve.tensor_tensor(kres[:, :], Kf[:, :], Kp[:, 0, :], ALU.subtract))
                    then_wait(dve.tensor_copy(Kp[:, 1, :], kres[:, :]))
                    dve.tensor_tensor(Kp[:, 2, :], kres[:, :], Kp[:, 1, :], ALU.subtract).then_inc(kp_ready, 1)
                if step == "v":
                    if a < 2:
                        dve.wait_ge(stack_init, 2)
                        dve.wait_ge(in_att, 16 * 17)
                    ps = take("misc", "v", a)
                    bias = vbias[:, a // 2, :].rearrange("p (h d) -> p h d", d=HD)
                    dve.tensor_tensor(Vs[:, b, :, :, 0:HD],
                                      ps[:, :].rearrange("p (t h d) -> p t h d", t=NT, d=HD),
                                      bias.unsqueeze(1).to_broadcast([P, NT, HEADS, HD]), ALU.add)\
                       .then_inc(free["misc"], 1)
                if step == "scores":
                    h, t = i // NT, i % NT
                    ps = take(SCORES[a, i], "scores", a, i)
                    w = (t + 1) * P if a < 2 else S
                    dve.tensor_reduce(mx[:, b, t, h:h + 1], ps[:, 0:w], AX, ALU.max).then_inc(free[SCORES[a, i]], 1)
                if step == "max":
                    for n in range((i + 1) * HALF * NT - 4, (i + 1) * HALF * NT):
                        dve.wait_ge(free[SCORES[a, n]], filled(SCORES[a, n], "scores", a, n))
                    heads = slice(i * HALF, (i + 1) * HALF)
                    m, high, low = mx[:, b, :, heads], nm[:, b, :, i, 0, :], nm[:, b, :, i, 1, :]
                    if a < 2:
                        image = take("misc", "image", a, i)[:, 0:NT * HALF].rearrange("p (t h) -> p t h", h=HALF)
                        then_wait(dve.tensor_tensor(m, image, m, ALU.max))
                    then_wait(dve.tensor_scalar(high, m, -1.0, None, ALU.mult))
                    dve.scalar_tensor_tensor(out=low, in0=m, scalar=-1.0, in1=high,
                                             op0=ALU.mult, op1=ALU.subtract).then_inc(nm_ready, 1)
                    if a < 2:
                        dve.tensor_tensor(simg[:, b, :, heads], image, high, ALU.add).then_inc(free["misc"], 1)
                        dve.wait_ge(free["misc"], filled("misc", "image", a, i))
                        dve.wait_ge(nm_ready, NTH[step, a, i])
                        dve.tensor_tensor(simg[:, b, :, heads], simg[:, b, :, heads], low, ALU.add)\
                           .then_inc(simg_ready, 1)
                if step == "turn_back":
                    ps = take("misc", "turn_back", a, i)
                    tb = ps[:, :].rearrange("p (t j c) -> p t j c", j=GROUP, c=HC)
                    heads = slice(i * GROUP, (i + 1) * GROUP)
                    if a < 2:
                        dve.wait_ge(zimg_ready, NTH["max", a, i * GROUP // HALF])
                        if a * ROUNDS + i > 0:
                            dve.wait_ge(turned_ready, a * ROUNDS + i)
                        dve.tensor_tensor(sums[:, :, :, :], tb[:, :, :, 0:HD + 1], Zimg[:, b, :, heads, :], ALU.add)\
                           .then_inc(free["misc"], 1)
                        dve.wait_ge(free["misc"], filled("misc", "turn_back", a, i))
                        tb = sums
                    then_wait(dve.reciprocal(rden[:, :, :], tb[:, :, :, HD]))
                    last = dve.tensor_tensor(On[:, :, heads, :], tb[:, :, :, 0:HD],
                                             rden[:, :, :].unsqueeze(3).to_broadcast([P, NT, GROUP, HD]), ALU.mult)
                    if a >= 2:
                        last.then_inc(free["misc"], 1)
                    else:
                        last.then_inc(turned_ready, 1)
                if step == "sum":
                    dve.wait_ge(in_moe, 16 * 9)
                    norm_stats(take("misc", "sum", a)[:, :].rearrange("p (t d) -> p t d", d=D))
                    norm(place["misc"][:, :].rearrange("p (t d) -> p t d", d=D), X3[:, :, :], 0,
                         lambda t: norm_gb[:, 1, :], free["misc"], filled("misc", "sum", a)).then_inc(x3_ready, 1)
                if step == "router":
                    ps = take("misc", "router", a)
                    dve.tensor_tensor(lg[:, :, :],
                                      ps[:, 0:NT * (NG + EXPERTS)].rearrange("p (t n) -> p t n", t=NT),
                                      rbias[:, :].unsqueeze(1).to_broadcast([P, NT, NG + EXPERTS]), ALU.add)\
                       .then_inc(free["misc"], 1)
                    dve.wait_ge(free["misc"], filled("misc", "router", a))
                    pair = lg[:, :, NG:].rearrange("p t (g e) -> p t g e", e=2)
                    dve.tensor_reduce(rs[:, 0, :], lg[:, :, 0:NG], AX, ALU.max)
                    then_wait(dve.tensor_tensor(rg[:, 0, :, :], pair[:, :, :, 0], pair[:, :, :, 1], ALU.max))
                    dve.tensor_tensor(dl[:, :, 0:NG], lg[:, :, 0:NG],
                                      rs[:, 0, :].unsqueeze(2).to_broadcast([P, NT, NG]), ALU.subtract)
                    then_wait(dve.tensor_tensor(dl[:, :, NG:].rearrange("p t (g e) -> p t g e", e=2), pair,
                                                rg[:, 0, :, :].unsqueeze(3).to_broadcast([P, NT, NG, 2]),
                                                ALU.subtract))
                    dve.scalar_tensor_tensor(out=rg[:, 1, :, :], in0=dl[:, :, 0:NG], scalar=0.0,
                                             in1=prior[:, :, :], op0=ALU.is_equal, op1=ALU.mult).then_inc(dl_ready, 1)
                if step == "route":
                    dve.wait_ge(dl_ready, a + 1)
                    then_wait(dve.tensor_reduce(rs[:, 1, :], rg[:, 1, :, :], AX, ALU.max))
                    dve.tensor_tensor(rg[:, 2, :, :], rg[:, 1, :, :],
                                      rs[:, 1, :].unsqueeze(2).to_broadcast([P, NT, NG]), ALU.is_equal)
                    dve.wait_ge(ex_ready, a + 1)
                    pex = ex[:, :, NG:].rearrange("p t (g e) -> p t g e", e=2)
                    dve.tensor_reduce(rs[:, 2, :], ex[:, :, 0:NG], AX, ALU.add)
                    then_wait(dve.tensor_tensor(rg[:, 3, :, :], pex[:, :, :, 0], pex[:, :, :, 1], ALU.add))
                    then_wait(dve.tensor_tensor(rg[:, 3, :, :], rg[:, 3, :, :],
                                                rs[:, 2, :].unsqueeze(2).to_broadcast([P, NT, NG]), ALU.mult))
                    then_wait(dve.reciprocal(rg[:, 0, :, :], rg[:, 3, :, :]))
                    then_wait(dve.tensor_tensor(rg[:, 0, :, :], rg[:, 0, :, :], rg[:, 2, :, :], ALU.mult))
                    dpair = dl[:, :, NG:].rearrange("p t (g e) -> p t g e", e=2)
                    then_wait(dve.scalar_tensor_tensor(out=comb[:, a, :, :, 0], in0=dpair[:, :, :, 0], scalar=0.0,
                                                       in1=rg[:, 0, :, :], op0=ALU.is_equal, op1=ALU.mult))
                    dve.tensor_tensor(comb[:, a, :, :, 1], rg[:, 0, :, :], comb[:, a, :, :, 0], ALU.subtract)\
                       .then_inc(comb_ready, 1)
                if step == "combine":
                    dve.wait_ge(comb_ready, a + 1)
                if step == "bias2":
                    ps = take("misc", "bias2", a)
                    dve.tensor_tensor(acc[:, a, :, :], ps[:, :].rearrange("p (t d) -> p t d", d=D),
                                      X3[:, :, :], ALU.add).then_inc(free["misc"], 1)
                if step == "hidden":
                    ps = take("s0", "hidden", a, i)
                    dve.tensor_scalar(hid[:, i % 2, 0, :], ps[:, :], cols17[:, 2 * i:2 * i + 1], 0.0,
                                      ALU.add, ALU.max).then_inc(free["s0"], 1)
                if step == "y":
                    if i == 0:
                        dve.wait_ge(free["misc"], filled("misc", "bias2", a))
                    else:
                        dve.wait_ge(free["misc"], filled("misc", "y", a, i - 1))
                    ps = take("misc", "y", a, i)
                    for t in range(NT):
                        last = dve.scalar_tensor_tensor(
                            out=acc[:, a, t, :], in0=ps[:, t * D:(t + 1) * D],
                            scalar=comb[:, a, t, i // 2, i % 2:i % 2 + 1], in1=acc[:, a, t, :],
                            op0=ALU.mult, op1=ALU.add)
                    last.then_inc(free["misc"], 1)
                if step == "out":
                    dve.wait_ge(free["misc"], filled("misc", "y", a, EXPERTS - 1))
                    norm_stats(acc[:, a, :, :])
                    dve.wait_ge(residual_ready, a + 1)
                    norm(acc[:, a, :, :], acc[:, a, :, :], 2, lambda t: X1[:, a * NT + t, :],
                         gained, a + 1).then_inc(out_ready, 1)

        @block.tensor
        def _(pe):
            def put(n, *name):
                if JOB[n][name] > 0:
                    pe.wait_ge(free[n], JOB[n][name])
                return place[n]

            for step, a, i in ORDER:
                b = a % 2
                if step == "setup":
                    pe.wait_ge(pool_const, 1)
                    pe.wait_ge(sums_ready, 1)
                    ps = put("misc", "sums")
                    pe.matmul(ps[:, 0:3], ones[:, :], absum[:, :], start=True, stop=True).then_inc(full["misc"], 1)
                    pe.wait_ge(ternary_ready, 1)
                    ps = put("t1", "ternary")
                    for n in range(8):
                        pe.transpose(ps[:, n * P // 2:(n + 1) * P // 2].bitcast(bf16),
                                     Wt[:, n // NC, (n % NC) * P:(n % NC + 1) * P], identb[:, :])
                    for n in range(NC):
                        mm = pe.transpose(ps[:, S + n * P // 2:S + (n + 1) * P // 2].bitcast(bf16),
                                          Wt[:, 2, n * P:(n + 1) * P], identb[:, :])
                    mm.then_inc(full["t1"], 1)
                if step == "turn_weights":
                    pe.wait_ge(in_att, 16 * 17)
                    ps = put("misc", "wi")
                    for n in range(3):
                        mm = pe.transpose(ps[:, n * D:(n + 1) * D], Win[:, n, :], ident[:, :])
                    mm.then_inc(full["misc"], 1)
                    ps = put("t0", "turned")
                    for n in range(3):
                        pe.transpose(ps[:, n * D:(n + 1) * D], Wsq[:, n, :], ident[:, :])
                    pe.transpose(ps[:, 3 * D:3 * D + B], condr[:, :], ident[0:B, 0:B]).then_inc(full["t0"], 1)
                    ps = put("t1", "projection")
                    pe.transpose(ps[:, 0:D], Wcp[:, :], ident[:, :]).then_inc(full["t1"], 1)
                if step == "prepare":
                    pe.wait_ge(setup_pe, 1)
                    ps = put("misc", "small")
                    pe.transpose(ps[:, 0:5], rows5p[:, :], ident[0:5, 0:5])
                    pe.transpose(ps[:, 8:25], rows17[:, :], ident[0:17, 0:17])
                    pe.wait_ge(free["t0"], filled("t0", "turned"))
                    pe.matmul(ps[:, 32:32 + B], WsqT[:, 1, :], condT[:, :], start=True, stop=True)\
                      .then_inc(full["misc"], 1)
                    ps = put("s0", "image_v")
                    for n in range(B):
                        pe.matmul(ps[:, n * D:(n + 1) * D], condT[:, n:n + 1].to_broadcast([P, P]),
                                  WsqT[:, 2, :], start=True, stop=False)
                        pe.matmul(ps[:, n * D:(n + 1) * D], ones[0:1, :], brow[:, 1, :], start=False, stop=True)
                    pe.wait_ge(free["t1"], filled("t1", "projection"))
                    pe.wait_ge(free["misc"], filled("misc", "small"))
                    pe.matmul(ps[:, B * D:(B + 1) * D], cols17[:, 16:17].to_broadcast([P, P]), WinT[:, 2, :],
                              start=True, stop=False)
                    pe.matmul(ps[:, B * D:(B + 1) * D], ones[0:1, :], brow[:, 0, :], start=False, stop=True)
                    for n in range(2):
                        mm = pe.matmul(ps[:, (B + 1) * D + n:(B + 1) * D + n + 1], WinT[:, n, :],
                                       cols17[:, 16:17], start=True, stop=True)
                    mm.then_inc(full["s0"], 1)
                    ps = put("s1", "joined")
                    pe.matmul(ps[:, 0:3 * D], WcpT[:, :], WinT[:, :, :].rearrange("p n d -> p (n d)"),
                              start=True, stop=True).then_inc(full["s1"], 1)
                if step == "ffn_in":
                    pe.wait_ge(r1_ready, 1)
                    ps = put("misc", "rt", a)
                    for t in range(NT):
                        mm = pe.transpose(ps[:, t * P // 2:(t + 1) * P // 2].bitcast(bf16),
                                          R1[:, a * NT + t, :], identb[:, :])
                    mm.then_inc(full["misc"], 1)
                if step == "ffn_up":
                    if i == 0:
                        pe.wait_ge(free["misc"], filled("misc", "rt", a))
                        pe.wait_ge(free["t1"], filled("t1", "ternary"))
                    ps = put(f"t{i % 2}", "up", a, i)
                    for n in range(2):
                        mm = pe.matmul(ps[:, n * INNER:(n + 1) * INNER], RT[:, a, i * P:(i + 1) * P],
                                       WtT[:, n * NC:(n + 1) * NC, :].rearrange("p a d -> p (a d)"),
                                       start=True, stop=True)
                    mm.then_inc(full[f"t{i % 2}"], 1)
                if step == "r2t":
                    t = a * NT + i
                    pe.wait_ge(r2_ready, t + 1)
                    ps = put(f"t{i % 2}", "r2t", a, i)
                    for c in range(NC):
                        mm = pe.transpose(ps[:, c * P // 2:(c + 1) * P // 2].bitcast(bf16),
                                          R2[:, t % 2, c * P:(c + 1) * P], identb[:, :])
                    mm.then_inc(full[f"t{i % 2}"], 1)
                if step == "down":
                    pe.wait_ge(free[f"t{i % 2}"], filled(f"t{i % 2}", "r2t", a, i))
                    if i == 0:
                        put("pv", "down", a)
                    for c in range(NC):
                        mm = pe.matmul(place["pv"][:, i * D:(i + 1) * D], R2T[:, i % 2, c * P:(c + 1) * P],
                                       WtT[:, 2 * NC + c, :], start=(c == 0), stop=(c == NC - 1))
                    if i == NT - 1:
                        mm.then_inc(full["pv"], 1)
                if step == "x1t":
                    pe.wait_ge(free["pv"], filled("pv", "down", a))
                    ps = put("misc", "x1t", a)
                    for t in range(NT):
                        mm = pe.transpose(ps[:, t * P:(t + 1) * P], X1[:, a * NT + t, :], ident[:, :])
                    mm.then_inc(full["misc"], 1)
                if step == "q":
                    if a < 2:
                        pe.wait_ge(perm_ready, 1)
                        pe.wait_ge(wcaq_ready, 1)
                        pe.wait_ge(free["misc"], filled("misc", "x1t", a))
                    else:
                        pe.wait_ge(free["misc"], filled("misc", "o_rows", a - 2))
                        if a == 2:
                            pe.wait_ge(free["s0"], filled("s0", "image_v"))
                            pe.wait_ge(free["s1"], filled("s1", "joined"))
                    ps = put("misc", "q", a)
                    w, x = (Wcaq[:, 0, :], XT[:, b, :]) if a < 2 else (Wjoin[:, 0, :], OT[:, b, :])
                    pe.matmul(ps[:, :], w, x, start=True, stop=True).then_inc(full["misc"], 1)
                if step == "k":
                    ps = put("misc", "k", a)
                    w, x = (Wcaq[:, 1, :], XT[:, b, :]) if a < 2 else (Wjoin[:, 1, :], OT[:, b, :])
                    pe.matmul(ps[:, :], w, x, start=True, stop=True).then_inc(full["misc"], 1)
                if step == "v":
                    w, x = (Wca[:, 2 * D:3 * D], XT) if a < 2 else (Wjoin[:, 2, :], OT)
                    ps = put("misc", "v", a)
                    for t in range(NT):
                        mm = pe.matmul(ps[:, t * D:(t + 1) * D], x[:, b, t * P:(t + 1) * P], w, start=True, stop=True)
                    mm.then_inc(full["misc"], 1)
                if step == "scores":
                    if i == HEADS * NT // 2:
                        pe.wait_ge(stacked[a][1], 16 * 2 * PARTS)
                    if i == 0:
                        pe.wait_ge(stacked[a][0], 16 * 2 * PARTS)
                        if a < 2:
                            pe.wait_ge(fixed_rows, 16 * 2 * (PARTS + 3))
                    rows = MASK + PARTS if a < 2 else STACK
                    h, t = i // NT, i % NT
                    ps = put(SCORES[a, i], "scores", a, i)
                    w = (t + 1) * P if a < 2 else S
                    mm = pe.matmul(ps[:, 0:w], Qs[0:rows, b, h, t * P:(t + 1) * P], Ks[0:rows, b, h, 0:w],
                                   start=True, stop=(a >= 2))
                    if a < 2:
                        mm = pe.matmul(ps[:, w - P:w], identb[:, :], causal_q[:, :], start=False, stop=True)
                    mm.then_inc(full[SCORES[a, i]], 1)
                if step == "max" and a < 2:
                    ps = put("misc", "image", a, i)
                    for t in range(NT):
                        mm = pe.matmul(ps[:, t * HALF:(t + 1) * HALF], Qf[:, b, t * P:(t + 1) * P],
                                       Kimg[:, b, i * HALF:(i + 1) * HALF], start=True, stop=True)
                    mm.then_inc(full["misc"], 1)
                if step == "max_rows":
                    pe.wait_ge(nm_ready, NTH[step, a, i])
                    ps = put("misc", "max_rows", a, i)
                    for t in range(NT):
                        mm = pe.transpose(ps[0:HEADS, t * P // 2:(t + 1) * P // 2].bitcast(bf16),
                                          nm[:, b, t, i, :, :].rearrange("p n h -> p (n h)"), identb[:, :])
                    mm.then_inc(full["misc"], 1)
                if step == "attend":
                    if i % (UNITS // 2) == 0:
                        pe.wait_ge(shifted[a][i // (UNITS // 2)], 16)
                    rows = MASK + PARTS if a < 2 else MASK
                    r, u, j = unit(i)
                    h = r * GROUP + j
                    ps = put(f"t{i % 2}", "weights", a, i)
                    for kb, col, w in blocks_of(a, u):
                        mm = pe.matmul(ps[:, col:col + w], Ks[0:rows, b, h, kb * P:(kb + 1) * P],
                                       Qs[0:rows, b, h, S - w:S], start=True, stop=(a >= 2))
                        if a < 2:
                            mm = pe.matmul(ps[:, col:col + P], identb[:, :], causal_k[:, :],
                                           start=False, stop=True)
                    mm.then_inc(full[f"t{i % 2}"], 1)
                if step == "values":
                    r, kb = i // NT, i % NT
                    u = kb // 2
                    half = 2 * (a * ROUNDS + r) + u
                    ps = put("pv", "values", a, r) if kb == 0 else place["pv"]
                    if kb % 2 == 0:
                        for n in (2 * GROUP * r + GROUP * u + 2, 2 * GROUP * r + GROUP * u + 3):
                            pe.wait_ge(free[f"t{n % 2}"], filled(f"t{n % 2}", "weights", a, n))
                    _, col, w = blocks_of(a, u)[kb % 2]
                    for j in range(GROUP):
                        mm = pe.matmul(ps[j * HC:(j + 1) * HC, S - w:S], Vs[:, b, kb, r * GROUP + j, :],
                                       probs[:, half % 2, j, col:col + w], start=(kb == 0),
                                       stop=(kb == NT - 1))
                    if kb == 1:
                        mm.then_inc(half_done, 1)
                    if kb == NT - 1:
                        mm.then_inc(full["pv"], 1)
                if step == "turn_back":
                    pe.wait_ge(free["pv"], filled("pv", "values", a, i))
                    ps = put("misc", "turn_back", a, i)
                    for t in range(NT):
                        mm = pe.transpose(ps[:, t * P:(t + 1) * P], Ou[:, i % 2, t * P:(t + 1) * P], ident[:, :])
                    mm.then_inc(full["misc"], 1)
                if step == "o_rows":
                    pe.wait_ge(free["misc"], filled("misc", "turn_back", a, ROUNDS - 1))
                    if a < 2:
                        pe.wait_ge(turned_ready, (a + 1) * ROUNDS)
                    ps = put("misc", "o_rows", a)
                    for t in range(NT):
                        mm = pe.transpose(ps[:, t * P:(t + 1) * P],
                                          On[:, t, :, :].rearrange("p h d -> p (h d)"), ident[:, :])
                    mm.then_inc(full["misc"], 1)
                if step == "sum":
                    pe.wait_ge(bias_ready, 1)
                    pe.wait_ge(free["misc"], filled("misc", "o_rows", 2 + a))
                    ps = put("misc", "sum", a)
                    for t in range(NT):
                        o = ps[:, t * D:(t + 1) * D]
                        pe.matmul(o, OT[:, a, t * P:(t + 1) * P], Wcp[:, :], start=True, stop=False)
                        pe.matmul(o, OT[:, 2 + a, t * P:(t + 1) * P], WsqT[:, 0, :], start=False, stop=False)
                        mm = pe.matmul(o, ones[0:1, :], brow[:, 2, :], start=False, stop=True)
                    mm.then_inc(full["misc"], 1)
                if step == "x3t":
                    pe.wait_ge(x3_ready, a + 1)
                    ps = put("misc", "x3t", a)
                    for t in range(NT):
                        mm = pe.transpose(ps[:, t * P:(t + 1) * P], X3[:, t, :], ident[:, :])
                    mm.then_inc(full["misc"], 1)
                if step == "router":
                    pe.wait_ge(in_moe, 16 * 9)
                    pe.wait_ge(free["misc"], filled("misc", "x3t", a))
                    ps = put("misc", "router", a)
                    n = NG + EXPERTS
                    for t in range(NT):
                        mm = pe.matmul(ps[:, t * n:(t + 1) * n], X3T[:, a, t * P:(t + 1) * P], Wr[:, :],
                                       start=True, stop=True)
                    mm.then_inc(full["misc"], 1)
                if step == "combine":
                    pe.wait_ge(comb_ready, a + 1)
                    ps = put("misc", "combine", a)
                    for t in range(NT):
                        mm = pe.transpose(ps[0:EXPERTS, t * P:(t + 1) * P],
                                          comb[:, a, t, :, :].rearrange("p g e -> p (g e)"), ident[:, :])
                    mm.then_inc(full["misc"], 1)
                if step == "bias2":
                    pe.wait_ge(free["misc"], filled("misc", "combine", a))
                    ps = put("misc", "bias2", a)
                    for t in range(NT):
                        mm = pe.matmul(ps[:, t * D:(t + 1) * D], combT[:, t * P:(t + 1) * P], B2[:, :],
                                       start=True, stop=True)
                    mm.then_inc(full["misc"], 1)
                if step == "hidden":
                    if a == 0 and i == 0:
                        pe.wait_ge(in_experts, 16 * 2)
                    if i == 0:
                        pe.wait_ge(free["misc"], filled("misc", "x3t", a))
                    for h in range(FH):
                        ps = put(f"s{h}", "hidden", a, i)
                        pe.matmul(ps[:, :], W1[:, i, h * P:(h + 1) * P], X3T[:, a, :], start=True, stop=True)\
                          .then_inc(full[f"s{h}"], 1)
                if step == "y":
                    for h in range(FH):
                        pe.wait_ge(free[f"s{h}"], filled(f"s{h}", "hidden", a, i))
                    ps = put("misc", "y", a, i)
                    for t in range(NT):
                        for h in range(FH):
                            mm = pe.matmul(ps[:, t * D:(t + 1) * D], hid[:, i % 2, h, t * P:(t + 1) * P],
                                           W2[:, i, h, :], start=(h == 0), stop=(h == FH - 1))
                    mm.then_inc(full["misc"], 1)


INPUTS = [
    "x", "cond_1024", "mask_Bx1x1xS_ff0", "L0_ffn_w_gate", "L0_ffn_w_up", "L0_ffn_w_down",
    "L1_cond_c_attn_w", "L1_cond_c_attn_b", "L1_cond_c_proj_w", "L1_cond_c_proj_b", "L1_cond_uk_w",
    "L1_cond_uk_b", "L1_cond_uv_w", "L1_cond_uv_b", "L1_ffn_in_proj_w", "L1_ffn_in_proj_b",
    "L1_ffn_out_proj_w", "L1_ffn_out_proj_b", "L1_ffn_ln1_g", "L1_ffn_ln1_b", "L1_ffn_ln2_g",
    "L1_ffn_ln2_b", "L1_ffn_w_group", "L1_ffn_b_group", "L1_ffn_w_expert", "L1_ffn_b_expert",
    "L1_ffn_w1", "L1_ffn_b1", "L1_ffn_w2", "L1_ffn_b2",
]


def kernel(**inputs):
    import numpy as _np
    import concourse.bacc as _bacc
    from concourse import mybir as _mybir
    from concourse.bass_utils import run_bass_kernel_spmd as _run

    nc = _bacc.Bacc("TRN2", target_bir_lowering=False, num_devices=1)
    arrays, aps = {}, {}
    for name in INPUTS:
        a = _np.ascontiguousarray(inputs[name])
        arrays[f"in_{name}"] = a
        aps[name] = nc.dram_tensor(f"in_{name}", a.shape, _mybir.dt.from_np(a.dtype), kind="ExternalInput").ap()
    out = nc.dram_tensor("out_x", (B, S, D), _mybir.dt.float32, kind="ExternalOutput").ap()
    two_layers(nc, aps, out)
    r = _run(nc, [arrays], core_ids=[0])
    return r.results[0]["out_x"]
```
